# Optimizing a Trainium2 kernel written in Bass

```python
import numpy as np
import jax
import jax.numpy as jnp

def _softmax(x, axis=-1):
    return jax.nn.softmax(x, axis=axis)

def _gelu(x):
    return jax.nn.gelu(x, approximate=True)

def _silu(x):
    return jax.nn.silu(x)

def _sigmoid(x):
    return jax.nn.sigmoid(x)

def _layernorm(x, axis=-1, eps=1e-05):
    m = jnp.mean(x, axis=axis, keepdims=True)
    v = jnp.var(x, axis=axis, keepdims=True)
    return (x - m) / jnp.sqrt(v + eps)

def _scatter_add(tgt, idx, src, axis=0):
    return tgt.at[idx].add(src)

def _segment_sum(src, seg, n):
    return jax.ops.segment_sum(src, seg, n)
kernel_name = 'mk_cond_seq_d2_seqx_r8_97dd11'

def setup_inputs(seed: int=0):
    np.random.seed(seed)
    _w = jnp.asarray

    def _rec_inputs():
        import jax
        import jax.numpy as jnp
        _rk = jax.random.key(seed)
        x = 1.648e-05 + 1 * jax.random.normal(jax.random.fold_in(_rk, 1), (16, 128, 144), jnp.float32)
        _lenS = 128 - jax.random.randint(jax.random.fold_in(_rk, 7), (16,), 0, max(1, 128 // 4) + 1, jnp.int32)
        _lenS2 = 128 - jax.random.randint(jax.random.fold_in(_rk, 8), (16,), 0, max(1, 128 // 4) + 1, jnp.int32)
        cond_1152 = 0.00914911 + 1.00357 * jax.random.normal(jax.random.fold_in(_rk, 11), (16, 144), jnp.float32)
        return (x, cond_1152)
    x, cond_1152 = _rec_inputs()

    def _L0_cond_setup():
        import jax, jax.numpy as jnp
        import numpy as np
        B, L, C = (8, 128, 144)
        H = 16
        D = C // H
        FF = int(C * 4.0)
        EPS = 1e-06

        def _layernorm(x):
            mu = jnp.mean(x, axis=-1, keepdims=True)
            var = jnp.mean(jnp.square(x - mu), axis=-1, keepdims=True)
            return (x - mu) * jax.lax.rsqrt(var + EPS)

        def _modulate(x, shift, scale):
            return x * (1.0 + scale) + shift

        def _attention(h, W_qkv, b_qkv, W_proj, b_proj):
            b, l, c = h.shape
            qkv = h @ W_qkv + b_qkv
            qkv = qkv.reshape(b, l, 3, H, D)
            q, k, v = (qkv[:, :, 0], qkv[:, :, 1], qkv[:, :, 2])
            scale = D ** (-0.5)
            scores = jnp.einsum('blhd,bmhd->bhlm', q * scale, k)
            attn = jax.nn.softmax(scores, axis=-1)
            o = jnp.einsum('bhlm,bmhd->blhd', attn, v).reshape(b, l, c)
            return o @ W_proj + b_proj
        key = jax.random.key(seed)
        ks = jax.random.split(key, 12)
        s = 0.02
        return {'x': jax.random.normal(ks[0], (B, L, C), jnp.float32), 'c': jax.random.normal(ks[1], (B, 1, C), jnp.float32), 'W_qkv': jax.random.normal(ks[2], (C, 3 * C), jnp.float32) * s, 'b_qkv': jnp.zeros((3 * C,), jnp.float32), 'W_proj': jax.random.normal(ks[3], (C, C), jnp.float32) * s, 'b_proj': jnp.zeros((C,), jnp.float32), 'W_fc1': jax.random.normal(ks[4], (C, FF), jnp.float32) * s, 'b_fc1': jnp.zeros((FF,), jnp.float32), 'W_fc2': jax.random.normal(ks[5], (FF, C), jnp.float32) * s, 'b_fc2': jnp.zeros((C,), jnp.float32), 'W_ada': jax.random.normal(ks[6], (C, 6 * C), jnp.float32) * s, 'b_ada': jnp.zeros((6 * C,), jnp.float32)}
    _L0_cond_all = _L0_cond_setup()
    _L0_cond_in = {k: v for k, v in _L0_cond_all.items() if k in ('W_qkv', 'b_qkv', 'W_proj', 'b_proj', 'W_fc1', 'b_fc1', 'W_fc2', 'b_fc2', 'W_ada', 'b_ada')}
    del _L0_cond_all

    def _L1_cond_setup():
        import jax, jax.numpy as jnp
        import numpy as np
        from jax.scipy.linalg import expm
        N, D, COND_DIM = (144, 64, 144)
        B, T = (16, 128)

        def _rotation(cond, W, b):
            v = jax.nn.silu(cond) @ W.T + b
            iu, ju = jnp.triu_indices(D, k=1)
            A = jnp.zeros((cond.shape[0], D, D), dtype=v.dtype)
            A = A.at[:, iu, ju].set(v).at[:, ju, iu].set(-v)
            return expm(A)
        key = jax.random.key(seed)
        k1, k2, k3, k4, k5 = jax.random.split(key, 5)
        x = jax.random.normal(k1, (B, T, N), dtype=jnp.float32)
        cond = jax.random.normal(k2, (B, COND_DIM), dtype=jnp.float32)
        P = jax.random.normal(k3, (N, D), dtype=jnp.float32)
        n_skew = D * (D - 1) // 2
        bound = 1.0 / np.sqrt(COND_DIM)
        W = jax.random.uniform(k4, (n_skew, COND_DIM), minval=-bound, maxval=bound, dtype=jnp.float32)
        b = jax.random.uniform(k5, (n_skew,), minval=-bound, maxval=bound, dtype=jnp.float32)
        return {'x': x, 'cond': cond, 'P': P, 'W': W, 'b': b}
    _L1_cond_all = _L1_cond_setup()
    _L1_cond_in = {k: v for k, v in _L1_cond_all.items() if k in ('P', 'W', 'b')}
    del _L1_cond_all
    return {'x': x, 'cond_1152': cond_1152, 'L0_cond_W_qkv': _L0_cond_in['W_qkv'], 'L0_cond_b_qkv': _L0_cond_in['b_qkv'], 'L0_cond_W_proj': _L0_cond_in['W_proj'], 'L0_cond_b_proj': _L0_cond_in['b_proj'], 'L0_cond_W_fc1': _L0_cond_in['W_fc1'], 'L0_cond_b_fc1': _L0_cond_in['b_fc1'], 'L0_cond_W_fc2': _L0_cond_in['W_fc2'], 'L0_cond_b_fc2': _L0_cond_in['b_fc2'], 'L0_cond_W_ada': _L0_cond_in['W_ada'], 'L0_cond_b_ada': _L0_cond_in['b_ada'], 'L1_cond_P': _L1_cond_in['P'], 'L1_cond_W': _L1_cond_in['W'], 'L1_cond_b': _L1_cond_in['b']}

def reference(x, cond_1152, L0_cond_W_qkv, L0_cond_b_qkv, L0_cond_W_proj, L0_cond_b_proj, L0_cond_W_fc1, L0_cond_b_fc1, L0_cond_W_fc2, L0_cond_b_fc2, L0_cond_W_ada, L0_cond_b_ada, L1_cond_P, L1_cond_W, L1_cond_b):
    import jax
    import jax.numpy as jnp

    def _L0_cond_ref(x, c, W_qkv, b_qkv, W_proj, b_proj, W_fc1, b_fc1, W_fc2, b_fc2, W_ada, b_ada):
        import jax, jax.numpy as jnp
        import numpy as np
        B, L, C = (8, 128, 144)
        H = 16
        D = C // H
        FF = int(C * 4.0)
        EPS = 1e-06

        def _layernorm(x):
            mu = jnp.mean(x, axis=-1, keepdims=True)
            var = jnp.mean(jnp.square(x - mu), axis=-1, keepdims=True)
            return (x - mu) * jax.lax.rsqrt(var + EPS)

        def _modulate(x, shift, scale):
            return x * (1.0 + scale) + shift

        def _attention(h, W_qkv, b_qkv, W_proj, b_proj):
            b, l, c = h.shape
            qkv = h @ W_qkv + b_qkv
            qkv = qkv.reshape(b, l, 3, H, D)
            q, k, v = (qkv[:, :, 0], qkv[:, :, 1], qkv[:, :, 2])
            scale = D ** (-0.5)
            scores = jnp.einsum('blhd,bmhd->bhlm', q * scale, k)
            attn = jax.nn.softmax(scores, axis=-1)
            o = jnp.einsum('bhlm,bmhd->blhd', attn, v).reshape(b, l, c)
            return o @ W_proj + b_proj
        ada = jax.nn.silu(c) @ W_ada + b_ada
        shift_msa, scale_msa, gate_msa, shift_mlp, scale_mlp, gate_mlp = jnp.split(ada, 6, axis=-1)
        h = _modulate(_layernorm(x), shift_msa, scale_msa)
        x = x + gate_msa * _attention(h, W_qkv, b_qkv, W_proj, b_proj)
        h = _modulate(_layernorm(x), shift_mlp, scale_mlp)
        mlp = jax.nn.gelu(h @ W_fc1 + b_fc1, approximate=True) @ W_fc2 + b_fc2
        x = x + gate_mlp * mlp
        return x

    def _L1_cond_ref(x, cond, P, W, b):
        import jax, jax.numpy as jnp
        import numpy as np
        from jax.scipy.linalg import expm
        N, D, COND_DIM = (144, 64, 144)
        B, T = (16, 128)

        def _rotation(cond, W, b):
            v = jax.nn.silu(cond) @ W.T + b
            iu, ju = jnp.triu_indices(D, k=1)
            A = jnp.zeros((cond.shape[0], D, D), dtype=v.dtype)
            A = A.at[:, iu, ju].set(v).at[:, ju, iu].set(-v)
            return expm(A)
        U, _ = jnp.linalg.qr(P)
        R = _rotation(cond, W, b)
        z = jnp.einsum('btn,nd->btd', x, U)
        z_rot = jnp.einsum('btd,bde->bte', z, R)
        x_rot = x + jnp.einsum('btd,nd->btn', z_rot - z, U)
        return x_rot
    x = _L0_cond_ref(x, cond_1152[:, None, :], L0_cond_W_qkv, L0_cond_b_qkv, L0_cond_W_proj, L0_cond_b_proj, L0_cond_W_fc1, L0_cond_b_fc1, L0_cond_W_fc2, L0_cond_b_fc2, L0_cond_W_ada, L0_cond_b_ada)
    x = _L1_cond_ref(x, cond_1152, L1_cond_P, L1_cond_W, L1_cond_b)
    return x

_drawn_inputs = setup_inputs


def setup_inputs(seed=0):
    import zlib

    import numpy as np

    out = dict(_drawn_inputs(seed))
    spreads = {'L0_cond_b_qkv': (0.0, 0.8),
     'L0_cond_b_proj': (0.0, 0.482),
     'L0_cond_b_fc1': (0.0, 0.8),
     'L0_cond_b_fc2': (0.0, 0.479),
     'L0_cond_b_ada': (0.0, 0.502)}
    factors = {'L0_cond_W_qkv': 8.0,
     'L0_cond_W_proj': 8.0,
     'L0_cond_W_fc1': 5.383,
     'L0_cond_W_fc2': 5.013}
    for name, (base, spread) in spreads.items():
        noise = np.random.default_rng([zlib.crc32(name.encode()), seed]).standard_normal(out[name].shape)
        drawn = base * np.exp(spread * noise) if base else spread * noise
        out[name] = jnp.asarray(drawn.astype(out[name].dtype))
    for name, factor in factors.items():
        out[name] = (out[name] * factor).astype(out[name].dtype)
    return out
```

```python
from contextlib import ExitStack
from math import factorial

import concourse.bass as bass
from concourse import mybir

ALU = mybir.AluOpType
ACT = mybir.ActivationFunctionType
AX = mybir.AxisListType
F32 = mybir.dt.float32
BF16 = mybir.dt.bfloat16
I32 = mybir.dt.int32


class Links:

    def __init__(self, eng, sem, apart=None):
        self.eng, self.sem, self.base, self.n, self.apart = eng, sem, 0, 0, apart

    def link(self, ins):
        self.n += 1
        ins.then_inc(self.sem, 1)
        wait(self.eng, self.sem, self.base + self.n, self.apart)

    def mark(self, ins):
        self.n += 1
        ins.then_inc(self.sem, 1)

    def rolled(self, body, first, last):
        start = self.n
        body(first)
        per = self.n - start
        if last == first:
            return
        if last == first + 1:
            body(last)
            return
        with self.eng.Fori(first + 1, last + 1) as i:
            outer_n, outer_base = self.n, self.base
            self.base, self.n = (i - (first + 1)) * per + (outer_base + outer_n), 0
            body(i)
            assert self.n == per
            self.base, self.n = outer_base, outer_n
        self.n += per * (last - first)


def wait(eng, sem, value, apart=None):
    if isinstance(value, int) and value <= 0:
        return
    eng.wait_ge(sem, value)
    if apart is not None and not isinstance(value, int):
        eng.sem_inc(apart, 1)


def adaln_block_then_rotation(nc, x, cond, W_qkv, b_qkv, W_proj, b_proj, W_fc1, b_fc1, W_fc2, b_fc2,
                              W_ada, b_ada, P, W, bvec, gates_dram, out):
    B, L, C = x.shape
    H = 16
    D = C // H
    FF = W_fc1.shape[1]
    RD = P.shape[1]
    NSK = W.shape[0]
    EPS = 1e-6
    SCALE = float(D) ** -0.5
    C1, C2 = 128, C - 128
    K2 = C2 + 1
    SL = 64
    NP6 = 6 * D
    NC = B // 2
    FK = FF // 128
    FR = FF - 128 * FK
    WP = 126
    WK = NSK // WP
    QR_PER_BATCH = RD // B
    N_ID, N_ALL = 16, 16
    SQ = 4
    THETA = 1.58
    XSQ = 12
    assert L == 128 and NSK == RD * (RD - 1) // 2 and WP * WK == NSK and B % 2 == 0

    with ExitStack() as ctx:
        def sb(name, shape, dt=F32):
            return ctx.enter_context(nc.sbuf_tensor(name, shape, dt))

        def sem(name):
            return ctx.enter_context(nc.semaphore(name))

        bank = [ctx.enter_context(nc.psum_tensor(f"bank{i}", [128, 512], F32)) for i in range(8)]

        x_all = sb("x_all", [128, B, C])
        cond_sb = sb("cond_sb", [B, C])
        wada1, wada2 = sb("wada1", [C1, 6 * C]), sb("wada2", [K2, 6 * C])
        wqkv1, wqkv2 = sb("wqkv1", [C1, 3 * C]), sb("wqkv2", [K2, 3 * C])
        wfc1a, wfc1b = sb("wfc1a", [C1, FF]), sb("wfc1b", [K2, FF])
        wfc2a, wfc2b = sb("wfc2a", [128, FK, C]), sb("wfc2b", [FR + 1, C])
        wproj = sb("wproj", [128, 4, C])
        wskew = sb("wskew", [WP, WK, C])
        wskT1, wskT2 = sb("wskT1", [C1, NSK]), sb("wskT2", [K2, NSK])
        p1, p2 = sb("p1", [C1, 2, RD]), sb("p2", [C2, 2, RD])
        ident = sb("ident", [128, 128])
        identb = sb("identb", [128, 128], BF16)
        eye2 = sb("eye2", [128, RD])
        ones = sb("ones", [128, 32])
        halves = sb("halves", [128, 128])
        lower = sb("lower", [128, RD])
        negmask = sb("negmask", [128, RD])
        headsel = sb("headsel", [128, 8, 128], BF16)
        zeros = sb("zeros", [128, 128])
        mhalf = sb("mhalf", [128, B])
        mone = sb("mone", [128, 1])
        sil = sb("sil", [B, C])
        sexp = sb("sexp", [B, C])
        sT1, sT2 = sb("sT1", [C1, B]), sb("sT2", [K2, B])
        mod1, mod2 = sb("mod1", [C1, 4, B]), sb("mod2", [C2, 4, B])
        gates_sb = sb("gates_sb", [B, 2 * C])
        gates = sb("gates", [128, B, 2 * C])
        stats = sb("stats", [128, B, 6])
        mv = sb("mv", [128, B, 2])
        rstd = sb("rstd", [128, B])
        xn = sb("xn", [128, C])
        hT1, hT2 = sb("hT1", [C1, 128]), sb("hT2", [K2, 128])
        qk32 = sb("qk32", [128, 2, C])
        res = sb("res", [128, 2, C])
        qs = sb("qs", [128, H, SL], BF16)
        ks = sb("ks", [128, H, SL], BF16)
        QT = sb("QT", [128, H // 2, 128], BF16)
        KT = sb("KT", [128, H // 2, 128], BF16)
        V = sb("V", [128, H, 32])
        nmax = sb("nmax", [128, 2, 8])
        nmr = sb("nmr", [128, 2, 8])
        NM = sb("NM", [128, 2, SL], BF16)
        NMT = sb("NMT", [128, 128], BF16)
        E = sb("E", [128, 2, 4, 128])
        rden = sb("rden", [128, 4, 128])
        ON = sb("ON", [128, 4, 128])
        tmp = sb("tmp", [128, C])
        gT = sb("gT", [128, FK + 1, 128])
        x2 = sb("x2", [128, C])
        xT1, xT2 = sb("xT1", [C1, 128]), sb("xT2", [C2, 128])
        zT = sb("zT", [RD, 128])
        M_all = sb("M_all", [RD, B, C])
        UT = sb("UT", [128, C])
        U1, U2 = sb("U1", [C1, RD]), sb("U2", [C2, RD])
        ET = sb("ET", [RD, 2, RD])
        PT = sb("PT", [RD, C])
        Z = sb("Z", [128, 3 * RD])
        zrow = sb("zrow", [128, 3 * RD])
        zupd = sb("zupd", [128, 3 * RD])
        sel = sb("sel", [RD, 2, 128])
        qc = sb("qc", [128, 12])
        zdiag = sb("zdiag", [128, 2])
        dG, dB, usc = sb("dG", [128, RD]), sb("dB", [128, RD]), sb("usc", [128, 4])
        v = sb("v", [B, NSK + 1])
        A0, Bm = sb("A0", [128, NC, RD]), sb("Bm", [128, NC, RD])
        Cm, Dm, Fm = sb("Cm", [128, NC, RD]), sb("Dm", [128, NC, RD]), sb("Fm", [128, NC, RD])
        eo = [sb(f"eo{i}", [128, NC, 2, RD]) for i in range(3)]
        T1 = sb("T1", [128, NC, 2, RD])
        Xm = sb("Xm", [128, NC, RD])
        Ym = sb("Ym", [128, NC, RD])
        rowsq = sb("rowsq", [128, NC])
        fro = sb("fro", [128, NC])
        over = sb("over", [128, NC, XSQ])
        nsc = sb("nsc", [128, NC])
        mstep = sb("mstep", [128, NC])
        flag = sb("flag", [1, 2], I32)

        s_ldc, s_lda, s_ldw, s_ldx, s_ldq, s_ldp, s_ldm, s_ldP = (
            sem(n) for n in ("s_ldc", "s_lda", "s_ldw", "s_ldx", "s_ldq", "s_ldp", "s_ldm", "s_ldP"))
        s_gst, s_gld, s_out = sem("s_gst"), sem("s_gld"), sem("s_out")
        o_dve, o_act, o_pool = sem("o_dve"), sem("o_act"), sem("o_pool")
        s_apart = [sem(f"s_apart{i}") for i in range(4)]
        k_id, k_zero, k_all = sem("k_id"), sem("k_zero"), sem("k_all")
        s_sil, s_sTp, s_sT, s_adaP, s_mod, s_gsb, s_wTp, s_wTd1, s_wTd2, s_vP, s_v = (
            sem(n) for n in ("s_sil", "s_sTp", "s_sT", "s_adaP", "s_mod", "s_gsb", "s_wTp", "s_wTd1", "s_wTd2", "s_vP", "s_v"))
        s_LP, s_L, s_LTp, s_B, s_rsq, s_frp, s_anyp, s_flag = (
            sem(n) for n in ("s_LP", "s_L", "s_LTp", "s_B", "s_rsq", "s_frp", "s_anyp", "s_flag"))
        s_Bs, s_nCp, s_C, s_DFp0, s_DFp, s_DF, s_hp, s_h, s_XY, s_over, s_sqp, s_sqX, s_sqY, s_xsp, s_xs, s_xd, s_R = (
            sem(n) for n in ("s_Bs", "s_nCp", "s_C", "s_DFp0", "s_DFp", "s_DF", "s_hp", "s_h", "s_XY", "s_over", "s_sqp",
                             "s_sqX", "s_sqY", "s_xsp", "s_xs", "s_xd", "s_R"))
        s_Gp, s_Z, s_var1, s_rstd1, s_var2, s_rstd2 = (
            sem(n) for n in ("s_Gp", "s_Z", "s_var1", "s_rstd1", "s_var2", "s_rstd2"))
        (s_xn, s_xnT, s_hT, s_qkv, s_qk32, s_V, s_qst, s_kst, s_QTp, s_KTp, s_QT, s_KT, s_S, s_max, s_nm,
         s_nmT, s_NMT, s_ST, s_E, s_pv, s_on, s_proj, s_x1, s_st1) = (
            sem(n) for n in ("s_xn", "s_xnT", "s_hT", "s_qkv", "s_qk32", "s_V", "s_qst", "s_kst", "s_QTp", "s_KTp",
                             "s_QT", "s_KT", "s_S", "s_max", "s_nm", "s_nmT", "s_NMT", "s_ST", "s_E", "s_pv",
                             "s_on", "s_proj", "s_x1", "s_st1"))
        s_sel, s_zbc, s_zrow, s_zupd = (sem(n) for n in ("s_sel", "s_zbc", "s_zrow", "s_zupd"))
        s_diag, s_dred, s_usc, s_ETp, s_ET, s_UTp, s_UT, s_Up, s_U, s_Mp, s_M = (
            sem(n) for n in ("s_diag", "s_dred", "s_usc", "s_ETp", "s_ET", "s_UTp", "s_UT", "s_Up", "s_U", "s_Mp", "s_M"))
        (m_xn, m_xnT, m_hT, m_fc1, m_gT, m_fc2, m_x2, m_x2T, m_xT, m_z, m_zT, m_rot, m_out) = (
            sem(n) for n in ("m_xn", "m_xnT", "m_hT", "m_fc1", "m_gT", "m_fc2", "m_x2", "m_x2T", "m_xT", "m_z",
                             "m_zT", "m_rot", "m_out"))

        def slot(h):
            g, p = h // 2, h % 2
            return g, p, 2 * (g // 4) + p, g % 4

        def head(q, i):
            return 2 * (4 * (q // 2) + i) + q % 2

        block = ctx.enter_context(nc.Block())

        @block.sync
        def _(sp):
            sp.dma_start(cond_sb[:, :], cond).then_inc(s_ldc, 16)
            wv = W.rearrange("(k p) c -> p k c", p=WP)
            for n in range(4):
                sp.dma_start(wskew[:, 4 * n:4 * n + 4, :], wv[:, 4 * n:4 * n + 4, :]).then_inc(s_ldw, 16)
            sp.dma_start(wskT2[C2:K2, :], bvec.rearrange("(a n) -> a n", a=1)).then_inc(s_ldw, 16)
            xv = x.rearrange("b t c -> t b c")
            for n in range(4):
                sp.dma_start(x_all[:, 4 * n:4 * n + 4, :], xv[:, 4 * n:4 * n + 4, :]).then_inc(s_ldx, 16)
            sp.dma_start(wfc1a[:, :], W_fc1[0:C1, :]).then_inc(s_ldm, 16)
            sp.dma_start(wfc1b[0:C2, :], W_fc1[C1:C, :]).then_inc(s_ldm, 16)
            sp.dma_start(wfc1b[C2:K2, :], b_fc1.rearrange("(a n) -> a n", a=1)).then_inc(s_ldm, 16)
            sp.dma_start(wfc2a[:, :, :], W_fc2[0:128 * FK, :].rearrange("(k p) n -> p k n", p=128)).then_inc(s_ldm, 16)
            sp.dma_start(wfc2b[0:FR, :], W_fc2[128 * FK:FF, :]).then_inc(s_ldm, 16)
            sp.dma_start(wfc2b[FR:FR + 1, :], b_fc2.rearrange("(a n) -> a n", a=1)).then_inc(s_ldm, 16)
            sp.wait_ge(s_gsb, 1)
            sp.dma_start(gates_dram, gates_sb[:, :]).then_inc(s_gst, 16)
            sp.wait_ge(s_gst, 16)
            gd = gates_dram.rearrange("(a b) n -> a (b n)", a=1)
            sp.dma_start(gates[:, :, :].rearrange("p b n -> p (b n)"),
                         gd.to_broadcast([128, B * 2 * C])).then_inc(s_gld, 16)

            def store(b):
                wait(sp, m_out, b + 1)
                sp.dma_start(out[bass.ds(b, 1), :, :].rearrange("a t c -> t (a c)"),
                             x_all[:, bass.ds(b, 1), :].rearrange("p a c -> p (a c)")).then_inc(s_out, 16)

            store(0)
            with sp.Fori(1, B) as b:
                store(b)
            sp.wait_ge(s_out, 16 * B)

        @block.gpsimd
        def _(pool):
            lk = Links(pool, o_pool, s_apart[0])
            link = lk.link
            made = {}

            def make(ins, done):
                made[done] = made.get(done, 0) + 1
                ins.then_inc(done, 1)
                pool.wait_ge(done, made[done])

            def diagonal(t, own=slice(0, 128)):
                size = t.shape[1]
                make(nc.gpsimd.affine_select(out=t, in_=zeros[own, 0:size], compare_op=ALU.not_equal, fill=1.0,
                                             base=0, pattern=[[-1, size]], channel_multiplier=1), k_id)

            def below_diagonal(t, own, fill):
                make(nc.gpsimd.affine_select(out=t, in_=zeros[own, 0:RD], compare_op=ALU.is_ge, fill=fill,
                                             base=0, pattern=[[1, RD]], channel_multiplier=-1), k_id)

            lo, hi = slice(0, 64), slice(64, 128)
            make(nc.gpsimd.memset(zeros[:, :], 0.0), k_zero)
            diagonal(ident[:, :])
            make(nc.gpsimd.memset(mhalf[:, :], -0.5), k_id)
            make(nc.gpsimd.memset(mone[:, :], -1.0), k_id)
            for own in (lo, hi):
                diagonal(eye2[own, :], own)
            for own in (lo, hi):
                below_diagonal(negmask[own, :], own, -1.0)
            make(nc.gpsimd.memset(sT2[:, :], 1.0), k_id)
            make(nc.gpsimd.memset(v[:, 0:1], 0.0), k_id)
            make(nc.gpsimd.memset(A0[:, :, :], 0.0), k_id)
            make(nc.gpsimd.memset(ones[:, :], 1.0), k_id)
            for own in (lo, hi):
                below_diagonal(lower[own, :], own, 1.0)
            make(nc.gpsimd.memset(halves[:, :], 0.0), k_id)
            make(nc.gpsimd.memset(halves[lo, 0:64], 1.0), k_id)
            make(nc.gpsimd.memset(halves[hi, 64:128], 1.0), k_id)
            made_id = made[k_id]
            make(nc.gpsimd.memset(wproj[:, :, :], 0.0), k_all)
            wp = W_proj.rearrange("(a i b d) n -> i a b d n", a=2, i=4, b=2)
            for i in range(4):
                for q in range(4):
                    pool.dma_start(wproj[32 * i:32 * i + D, q, :], wp[i, q // 2, q % 2, :, :]).then_inc(s_ldp, 16)
            pool.dma_start(wproj[D:D + 1, 0, :], b_proj.rearrange("(a n) -> a n", a=1)).then_inc(s_ldp, 16)
            make(nc.gpsimd.tensor_copy(identb[:, :], ident[:, :]), k_all)
            make(nc.gpsimd.memset(hT2[:, :], 1.0), k_all)
            make(nc.gpsimd.memset(qs[:, :, :], 0.0), k_all)
            make(nc.gpsimd.memset(ks[:, :, :], 0.0), k_all)
            make(nc.gpsimd.memset(NM[:, :, :], 0.0), k_all)
            make(nc.gpsimd.memset(V[:, :, :], 0.0), k_all)
            make(nc.gpsimd.memset(V[:, :, D:D + 1], 1.0), k_all)
            make(nc.gpsimd.memset(gT[:, FK, :], 1.0), k_all)
            make(nc.gpsimd.memset(headsel[:, :, :], 0.0), k_all)
            for own in (lo, hi):
                rows = headsel[own, :, :]
                for r in range(3):
                    make(nc.gpsimd.affine_select(out=rows, in_=rows, compare_op=ALU.not_equal, fill=1.0, base=-r,
                                                 pattern=[[-3, 8], [0, 128]], channel_multiplier=1), k_all)
            assert (made_id, made[k_all]) == (N_ID, N_ALL)

            def inverse_roots(seen, n, done):
                wait(pool, seen, n, s_apart[0])
                var = mv[:, :, 1:2].rearrange("p b a -> p (b a)")
                link(nc.gpsimd.tensor_scalar(rstd[:, :], var, EPS, None, ALU.add))
                nc.gpsimd.tensor_tensor(rstd[:, :], rstd[:, :], mhalf[:, :], ALU.pow).then_inc(done, 1)

            inverse_roots(s_var1, 1, s_rstd1)

            def split_q(b):
                wait(pool, s_qk32, 2 * b + 1, s_apart[0])
                wait(pool, s_QTp, b, s_apart[0])
                src = qk32[:, 0, :].rearrange("p (h a d) -> p h a d", h=H, a=1)
                r1 = res[:, 0, :].rearrange("p (h a d) -> p h a d", h=H, a=1)

                def part(s, n):
                    return qs[:, :, D * s:D * (s + n)].rearrange("p h (a d) -> p h a d", a=n)

                link(nc.gpsimd.tensor_copy(part(0, 3), src.to_broadcast([128, H, 3, D])))
                link(nc.gpsimd.tensor_tensor(r1, src, part(0, 1), ALU.subtract))
                link(nc.gpsimd.tensor_copy(part(3, 2), r1.to_broadcast([128, H, 2, D])))
                nc.gpsimd.tensor_tensor(part(5, 1), r1, part(3, 1), ALU.subtract).then_inc(s_qst, 1)

            def qr_select(k, n):
                wait(pool, s_zbc, k - 1, s_apart[0])
                nc.gpsimd.tensor_copy(sel[:, n % 2, :], ident[0:RD, bass.ds(k, 1)].to_broadcast([RD, 128])).then_inc(s_sel, 1)

            def qr_step(k):
                colG, colB, below, half_inv, r, inv, cG, c, sg, w, wi, cB = (qc[:, i:i + 1] for i in range(12))
                gkk, bkk = zdiag[:, 0:1], zdiag[:, 1:2]
                TT, TS, CP = nc.gpsimd.tensor_tensor, nc.gpsimd.tensor_scalar, nc.gpsimd.tensor_copy
                link(CP(colG, Z[:, bass.ds(k, 1)]))
                link(CP(colB, Z[:, bass.ds(k + 2 * RD, 1)]))
                link(CP(below, negmask[:, bass.ds(k, 1)]))
                wait(pool, s_zrow, 2 * k + 2, s_apart[0])
                lk.mark(TT(inv, gkk, mone[:, :], ALU.pow))
                lk.mark(TT(half_inv, gkk, mhalf[:, 0:1], ALU.pow))
                link(TS(sg, bkk, 0.0, 2.0, ALU.is_ge, ALU.mult))
                lk.mark(TS(cG, colG, inv, below, ALU.mult, ALU.mult))
                link(TT(r, gkk, half_inv, ALU.mult))
                lk.mark(TS(w, sg, 1.0, r, ALU.subtract, ALU.mult))
                link(TT(c, cG, bkk, ALU.mult))
                lk.mark(TT(w, w, bkk, ALU.add))
                link(TT(c, c, colB, ALU.add))
                link(TT(wi, w, mone[:, :], ALU.pow))
                lk.mark(TS(zupd[:, 0:2 * RD], zrow[:, 0:2 * RD], cG, None, ALU.mult))
                link(TS(cB, c, wi, below, ALU.mult, ALU.mult))
                link(TT(cB, cB, cG, ALU.add))
                link(TS(zupd[:, 2 * RD:3 * RD], zrow[:, 2 * RD:3 * RD], cB, None, ALU.mult))
                TT(Z[:, :], Z[:, :], zupd[:, :], ALU.add).then_inc(s_zupd, 1)

            def attention(b):
                for n in range(QR_PER_BATCH):
                    k = b * QR_PER_BATCH + n
                    qr_select(k, n)
                    qr_step(k)
                    if n == 1 and not (isinstance(b, int) and b == B - 1):
                        split_q(b + 1)
                    wait(pool, s_zupd, k + 1, s_apart[0])

            pool.wait_ge(k_all, N_ALL)
            split_q(0)
            pool.wait_ge(s_Z, 3)
            lk.rolled(attention, 0, B - 2)
            attention(B - 1)

            pool.wait_ge(s_zupd, RD)
            nc.gpsimd.tensor_tensor(dG[:, :], Z[:, 0:RD], eye2[:, :], ALU.mult).then_inc(s_diag, 1)
            nc.gpsimd.tensor_tensor(dB[:, :], Z[:, 2 * RD:3 * RD], eye2[:, :], ALU.mult).then_inc(s_diag, 1)
            pool.wait_ge(s_dred, 2)
            link(nc.gpsimd.tensor_tensor(usc[:, 2:3], usc[:, 0:1], mhalf[:, 0:1], ALU.pow))
            link(nc.gpsimd.tensor_scalar(usc[:, 3:4], usc[:, 1:2], 0.0, -2.0, ALU.is_ge, ALU.mult))
            nc.gpsimd.tensor_scalar(usc[:, 0:1], usc[:, 3:4], 1.0, usc[:, 2:3], ALU.add, ALU.mult).then_inc(s_usc, 1)
            inverse_roots(s_var2, 1, s_rstd2)

        @block.scalar
        def _(act):
            lk = Links(act, o_act)
            link = lk.link
            act.dma_start(wada1[:, :], W_ada[0:C1, :]).then_inc(s_lda, 16)
            act.dma_start(wada2[0:C2, :], W_ada[C1:C, :]).then_inc(s_lda, 16)
            act.dma_start(wada2[C2:K2, :], b_ada.rearrange("(a n) -> a n", a=1)).then_inc(s_lda, 16)
            act.dma_start(wqkv1[:, :], W_qkv[0:C1, :]).then_inc(s_ldq, 16)
            act.dma_start(wqkv2[0:C2, :], W_qkv[C1:C, :]).then_inc(s_ldq, 16)
            act.dma_start(wqkv2[C2:K2, :], b_qkv.rearrange("(a n) -> a n", a=1)).then_inc(s_ldq, 16)
            for p in range(2):
                act.dma_start(p1[:, p, :], P[0:C1, :]).then_inc(s_ldP, 16)
                act.dma_start(p2[:, p, :], P[C1:C, :]).then_inc(s_ldP, 16)
            act.wait_ge(s_ldc, 16)
            nc.scalar.activation(sexp[:, :], cond_sb[:, :], ACT.Exp, scale=-1.0).then_inc(s_sil, 1)
            for n in range(4):
                wait(act, s_wTp, n + 1)
                nc.scalar.activation(wskT1[:, 504 * n:504 * n + 504], bank[2 * (n % 2)][:, 0:504], ACT.Copy).then_inc(s_wTd1, 1)
            for n in range(4):
                wait(act, s_vP, n + 1)
                nc.scalar.activation(v[:, 1 + 504 * n:505 + 504 * n], bank[n][0:B, 0:504], ACT.Copy).then_inc(s_v, 1)
            for n in range(SQ):
                wait(act, s_sqp, 2 * n + 2)
                nc.scalar.activation(Ym[:, :, :].rearrange("p c n -> p (c n)"), bank[5][:, :], ACT.Copy).then_inc(s_sqY, 1)

            def modulated(b, tp, done, free, freed, row, src):
                wait(act, tp, b + 1)
                wait(act, free, freed)
                for t, m, n in ((hT1[:, :], mod1, C1), (hT2[0:C2, :], mod2, C2)):
                    nc.scalar.activation(t, src[0:n, (0 if n == C1 else 128):(128 if n == C1 else 256)], ACT.Identity,
                                         bias=m[:, row, bass.ds(b, 1)], scale=m[:, row + 1, bass.ds(b, 1)]).then_inc(done, 1)

            def k_transposed(b):
                wait(act, s_KTp, b + 1)
                wait(act, s_ST, 4 * b)
                nc.scalar.activation(KT[:, :, :].rearrange("p g t -> p (g t)"), bank[2][:, :].bitcast(BF16),
                                     ACT.Copy).then_inc(s_KT, 1)

            def qr_row(k):
                wait(act, s_zbc, k + 1)
                wait(act, s_zupd, k)
                for n, at in enumerate((0, 2 * RD)):
                    ins = nc.scalar.activation(zdiag[:, n:n + 1], bank[7][:, bass.ds(k + at, 1)], ACT.Copy)
                ins.then_inc(s_zrow, 1)
                nc.scalar.activation(zrow[:, :], bank[7][:, 0:3 * RD], ACT.Copy).then_inc(s_zrow, 1)

            def attention(b):
                more = not (isinstance(b, int) and b == B - 1)
                k = b * QR_PER_BATCH
                qr_row(k)
                if more:
                    modulated(b + 1, s_xnT, s_hT, s_qkv, b + 1, 0, bank[0])
                qr_row(k + 1)
                if more:
                    qkv_out_qk(b + 1)
                wait(act, s_nmT, b + 1)
                wait(act, s_ST, 4 * b)
                nc.scalar.activation(NMT[:, :], bank[0][:, 256:320].bitcast(BF16), ACT.Copy).then_inc(s_NMT, 1)
                for q in range(4):
                    wait(act, s_ST, 4 * b + q + 1)
                    wait(act, s_pv, 4 * b + q - 1)
                    nc.scalar.activation(E[:, q % 2, :, :].rearrange("p i t -> p (i t)"), bank[3 + q % 2][:, :],
                                         ACT.Exp).then_inc(s_E, 1)
                    if q == 1:
                        qr_row(k + 2)
                qr_row(k + 3)
                if more:
                    qkv_out_v(b + 1)
                    k_transposed(b + 1)

            def qkv_out_qk(b):
                wait(act, s_qkv, b + 1)
                wait(act, s_qst, b)
                nc.scalar.activation(qk32[:, 0, :], bank[1][:, 0:C], ACT.Copy, scale=SCALE).then_inc(s_qk32, 1)
                wait(act, s_kst, b)
                nc.scalar.activation(qk32[:, 1, :], bank[1][:, C:2 * C], ACT.Copy).then_inc(s_qk32, 1)

            def qkv_out_v(b):
                wait(act, s_pv, 4 * b)
                nc.scalar.activation(V[:, :, 0:D], bank[1][:, 2 * C:3 * C].rearrange("p (h d) -> p h d", h=H),
                                     ACT.Copy).then_inc(s_V, 1)

            act.wait_ge(s_mod, 4)
            act.wait_ge(k_all, N_ALL)
            modulated(0, s_xnT, s_hT, s_qkv, 0, 0, bank[0])
            qkv_out_qk(0)
            qkv_out_v(0)
            k_transposed(0)
            lk.rolled(attention, 0, B - 2)
            attention(B - 1)

            def gelu(b):
                wait(act, m_fc1, b + 1)
                wait(act, m_fc2, b)
                nc.scalar.activation(gT[:, 0:FK, :].rearrange("p k t -> p (k t)"), bank[1][:, :],
                                     ACT.Gelu_apprx_tanh).then_inc(m_gT, 1)
                nc.scalar.activation(gT[0:FR, FK, :], bank[2][0:FR, 0:128], ACT.Gelu_apprx_tanh).then_inc(m_gT, 1)

            def mlp(b):
                more = not (isinstance(b, int) and b == B - 1)
                if more:
                    modulated(b + 1, m_xnT, m_hT, m_fc1, b + 1, 2, bank[0])
                    gelu(b + 1)

            act.wait_ge(k_all, N_ALL)
            modulated(0, m_xnT, m_hT, m_fc1, 0, 2, bank[0])
            gelu(0)
            lk.rolled(mlp, 0, B - 2)

        @block.vector
        def _(dve):
            lk = Links(dve, o_dve)
            link = lk.link
            TT, TS, STT = nc.vector.tensor_tensor, nc.vector.tensor_scalar, nc.vector.scalar_tensor_tensor

            def flat(t):
                return t[:, :, :].rearrange("p c n -> p (c n)")

            dve.wait_ge(k_id, N_ID)
            dve.wait_ge(s_Gp, 1)
            nc.vector.tensor_copy(Z[:, 0:RD], bank[7][:, 0:RD]).then_inc(s_Z, 1)
            nc.vector.tensor_copy(Z[:, 2 * RD:3 * RD], bank[7][:, RD:2 * RD]).then_inc(s_Z, 1)
            nc.vector.tensor_copy(Z[:, RD:2 * RD], eye2[:, :]).then_inc(s_Z, 1)
            nc.vector.tensor_copy(PT[:, :], bank[7][0:RD, 2 * RD:2 * RD + C]).then_inc(s_Z, 1)
            dve.wait_ge(s_sil, 1)
            link(TS(sexp[:, :], sexp[:, :], 1.0, None, ALU.add))
            link(nc.vector.reciprocal(sexp[:, :], sexp[:, :]))
            TT(sil[:, :], cond_sb[:, :], sexp[:, :], ALU.mult).then_inc(s_sil, 1)
            dve.wait_ge(s_sTp, 1)
            dve.wait_ge(k_id, N_ID)
            nc.vector.tensor_copy(sT1[:, :], bank[6][0:C1, 0:B]).then_inc(s_sT, 1)
            nc.vector.tensor_copy(sT2[0:C2, :], bank[6][0:C2, B:2 * B]).then_inc(s_sT, 1)
            for n in range(4):
                wait(dve, s_wTp, n + 1)
                nc.vector.tensor_copy(wskT2[0:C2, 504 * n:504 * n + 504],
                                      bank[1 + 2 * (n % 2)][0:C2, 0:504]).then_inc(s_wTd2, 1)
            dve.wait_ge(s_adaP, 1)
            for m, n, o in ((mod1, C1, 0), (mod2, C2, 64)):
                ps = bank[6][0:n, o:o + 4 * B].rearrange("p (k a b) -> p k a b", k=2, a=2)
                mm = m[:, :, :].rearrange("p (k a) b -> p k a b", k=2)
                nc.vector.tensor_copy(mm[:, :, 0, :], ps[:, :, 0, :]).then_inc(s_mod, 1)
                TS(mm[:, :, 1, :], ps[:, :, 1, :], 1.0, None, ALU.add).then_inc(s_mod, 1)
            nc.vector.tensor_copy(gates_sb[:, :], bank[6][0:B, 128:128 + 2 * C]).then_inc(s_gsb, 1)
            dve.wait_ge(s_ldx, 64)
            for b in range(B):
                ins = nc.vector.bn_stats(stats[:, b, :], x_all[:, b, :])
            link(ins)
            for b in range(B):
                ins = nc.vector.bn_aggr(mv[:, b, :], stats[:, b, :])
            ins.then_inc(s_var1, 1)
            dve.wait_ge(k_id, N_ID)
            dve.wait_ge(s_LP, 1)
            TT(A0[:, :, 0:RD - 1].rearrange("p c i -> p i c"),
               bank[4][:, 0:(RD - 1) * NC].rearrange("p (i c) -> p i c", c=NC),
               lower[:, 0:RD - 1].rearrange("p (i a) -> p i a", a=1).to_broadcast([128, RD - 1, NC]),
               ALU.mult).then_inc(s_L, 1)
            dve.wait_ge(s_LTp, 1)
            dve.wait_ge(s_L, 1)
            link(TT(flat(Bm), flat(A0), bank[0][:, :], ALU.subtract))
            link(TT(flat(A0), flat(Bm), flat(Bm), ALU.mult))
            nc.vector.tensor_reduce(rowsq[:, :], A0[:, :, :], AX.X, ALU.add).then_inc(s_rsq, 1)
            dve.wait_ge(s_frp, 1)
            link(nc.vector.tensor_copy(fro[:, :], bank[1][:, 0:NC]))
            for i in range(XSQ):
                ins = TS(over[:, :, i], fro[:, :], 2 * (THETA * 2 ** (SQ + i)) ** 2, 0.5 ** (i + 1), ALU.is_gt, ALU.mult)
            link(ins)
            link(nc.vector.tensor_reduce(nsc[:, :], over[:, :, :], AX.X, ALU.add))
            link(TS(nsc[:, :], nsc[:, :], -(0.5 ** SQ), 0.5 ** SQ, ALU.mult, ALU.add))
            TT(Bm[:, :, :], Bm[:, :, :], nsc[:, :].rearrange("p (c a) -> p c a", a=1).to_broadcast([128, NC, RD]),
               ALU.mult).then_inc(s_Bs, 1)
            dve.wait_ge(s_Bs, 1)
            eye_c = eye2[:, :].rearrange("p (a n) -> p a n", a=1).to_broadcast([128, NC, RD])

            def ev(i):
                return eo[i][:, :, 0, :]

            def od(i):
                return eo[i][:, :, 1, :]

            dve.wait_ge(s_nCp, 1)
            nc.vector.tensor_copy(flat(Cm), bank[0][:, :]).then_inc(s_C, 1)
            dve.wait_ge(s_C, 1)
            for i in range(3):
                if i < 2:
                    ins = TS(ev(i), eye_c, 1.0 / factorial(4 * i), None, ALU.mult)
                else:
                    ins = TS(ev(i), eye_c, 1.0 / factorial(8), None, ALU.mult)
            link(ins)
            for i in range(3):
                ins = STT(ev(i), Cm[:, :, :], -1.0 / factorial(4 * i + 2), ev(i), ALU.mult, ALU.add)
            link(ins)
            dve.wait_ge(s_DFp, 1)
            link(nc.vector.tensor_copy(flat(Dm), bank[1][:, :]))
            nc.vector.tensor_copy(flat(Fm), bank[2][:, :]).then_inc(s_DF, 1)
            for i in range(3):
                ins = TS(od(i), Bm[:, :, :], 1.0 / factorial(4 * i + 1), None, ALU.mult)
            link(ins)
            for i in range(3):
                ins = STT(od(i), Dm[:, :, :], -1.0 / factorial(4 * i + 3), od(i), ALU.mult, ALU.add)
            dve.wait_ge(s_DF, 1)
            link(ins)
            STT(ev(2), Fm[:, :, :], 1.0 / factorial(12), ev(2), ALU.mult, ALU.add).then_inc(s_DF, 1)

            def halfbank(n):
                return bank[4 + n][:, :].rearrange("p (c e n) -> p c e n", c=NC // 2, e=2)

            for step, (dst, add) in enumerate(((T1, eo[1]), (eo[0], eo[0]))):
                for n in range(2):
                    cs = slice(n * NC // 2, (n + 1) * NC // 2)
                    wait(dve, s_hp, 2 * step + n + 1)
                    TT(dst[:, cs, :, :], halfbank(n), add[:, cs, :, :], ALU.add).then_inc(s_h, 1)
            dve.wait_ge(s_h, 4)
            TT(Xm[:, :, :], ev(0), od(0), ALU.add).then_inc(s_XY, 1)
            TT(Ym[:, :, :], ev(0), od(0), ALU.subtract).then_inc(s_XY, 1)
            for n in range(SQ):
                wait(dve, s_sqp, 2 * n + 2)
                nc.vector.tensor_copy(flat(Xm), bank[4][:, :]).then_inc(s_sqX, 1)
            dve.wait_ge(s_anyp, 1)
            link(nc.vector.tensor_reduce(nsc[0:32, 0:1], bank[1][0:32, NC:2 * NC], AX.X, ALU.add))
            nc.vector.tensor_copy(flag[0:1, 0:1], nsc[0:1, 0:1]).then_inc(s_flag, 1)
            dve.wait_ge(s_flag, 1)
            dve.wait_ge(s_sqY, SQ)
            dve.wait_ge(s_sqX, SQ)
            more_squarings = dve.value_load(flag[0:1, 0:1])
            with dve.If(more_squarings > 0):
                with dve.Fori(0, XSQ) as i:
                    wait(dve, s_xsp, i + 1)
                    take, keep = mstep[:, :], nsc[:, :]
                    o = over[:, :, bass.ds(i, 1)].rearrange("p c a -> p (c a)")
                    TS(take, o, 0.0, None, ALU.is_gt).then_inc(s_xd, 1)
                    TS(keep, o, 0.0, None, ALU.is_equal).then_inc(s_xd, 1)
                    wait(dve, s_xd, 8 * i + 2)
                    tb, kb = (t.rearrange("p (c a) -> p c a", a=1).to_broadcast([128, NC, RD]) for t in (take, keep))
                    for M, bk, T in ((Xm, 4, A0), (Ym, 5, Dm)):
                        TT(T[:, :, :], bank[bk][:, :].rearrange("p (c n) -> p c n", c=NC), tb, ALU.mult).then_inc(s_xd, 1)
                        TT(M[:, :, :], M[:, :, :], kb, ALU.mult).then_inc(s_xd, 1)
                    wait(dve, s_xd, 8 * i + 6)
                    TT(flat(Xm), flat(Xm), flat(A0), ALU.add).then_inc(s_xd, 1)
                    TT(flat(Ym), flat(Ym), flat(Dm), ALU.add).then_inc(s_xd, 1)
                    wait(dve, s_xd, 8 * i + 8)
                    dve.sem_inc(s_xs, 1)
            TT(Xm[:, :, :], Xm[:, :, :], eye_c, ALU.subtract).then_inc(s_R, 1)

            def normalized(b, free, done):
                wait(dve, free, b)
                TS(xn[:, :], x_all[:, bass.ds(b, 1), :].rearrange("p a c -> p (a c)"),
                   mv[:, bass.ds(b, 1), 0:1].rearrange("p a c -> p (a c)"), rstd[:, bass.ds(b, 1)],
                   ALU.subtract, ALU.mult).then_inc(done, 1)

            def split_k(b):
                wait(dve, s_qk32, 2 * b + 2)
                wait(dve, s_KTp, b)
                src = qk32[:, 1, :].rearrange("p (h a d) -> p h a d", h=H, a=1)
                r1 = res[:, 1, :].rearrange("p (h a d) -> p h a d", h=H, a=1)
                thirds = ks[:, :, 0:NP6].rearrange("p h (s e) -> p h s e", s=2)
                hi, mid = thirds[:, :, :, 0:D], thirds[:, :, :, D:2 * D]
                lk.mark(nc.vector.tensor_copy(ks[:, :, 5 * D:6 * D], src[:, :, 0, :]))
                link(nc.vector.tensor_copy(hi, src.to_broadcast([128, H, 2, D])))
                link(TT(r1, src, hi[:, :, 0:1, :], ALU.subtract))
                link(nc.vector.tensor_copy(mid, r1.to_broadcast([128, H, 2, D])))
                TT(ks[:, :, 2 * D:3 * D], r1[:, :, 0, :], mid[:, :, 0, :], ALU.subtract).then_inc(s_kst, 1)

            def q_transposed(b):
                wait(dve, s_QTp, b + 1)
                wait(dve, s_ST, 4 * b)
                nc.vector.tensor_copy(QT[:, :, :].rearrange("p g t -> p (g t)"),
                                      bank[2][:, :].bitcast(BF16)).then_inc(s_QT, 1)

            def attention(b):
                more = not (isinstance(b, int) and b == B - 1)
                if more:
                    normalized(b + 1, s_xnT, s_xn)
                for q in range(4):
                    wait(dve, s_S, 4 * b + q + 1)
                    nc.vector.tensor_reduce(nmax[:, q % 2, 4 * (q // 2):4 * (q // 2) + 4],
                                            bank[3 + q % 2][:, :].rearrange("p (i m) -> p i m", i=4),
                                            AX.X, ALU.max, negate=True).then_inc(s_max, 1)
                wait(dve, s_max, 4 * b + 4)
                wait(dve, s_nmT, b)
                parts = NM[:, :, 0:24].rearrange("p s (g r) -> p s g r", r=3)
                link(nc.vector.tensor_copy(parts[:, :, :, 0], nmax[:, :, :]))
                link(TT(nmr[:, :, :], nmax[:, :, :], parts[:, :, :, 0], ALU.subtract))
                link(nc.vector.tensor_copy(parts[:, :, :, 1], nmr[:, :, :]))
                TT(parts[:, :, :, 2], nmr[:, :, :], parts[:, :, :, 1], ALU.subtract).then_inc(s_nm, 1)
                if more:
                    split_k(b + 1)
                    q_transposed(b + 1)
                wait(dve, s_pv, 4 * b + 4)
                link(nc.vector.reciprocal(rden[:, :, :].rearrange("p q t -> p (q t)"), bank[6][:, :]))
                TT(ON[:, :, :].rearrange("p q t -> p (q t)"), bank[5][:, :],
                   rden[:, :, :].rearrange("p q t -> p (q t)"), ALU.mult).then_inc(s_on, 1)
                wait(dve, s_proj, b + 1)
                link(TT(tmp[:, :], bank[1][:, 0:C],
                        gates[:, bass.ds(b, 1), 0:C].rearrange("p a c -> p (a c)"), ALU.mult))
                xb = x_all[:, bass.ds(b, 1), :].rearrange("p a c -> p (a c)")
                TT(xb, xb, tmp[:, :], ALU.add).then_inc(s_x1, 1)
                wait(dve, s_x1, b + 1)
                nc.vector.bn_stats(stats[:, bass.ds(b, 1), :].rearrange("p a c -> p (a c)"), xb).then_inc(s_st1, 1)

            dve.wait_ge(s_rstd1, 1)
            dve.wait_ge(k_all, N_ALL)
            normalized(0, s_xnT, s_xn)
            split_k(0)
            q_transposed(0)
            dve.wait_ge(s_gld, 16)
            lk.rolled(attention, 0, B - 2)
            attention(B - 1)

            dve.wait_ge(s_st1, B)
            for b in range(B):
                ins = nc.vector.bn_aggr(mv[:, b, :], stats[:, b, :])
            ins.then_inc(s_var2, 1)
            dve.wait_ge(s_diag, 2)
            nc.vector.tensor_reduce(usc[:, 0:1], dG[:, :], AX.X, ALU.add).then_inc(s_dred, 1)
            nc.vector.tensor_reduce(usc[:, 1:2], dB[:, :], AX.X, ALU.add).then_inc(s_dred, 1)
            dve.wait_ge(s_ETp, 1)
            for p in range(2):
                nc.vector.tensor_copy(ET[:, p, :], bank[0][0:RD, 0:RD]).then_inc(s_ET, 1)
            dve.wait_ge(s_UTp, 1)
            dve.wait_ge(s_usc, 1)
            TS(UT[:, :], bank[1][:, 0:C], usc[:, 0:1], None, ALU.mult).then_inc(s_UT, 1)
            dve.wait_ge(s_rstd2, 1)
            normalized(0, m_xnT, m_xn)
            dve.wait_ge(s_Up, 1)
            nc.vector.tensor_copy(U1[:, :], bank[1][:, 0:RD]).then_inc(s_U, 1)
            nc.vector.tensor_copy(U2[:, :], bank[1][0:C2, RD:2 * RD]).then_inc(s_U, 1)
            for p in range(2):
                dve.wait_ge(s_Mp, p + 1)
                for n in range(3):
                    cnt = 3 if n < 2 else 2
                    dst = M_all[:, :, :].rearrange("d (c b) n -> d c b n", b=2)[:, 3 * n:3 * n + cnt, p, :]
                    nc.vector.tensor_copy(dst, bank[2 + 3 * p + n][0:RD, 0:cnt * C].rearrange(
                        "d (c n) -> d c n", c=cnt)).then_inc(s_M, 1)

            def mlp(b):
                more = not (isinstance(b, int) and b == B - 1)
                if more:
                    normalized(b + 1, m_xnT, m_xn)
                xb = x_all[:, bass.ds(b, 1), :].rearrange("p a c -> p (a c)")
                wait(dve, m_fc2, b + 1)
                link(TT(tmp[:, :], bank[3][:, 0:C],
                        gates[:, bass.ds(b, 1), C:2 * C].rearrange("p a c -> p (a c)"), ALU.mult))
                TT(x2[:, :], tmp[:, :], xb, ALU.add).then_inc(m_x2, 1)
                wait(dve, m_x2T, b + 1)
                nc.vector.tensor_copy(xT1[:, :], bank[4][:, 0:128]).then_inc(m_xT, 1)
                nc.vector.tensor_copy(xT2[:, :], bank[4][0:C2, 128:256]).then_inc(m_xT, 1)
                wait(dve, m_z, b + 1)
                nc.vector.tensor_copy(zT[:, :], bank[5][0:RD, 0:128]).then_inc(m_zT, 1)
                wait(dve, m_rot, b + 1)
                wait(dve, m_x2, b + 1)
                TT(xb, x2[:, :], bank[6][:, 0:C], ALU.add).then_inc(m_out, 1)

            lk.rolled(mlp, 0, B - 2)
            mlp(B - 1)

        @block.tensor
        def _(pe):
            mm = nc.tensor.matmul
            pe.wait_ge(s_ldP, 64)
            pe.wait_ge(k_id, N_ID)

            def twice(t):
                return t.rearrange("p a n -> p (a n)")

            mm(bank[7][:, 0:RD], twice(p1[:, :, :]), p1[:, 0, :], start=True, stop=False)
            mm(bank[7][:, 0:RD], twice(p2[:, :, :]), p2[:, 0, :], start=False, stop=True)
            mm(bank[7][:, RD:2 * RD], twice(p1[0:RD, :, :]), ident[0:RD, 0:RD], start=True, stop=True)
            mm(bank[7][0:RD, 2 * RD:2 * RD + C1], p1[:, 0, :], ident[:, :], start=True, stop=True)
            mm(bank[7][0:RD, 2 * RD + C1:2 * RD + C], p2[:, 0, :], ident[0:C2, 0:C2], start=True, stop=True).then_inc(s_Gp, 1)
            pe.wait_ge(s_sil, 2)
            pe.transpose(bank[6][0:C1, 0:B], sil[:, 0:C1], ident[0:B, 0:B])
            pe.transpose(bank[6][0:C2, B:2 * B], sil[:, C1:C], ident[0:B, 0:B]).then_inc(s_sTp, 1)
            for n in range(4):
                pe.wait_ge(s_ldw, 80)
                wait(pe, s_wTd1, n - 1)
                wait(pe, s_wTd2, n - 1)
                for j in range(4):
                    pe.transpose(bank[2 * (n % 2)][:, WP * j:WP * j + WP], wskew[:, 4 * n + j, 0:C1], ident[0:WP, 0:WP])
                    ins = pe.transpose(bank[1 + 2 * (n % 2)][0:C2, WP * j:WP * j + WP], wskew[:, 4 * n + j, C1:C],
                                       ident[0:WP, 0:WP])
                ins.then_inc(s_wTp, 1)
            pe.wait_ge(s_sT, 2)
            pe.wait_ge(s_lda, 48)
            for kind, col in enumerate((0, 1, 3, 4)):
                for o, c0, n in ((0, 0, C1), (64, C1, C2)):
                    cols = slice(col * C + c0, col * C + c0 + n)
                    dst = bank[6][0:n, o + B * kind:o + B * kind + B]
                    mm(dst, wada1[:, cols], sT1[:, :], start=True, stop=False)
                    mm(dst, wada2[:, cols], sT2[:, :], start=False, stop=True)
            for n, col in enumerate((2, 5)):
                dst = bank[6][0:B, 128 + C * n:128 + C * n + C]
                mm(dst, sT1[:, :], wada1[:, col * C:col * C + C], start=True, stop=False)
                ins = mm(dst, sT2[:, :], wada2[:, col * C:col * C + C], start=False, stop=True)
            ins.then_inc(s_adaP, 1)
            pe.wait_ge(s_wTd1, 4)
            pe.wait_ge(s_wTd2, 4)
            for n in range(4):
                mm(bank[n][0:B, 0:504], sT1[:, :], wskT1[:, 504 * n:504 * n + 504], start=True, stop=False)
                mm(bank[n][0:B, 0:504], sT2[:, :], wskT2[:, 504 * n:504 * n + 504], start=False, stop=True).then_inc(s_vP, 1)
            pe.wait_ge(s_v, 4)
            for i in range(RD - 1):
                at = (RD - 1) * i - i * (i - 1) // 2 - i
                for p in range(2):
                    ins = mm(bank[4][64 * p:64 * p + RD, NC * i:NC * i + NC], v[:, at:at + RD],
                             ident[0:B, p:B:2], start=True, stop=True)
            ins.then_inc(s_LP, 1)

            def both(c):
                for p in range(2):
                    yield slice(64 * p, 64 * p + 64), slice(RD * c, RD * c + RD)

            def product(bk, lhs, rhs, done):
                for c in range(NC):
                    for own, cols in both(c):
                        ins = mm(bank[bk][own, cols], lhs[own, c, :], rhs[own, c, :], start=True, stop=True)
                ins.then_inc(done, 1)

            pe.wait_ge(s_L, 1)
            for c in range(NC):
                for own, cols in both(c):
                    ins = mm(bank[0][own, cols], A0[own, c, :], eye2[own, :], start=True, stop=True)
            ins.then_inc(s_LTp, 1)
            pe.wait_ge(s_rsq, 1)
            mm(bank[1][:, 0:NC], halves[:, :], rowsq[:, :], start=True, stop=True).then_inc(s_frp, 1)
            pe.wait_ge(s_Bs, 1)
            product(0, Bm, Bm, s_nCp)
            pe.wait_ge(s_C, 1)
            product(1, Cm, Bm, s_DFp0)
            product(2, Cm, Cm, s_DFp)
            pe.wait_ge(s_DF, 2)
            for step, src in enumerate((eo[2], T1)):
                for n in range(2):
                    if step:
                        pe.wait_ge(s_h, 2)
                    for c in range(NC // 2):
                        for p in range(2):
                            own = slice(64 * p, 64 * p + 64)
                            cc = n * NC // 2 + c
                            ins = mm(bank[4 + n][own, 128 * c:128 * c + 128], Fm[own, cc, :],
                                     src[own, cc, :, :].rearrange("p e n -> p (e n)"), start=True, stop=True)
                    ins.then_inc(s_hp, 1)
            pe.wait_ge(s_XY, 2)
            for n in range(SQ):
                wait(pe, s_sqX, n)
                wait(pe, s_sqY, n)
                product(4, Ym, Xm, s_sqp)
                product(5, Xm, Ym, s_sqp)
            mm(bank[1][0:32, NC:2 * NC], ones[:, :], over[:, :, 0], start=True, stop=True).then_inc(s_anyp, 1)
            pe.wait_ge(s_flag, 1)
            more_squarings = pe.value_load(flag[0:1, 0:1])
            with pe.If(more_squarings > 0):
                pe.wait_ge(s_sqX, SQ)
                pe.wait_ge(s_sqY, SQ)
                pe.sem_inc(s_xs, 1)
                with pe.Fori(0, XSQ) as i:
                    wait(pe, s_xs, i + 1, s_apart[1])
                    for c in range(NC):
                        for own, cols in both(c):
                            mm(bank[4][own, cols], Ym[own, c, :], Xm[own, c, :], start=True, stop=True)
                            ins = mm(bank[5][own, cols], Xm[own, c, :], Ym[own, c, :], start=True, stop=True)
                    ins.then_inc(s_xsp, 1)

            def transposed(b, src_ready, done, free, freed):
                wait(pe, src_ready, b + 1)
                wait(pe, free, freed)
                pe.transpose(bank[0][:, 0:128], xn[:, 0:C1], ident[:, :])
                pe.transpose(bank[0][0:C2, 128:256], xn[:, C1:C], ident[:, :]).then_inc(done, 1)

            def qkv(b):
                wait(pe, s_hT, 2 * b + 2)
                wait(pe, s_x1, b - 1)
                mm(bank[1][:, 0:3 * C], hT1[:, :], wqkv1[:, :], start=True, stop=False)
                mm(bank[1][:, 0:3 * C], hT2[:, :], wqkv2[:, :], start=False, stop=True).then_inc(s_qkv, 1)

            def stack_T(b, stack, ready, done, free, freed):
                wait(pe, ready, b + 1)
                wait(pe, free, freed)
                for g in range(H // 2):
                    ins = pe.transpose(bank[2][:, 64 * g:64 * g + 64].bitcast(BF16),
                                       stack[:, 2 * g:2 * g + 2, :].rearrange("p h s -> p (h s)"), identb[:, :])
                ins.then_inc(done, 1)

            def scores(q, b):
                for i in range(4):
                    g, p, _, _ = slot(head(q, i))
                    own = slice(64 * p, 64 * p + NP6)
                    ins = mm(bank[3 + q % 2][:, 128 * i:128 * i + 128], QT[own, g, :], KT[own, g, :],
                             start=True, stop=True)
                ins.then_inc(s_S, 1)

            def scores_T(q, b):
                for i in range(4):
                    g, p, _, _ = slot(head(q, i))
                    dst = bank[3 + q % 2][:, 128 * i:128 * i + 128]
                    own, mx = slice(64 * p, 64 * p + NP6), slice(64 * p, 64 * p + 24)
                    mm(dst, KT[own, g, :], QT[own, g, :], start=True, stop=False)
                    ins = mm(dst, headsel[mx, g, :], NMT[mx, :], start=False, stop=True)
                ins.then_inc(s_ST, 1)

            def values(q, b):
                wait(pe, s_E, 4 * b + q + 1)
                for i in range(4):
                    own, cols = slice(32 * i, 32 * i + 32), slice(128 * q, 128 * q + 128)
                    mm(bank[5][own, cols], V[:, head(q, i), :], E[:, q % 2, i, :], start=True, stop=True)
                for i in range(4):
                    own, cols = slice(32 * i, 32 * i + 32), slice(128 * q, 128 * q + 128)
                    ins = mm(bank[6][own, cols], ones[:, :], E[:, q % 2, i, :], start=True, stop=True)
                ins.then_inc(s_pv, 1)

            def qr_row(k, n):
                wait(pe, s_sel, k + 1)
                wait(pe, s_zupd, k)
                wait(pe, s_zrow, 2 * k)
                mm(bank[7][:, 0:3 * RD], sel[:, n % 2, :], Z[0:RD, :], start=True, stop=True).then_inc(s_zbc, 1)

            def attention(b):
                more = not (isinstance(b, int) and b == B - 1)
                k = b * QR_PER_BATCH
                wait(pe, s_QT, b + 1)
                wait(pe, s_KT, b + 1)
                wait(pe, s_E, 4 * b - 1)
                scores(0, b)
                wait(pe, s_E, 4 * b)
                scores(1, b)
                qr_row(k, 0)
                if more:
                    transposed(b + 1, s_xn, s_xnT, s_NMT, b)
                wait(pe, s_max, 4 * b + 1)
                scores(2, b)
                wait(pe, s_max, 4 * b + 2)
                scores(3, b)
                qr_row(k + 1, 1)
                if more:
                    qkv(b + 1)
                wait(pe, s_nm, b + 1)
                wait(pe, s_hT, 2 * b + 4 if more else 2 * b + 2)
                pe.transpose(bank[0][:, 256:320].bitcast(BF16), NM[:, :, :].rearrange("p s n -> p (s n)"),
                             identb[:, :]).then_inc(s_nmT, 1)
                wait(pe, s_NMT, b + 1)
                wait(pe, s_max, 4 * b + 4)
                scores_T(0, b)
                scores_T(1, b)
                qr_row(k + 2, 2)
                wait(pe, s_on, b)
                if isinstance(b, int) and b == 0:
                    pe.wait_ge(s_V, 1)
                else:
                    wait(pe, s_V, b + 1)
                values(0, b)
                scores_T(2, b)
                values(1, b)
                scores_T(3, b)
                values(2, b)
                if more:
                    stack_T(b + 1, qs, s_qst, s_QTp, s_KT, b + 1)
                qr_row(k + 3, 3)
                values(3, b)
                if more:
                    stack_T(b + 1, ks, s_kst, s_KTp, s_QT, b + 2)
                    pe.wait_ge(s_qk32, 2 * b + 4)
                    wait(pe, s_V, b + 2)
                wait(pe, s_on, b + 1)
                for q in range(4):
                    ins = mm(bank[1][:, 0:C], ON[:, q, :], wproj[:, q, :], start=(q == 0), stop=(q == 3))
                ins.then_inc(s_proj, 1)

            pe.wait_ge(s_ldq, 48)
            pe.wait_ge(k_all, N_ALL)
            transposed(0, s_xn, s_xnT, s_R, 1)
            pe.wait_ge(s_R, 1)
            qkv(0)
            stack_T(0, qs, s_qst, s_QTp, s_QT, 0)
            stack_T(0, ks, s_kst, s_KTp, s_QT, 1)
            pe.wait_ge(s_Z, 4)
            pe.wait_ge(s_ldp, 16 * 17)
            rolled(pe, attention, 0, B - 2)
            attention(B - 1)

            pe.wait_ge(s_zupd, RD)
            pe.wait_ge(s_NMT, B)
            pe.transpose(bank[0][0:RD, 0:RD], Z[0:RD, RD:2 * RD], ident[0:RD, 0:RD]).then_inc(s_ETp, 1)
            pe.wait_ge(s_ET, 2)
            pe.wait_ge(s_x1, B)
            mm(bank[1][:, 0:C], twice(ET[:, :, :]), PT[:, :], start=True, stop=True).then_inc(s_UTp, 1)
            pe.wait_ge(s_UT, 1)
            pe.transpose(bank[1][:, 0:RD], UT[0:RD, 0:C1], ident[0:RD, 0:RD])
            pe.transpose(bank[1][0:C2, RD:2 * RD], UT[0:RD, C1:C], ident[0:RD, 0:RD]).then_inc(s_Up, 1)
            pe.wait_ge(s_E, 4 * B)
            pe.wait_ge(s_on, B)
            pe.wait_ge(s_zrow, 2 * RD)
            for p in range(2):
                own = slice(64 * p, 64 * p + 64)
                for c in range(NC):
                    ins = mm(bank[2 + 3 * p + c // 3][0:RD, C * (c % 3):C * (c % 3) + C], Xm[own, c, :], UT[own, :],
                             start=True, stop=True)
                ins.then_inc(s_Mp, 1)

            def fc1(b):
                wait(pe, m_hT, 2 * b + 2)
                wait(pe, m_gT, 2 * b)
                for k in range(FK + 1):
                    n = 128 if k < FK else FR
                    dst = bank[1][:, 128 * k:128 * k + 128] if k < FK else bank[2][0:FR, 0:128]
                    mm(dst, wfc1a[:, 128 * k:128 * k + n], hT1[:, :], start=True, stop=False)
                    ins = mm(dst, wfc1b[:, 128 * k:128 * k + n], hT2[:, :], start=False, stop=True)
                ins.then_inc(m_fc1, 1)

            def fc2(b):
                wait(pe, m_gT, 2 * b + 2)
                wait(pe, m_x2, b)
                for k in range(FK):
                    mm(bank[3][:, 0:C], gT[:, k, :], wfc2a[:, k, :], start=(k == 0), stop=False)
                mm(bank[3][:, 0:C], gT[0:FR + 1, FK, :], wfc2b[:, :], start=False, stop=True).then_inc(m_fc2, 1)

            def rotation(b):
                wait(pe, m_x2, b + 1)
                wait(pe, m_xT, 2 * b)
                pe.transpose(bank[4][:, 0:128], x2[:, 0:C1], ident[:, :])
                pe.transpose(bank[4][0:C2, 128:256], x2[:, C1:C], ident[:, :]).then_inc(m_x2T, 1)
                wait(pe, m_xT, 2 * b + 2)
                wait(pe, m_zT, b)
                mm(bank[5][0:RD, 0:128], U1[:, :], xT1[:, :], start=True, stop=False)
                mm(bank[5][0:RD, 0:128], U2[:, :], xT2[:, :], start=False, stop=True).then_inc(m_z, 1)
                wait(pe, m_zT, b + 1)
                wait(pe, m_out, b)
                mm(bank[6][:, 0:C], zT[:, :], M_all[:, bass.ds(b, 1), :].rearrange("p a c -> p (a c)"),
                   start=True, stop=True).then_inc(m_rot, 1)

            def mlp(b):
                more = not (isinstance(b, int) and b == B - 1)
                if more:
                    transposed(b + 1, m_xn, m_xnT, m_hT, 2 * b + 2)
                fc2(b)
                if more:
                    fc1(b + 1)
                rotation(b)

            pe.wait_ge(s_ldm, 96)
            transposed(0, m_xn, m_xnT, s_ET, 2)
            pe.wait_ge(s_U, 2)
            pe.wait_ge(s_M, 6)
            fc1(0)
            rolled(pe, mlp, 0, B - 2)
            mlp(B - 1)


def rolled(eng, body, first, last):
    body(first)
    with eng.Fori(first + 1, last + 1) as i:
        body(i)


_INS = ["x", "cond_1152", "L0_cond_W_qkv", "L0_cond_b_qkv", "L0_cond_W_proj", "L0_cond_b_proj", "L0_cond_W_fc1",
        "L0_cond_b_fc1", "L0_cond_W_fc2", "L0_cond_b_fc2", "L0_cond_W_ada", "L0_cond_b_ada", "L1_cond_P", "L1_cond_W",
        "L1_cond_b"]


def kernel(**inputs):
    import numpy as _np
    import concourse.bacc as _bacc
    from concourse import mybir as _mybir
    from concourse.bass_utils import run_bass_kernel_spmd as _run

    nc = _bacc.Bacc("TRN2", target_bir_lowering=False, num_devices=1)
    arrays, args = {}, []
    for name in _INS:
        a = _np.ascontiguousarray(inputs[name])
        arrays[f"in_{name}_dram"] = a
        args.append(nc.dram_tensor(f"in_{name}_dram", a.shape, _mybir.dt.from_np(a.dtype), kind="ExternalInput").ap())
    B, L, C = inputs["x"].shape
    args.append(nc.dram_tensor("gates_dram", (B, 2 * C), _mybir.dt.float32, kind="Internal").ap())
    args.append(nc.dram_tensor("out_dram", (B, L, C), _mybir.dt.float32, kind="ExternalOutput").ap())
    adaln_block_then_rotation(nc, *args)
    r = _run(nc, [arrays], core_ids=[0])
    return r.results[0]["out_dram"]
```

```python
from contextlib import ExitStack
from math import factorial

import concourse.bass as bass
from concourse import mybir

ALU = mybir.AluOpType
ACT = mybir.ActivationFunctionType
AX = mybir.AxisListType
F32 = mybir.dt.float32
BF16 = mybir.dt.bfloat16
I32 = mybir.dt.int32


class Links:

    def __init__(self, eng, sem, apart=None):
        self.eng, self.sem, self.base, self.n, self.apart = eng, sem, 0, 0, apart

    def link(self, ins):
        self.n += 1
        ins.then_inc(self.sem, 1)
        wait(self.eng, self.sem, self.base + self.n, self.apart)

    def mark(self, ins):
        self.n += 1
        ins.then_inc(self.sem, 1)
        return self.n

    def need(self, mark):
        wait(self.eng, self.sem, self.base + mark, self.apart)

    def paired(self, body, per, last):
        for b in (-1, 0, 1):
            body(b, b % 2)
        with self.eng.Fori(1, (last + 1) // 2) as i:
            outer_n, outer_base = self.n, self.base
            self.base, self.n = (i - 1) * (2 * per) + (outer_base + outer_n), 0
            for parity in range(2):
                body(2 * i + parity, parity)
            assert self.n == 2 * per, self.n
            self.base, self.n = outer_base, outer_n
        self.n += per * (last - 1)
        for b in range(last + 1, last + 5):
            body(b, b % 2)

    def rolled(self, body, first, last):
        start = self.n
        body(first)
        per = self.n - start
        if last == first:
            return
        if last == first + 1:
            body(last)
            return
        with self.eng.Fori(first + 1, last + 1) as i:
            outer_n, outer_base = self.n, self.base
            self.base, self.n = (i - (first + 1)) * per + (outer_base + outer_n), 0
            body(i)
            assert self.n == per
            self.base, self.n = outer_base, outer_n
        self.n += per * (last - first)


def wait(eng, sem, value, apart=None):
    if isinstance(value, int) and value <= 0:
        return
    eng.wait_ge(sem, value)
    if apart is not None and not isinstance(value, int):
        eng.sem_inc(apart, 1)


def adaln_block_then_rotation(nc, x, cond, W_qkv, b_qkv, W_proj, b_proj, W_fc1, b_fc1, W_fc2, b_fc2,
                              W_ada, b_ada, P, W, bvec, gates_dram, out):
    B, L, C = x.shape
    H = 16
    D = C // H
    FF = W_fc1.shape[1]
    RD = P.shape[1]
    NSK = W.shape[0]
    EPS = 1e-6
    SCALE = float(D) ** -0.5
    C1, C2 = 128, C - 128
    K2 = C2 + 1
    SL = 64
    NP6 = 6 * D
    NC = B // 2
    FK = FF // 128
    FR = FF - 128 * FK
    WP = 126
    WK = NSK // WP
    QB = RD // B
    N_ID, N_ALL = 15, 30
    SQ = 4
    THETA = 1.58
    XSQ = 12
    assert L == 128 and NSK == RD * (RD - 1) // 2 and WP * WK == NSK and B % 2 == 0

    with ExitStack() as ctx:
        def sb(name, shape, dt=F32):
            return ctx.enter_context(nc.sbuf_tensor(name, shape, dt))

        def sem(name):
            return ctx.enter_context(nc.semaphore(name))

        bank = [ctx.enter_context(nc.psum_tensor(f"bank{i}", [128, 512], F32)) for i in range(8)]

        x_all = sb("x_all", [128, B, C])
        cond_sb = sb("cond_sb", [B, C])
        wada1, wada2 = sb("wada1", [C1, 6 * C]), sb("wada2", [K2, 6 * C])
        wqkv1, wqkv2 = sb("wqkv1", [C1, 3 * C]), sb("wqkv2", [128, 3 * C])
        wfc1a, wfc1b = sb("wfc1a", [C1, FF]), sb("wfc1b", [128, FF])
        wfc2a, wfc2b = sb("wfc2a", [128, FK, C]), sb("wfc2b", [FR + 1, C])
        wproj = sb("wproj", [128, 4, C])
        wskew = sb("wskew", [WP, WK, C])
        wskT1, wskT2 = sb("wskT1", [C1, NSK]), sb("wskT2", [K2, NSK])
        p1, p2 = sb("p1", [C1, 2, RD]), sb("p2", [C2, 2, RD])
        ident = sb("ident", [128, 128])
        identb = sb("identb", [128, 128], BF16)
        eye2 = sb("eye2", [128, RD])
        ones = sb("ones", [128, 32])
        halves = sb("halves", [128, 128])
        lower = sb("lower", [128, RD])
        negmask = sb("negmask", [128, RD])
        headsel = sb("headsel", [128, 2, 8, 128], BF16)
        zeros = sb("zeros", [128, 128])
        mhalf = sb("mhalf", [128, B])
        sumsel = sb("sumsel", [128, 4, 32])
        sumrow = sb("sumrow", [128, 4, 128])
        sil = sb("sil", [B, C])
        sexp = sb("sexp", [B, C])
        sT1, sT2 = sb("sT1", [C1, B]), sb("sT2", [K2, B])
        mod1, mod2 = sb("mod1", [C1, 4, B]), sb("mod2", [C2, 4, B])
        gates_sb = sb("gates_sb", [B, 2 * C])
        gates = sb("gates", [128, B, 2 * C])
        stats = sb("stats", [128, B, 6])
        mv = sb("mv", [128, B, 2])
        rstd = sb("rstd", [128, B])
        xn = sb("xn", [128, C])
        hT1, hT2 = sb("hT1", [C1, 128]), sb("hT2", [128, 128])
        qk32 = sb("qk32", [128, 2, C])
        res = sb("res", [128, 2, C])
        qs = sb("qs", [128, H, SL], BF16)
        ks = sb("ks", [128, H, SL], BF16)
        QT = [[sb(f"QT{p}{n}", [128, H // 4, 128], BF16) for n in range(2)] for p in range(2)]
        KT = [[sb(f"KT{p}{n}", [128, 2, H // 4, 128], BF16) for n in range(2)] for p in range(2)]
        V = [sb(f"V{p}", [128, H, 32]) for p in range(2)]
        nmax = sb("nmax", [128, 2, 8])
        nmr = sb("nmr", [128, 2, 8])
        NM = sb("NM", [128, 2, SL], BF16)
        NMT = sb("NMT", [128, 128], BF16)
        E = sb("E", [128, 4, 4, 128])
        Osb = sb("Osb", [128, 512])
        rsum = sb("rsum", [128, 128])
        ON = sb("ON", [128, 4, 128])
        tmp = sb("tmp", [128, C])
        gT = sb("gT", [128, FK + 1, 128])
        x2 = sb("x2", [128, C])
        xT1, xT2 = sb("xT1", [C1, 128]), sb("xT2", [C2, 128])
        zT = sb("zT", [RD, 128])
        M_all = sb("M_all", [RD, B, C])
        UT = sb("UT", [128, C])
        U1, U2 = sb("U1", [C1, RD]), sb("U2", [C2, RD])
        ET = sb("ET", [RD, 2, RD])
        PT = sb("PT", [RD, C])
        Z = sb("Z", [128, 3 * RD])
        sel = sb("sel", [128, QB, 128])
        rec = sb("rec", [128, RD])
        root, root2 = sb("root", [128, RD]), sb("root2", [128, RD])
        cG = sb("cG", [128, RD])
        cB, c, w = sb("cB", [128, 1]), sb("c", [128, 1]), sb("w", [128, 1])
        dG, dB, usc = sb("dG", [128, RD]), sb("dB", [128, RD]), sb("usc", [128, 4])
        v = sb("v", [B, NSK + 1])
        A0, Bm = sb("A0", [128, NC, RD]), sb("Bm", [128, NC, RD])
        Cm, Dm, Fm = sb("Cm", [128, NC, RD]), sb("Dm", [128, NC, RD]), sb("Fm", [128, NC, RD])
        eo = [sb(f"eo{i}", [128, NC, 2, RD]) for i in range(3)]
        T1 = sb("T1", [128, NC, 2, RD])
        Xm = sb("Xm", [128, NC, RD])
        Ym = sb("Ym", [128, NC, RD])
        rowsq = sb("rowsq", [128, NC])
        fro = sb("fro", [128, NC])
        over = sb("over", [128, NC, XSQ])
        nsc = sb("nsc", [128, NC])
        mstep = sb("mstep", [128, NC])
        flag = sb("flag", [1, 2], I32)

        s_ldc, s_lda, s_ldw, s_ldx, s_ldq, s_ldp, s_ldm, s_ldP = (
            sem(n) for n in ("s_ldc", "s_lda", "s_ldw", "s_ldx", "s_ldq", "s_ldp", "s_ldm", "s_ldP"))
        s_gst, s_gld, s_out = sem("s_gst"), sem("s_gld"), sem("s_out")
        o_dve, o_act, o_pool = sem("o_dve"), sem("o_act"), sem("o_pool")
        s_apart = [sem(f"s_apart{i}") for i in range(4)]
        k_id, k_zero, k_all, k_pad = sem("k_id"), sem("k_zero"), sem("k_all"), sem("k_pad")
        s_sil, s_sTp, s_sT, s_adaP, s_mod, s_gsb, s_wTp, s_wTd1, s_wTd2, s_vP, s_v = (
            sem(n) for n in ("s_sil", "s_sTp", "s_sT", "s_adaP", "s_mod", "s_gsb", "s_wTp", "s_wTd1", "s_wTd2", "s_vP", "s_v"))
        s_LP, s_L, s_LTp, s_B, s_rsq, s_frp, s_anyp, s_flag = (
            sem(n) for n in ("s_LP", "s_L", "s_LTp", "s_B", "s_rsq", "s_frp", "s_anyp", "s_flag"))
        s_Bs, s_nCp, s_C, s_DFp0, s_DFp, s_DF, s_hp, s_h, s_XY, s_over, s_sqp, s_sqX, s_sqY, s_xsp, s_xs, s_xd, s_R = (
            sem(n) for n in ("s_Bs", "s_nCp", "s_C", "s_DFp0", "s_DFp", "s_DF", "s_hp", "s_h", "s_XY", "s_over", "s_sqp",
                             "s_sqX", "s_sqY", "s_xsp", "s_xs", "s_xd", "s_R"))
        s_Gp, s_Z, s_var1, s_rstd1, s_var2, s_rstd2 = (
            sem(n) for n in ("s_Gp", "s_Z", "s_var1", "s_rstd1", "s_var2", "s_rstd2"))
        (s_xn, s_xnT, s_hT, s_qkv, s_qk32, s_V, s_hi, s_rest, s_mid, s_lo, s_QKp, s_QKT, s_S, s_max, s_nm,
         s_nmT, s_NMT, s_ST, s_E, s_pv, s_on, s_proj, s_x1, s_st1) = (
            sem(n) for n in ("s_xn", "s_xnT", "s_hT", "s_qkv", "s_qk32", "s_V", "s_hi", "s_rest", "s_mid", "s_lo",
                             "s_QKp", "s_QKT", "s_S", "s_max", "s_nm", "s_nmT", "s_NMT", "s_ST", "s_E", "s_pv",
                             "s_on", "s_proj", "s_x1", "s_st1"))
        s_sel, s_Grow, s_Gstep, s_root, s_Brow, s_Bstep, s_O, s_sums, s_rsum, s_div, s_pr = (
            sem(n) for n in ("s_sel", "s_Grow", "s_Gstep", "s_root", "s_Brow", "s_Bstep", "s_O", "s_sums", "s_rsum", "s_div", "s_pr"))
        s_diag, s_dred, s_usc, s_ETp, s_ET, s_UTp, s_UT, s_Up, s_U, s_Mp, s_M = (
            sem(n) for n in ("s_diag", "s_dred", "s_usc", "s_ETp", "s_ET", "s_UTp", "s_UT", "s_Up", "s_U", "s_Mp", "s_M"))
        (m_xn, m_xnT, m_hT, m_fc1, m_gT, m_fc2, m_x2, m_x2T, m_xT, m_z, m_zT, m_rot, m_out) = (
            sem(n) for n in ("m_xn", "m_xnT", "m_hT", "m_fc1", "m_gT", "m_fc2", "m_x2", "m_x2T", "m_xT", "m_z",
                             "m_zT", "m_rot", "m_out"))

        def slot(h):
            g, p = h // 2, h % 2
            return g, p, 2 * (g // 4) + p, g % 4

        def head(q, i):
            return 2 * (4 * (q // 2) + i) + q % 2

        def within(b, first, last):
            return not isinstance(b, int) or first <= b <= last

        def prepares(b):
            return within(b, -1, B - 2)

        def scoring(b):
            return within(b, 0, B - 1)

        def weighing(b):
            return within(b, 1, B)

        def closing(b):
            return within(b, 2, B + 1)

        def parts_of(stack, first, n, step):
            slots = stack[:, :, 0:NP6].rearrange("p h (s d) -> p h s d", d=D)
            return slots[:, :, first:first + (n - 1) * step + 1:step, :]

        PLACES = (((0, 3, 1), (3, 2, 2), (4, 1, 1)), ((2, 3, 1), (0, 2, 5), (1, 1, 1)))

        def heads_of(t, which):
            return t[:, which, :].rearrange("p (h a d) -> p h a d", h=H, a=1)

        block = ctx.enter_context(nc.Block())

        @block.sync
        def _(sp):
            sp.dma_start(cond_sb[:, :], cond).then_inc(s_ldc, 16)
            wv = W.rearrange("(k p) c -> p k c", p=WP)
            for n in range(4):
                sp.dma_start(wskew[:, 4 * n:4 * n + 4, :], wv[:, 4 * n:4 * n + 4, :]).then_inc(s_ldw, 16)
            sp.dma_start(wskT2[C2:K2, :], bvec.rearrange("(a n) -> a n", a=1)).then_inc(s_ldw, 16)
            xv = x.rearrange("b t c -> t b c")
            for n in range(4):
                sp.dma_start(x_all[:, 4 * n:4 * n + 4, :], xv[:, 4 * n:4 * n + 4, :]).then_inc(s_ldx, 16)
            sp.dma_start(wfc1a[:, :], W_fc1[0:C1, :]).then_inc(s_ldm, 16)
            sp.wait_ge(k_pad, 2)
            sp.dma_start(wfc1b[0:C2, :], W_fc1[C1:C, :]).then_inc(s_ldm, 16)
            sp.dma_start(wfc1b[C2:K2, :], b_fc1.rearrange("(a n) -> a n", a=1)).then_inc(s_ldm, 16)
            sp.dma_start(wfc2a[:, :, :], W_fc2[0:128 * FK, :].rearrange("(k p) n -> p k n", p=128)).then_inc(s_ldm, 16)
            sp.dma_start(wfc2b[0:FR, :], W_fc2[128 * FK:FF, :]).then_inc(s_ldm, 16)
            sp.dma_start(wfc2b[FR:FR + 1, :], b_fc2.rearrange("(a n) -> a n", a=1)).then_inc(s_ldm, 16)
            sp.wait_ge(s_gsb, 1)
            sp.dma_start(gates_dram, gates_sb[:, :]).then_inc(s_gst, 16)
            sp.wait_ge(s_gst, 16)
            gd = gates_dram.rearrange("(a b) n -> a (b n)", a=1)
            sp.dma_start(gates[:, :, :].rearrange("p b n -> p (b n)"),
                         gd.to_broadcast([128, B * 2 * C])).then_inc(s_gld, 16)

            def store(b):
                wait(sp, m_out, b + 1)
                sp.dma_start(out[bass.ds(b, 1), :, :].rearrange("a t c -> t (a c)"),
                             x_all[:, bass.ds(b, 1), :].rearrange("p a c -> p (a c)")).then_inc(s_out, 16)

            store(0)
            with sp.Fori(1, B) as b:
                store(b)
            sp.wait_ge(s_out, 16 * B)

        @block.gpsimd
        def _(pool):
            lk = Links(pool, o_pool, s_apart[0])
            link = lk.link
            made = {}

            def make(ins, done):
                made[done] = made.get(done, 0) + 1
                ins.then_inc(done, 1)
                pool.wait_ge(done, made[done])

            def diagonal(t, own=slice(0, 128)):
                size = t.shape[1]
                make(nc.gpsimd.affine_select(out=t, in_=zeros[own, 0:size], compare_op=ALU.not_equal, fill=1.0,
                                             base=0, pattern=[[-1, size]], channel_multiplier=1), k_id)

            def below_diagonal(t, own, fill):
                make(nc.gpsimd.affine_select(out=t, in_=zeros[own, 0:RD], compare_op=ALU.is_ge, fill=fill,
                                             base=0, pattern=[[1, RD]], channel_multiplier=-1), k_id)

            lo, hi = slice(0, 64), slice(64, 128)
            make(nc.gpsimd.memset(zeros[:, :], 0.0), k_zero)
            make(nc.gpsimd.memset(wqkv2[:, :], 0.0), k_pad)
            make(nc.gpsimd.memset(wfc1b[:, :], 0.0), k_pad)
            diagonal(ident[:, :])
            make(nc.gpsimd.memset(mhalf[:, :], -0.5), k_id)
            for own in (lo, hi):
                diagonal(eye2[own, :], own)
            for own in (lo, hi):
                below_diagonal(negmask[own, :], own, -1.0)
            make(nc.gpsimd.memset(sT2[:, :], 1.0), k_id)
            make(nc.gpsimd.memset(v[:, 0:1], 0.0), k_id)
            make(nc.gpsimd.memset(A0[:, :, :], 0.0), k_id)
            make(nc.gpsimd.memset(ones[:, :], 1.0), k_id)
            for own in (lo, hi):
                below_diagonal(lower[own, :], own, 1.0)
            make(nc.gpsimd.memset(halves[:, :], 0.0), k_id)
            make(nc.gpsimd.memset(halves[lo, 0:64], 1.0), k_id)
            make(nc.gpsimd.memset(halves[hi, 64:128], 1.0), k_id)
            made_id = made[k_id]
            make(nc.gpsimd.memset(wproj[:, :, :], 0.0), k_all)
            wp = W_proj.rearrange("(a i b d) n -> i a b d n", a=2, i=4, b=2)
            for i in range(4):
                for q in range(4):
                    pool.dma_start(wproj[32 * i:32 * i + D, q, :], wp[i, q // 2, q % 2, :, :]).then_inc(s_ldp, 16)
            pool.dma_start(wproj[D:D + 1, 0, :], b_proj.rearrange("(a n) -> a n", a=1)).then_inc(s_ldp, 16)
            make(nc.gpsimd.tensor_copy(identb[:, :], ident[:, :]), k_all)
            make(nc.gpsimd.memset(hT2[:, :], 1.0), k_all)
            make(nc.gpsimd.memset(qs[:, :, :], 0.0), k_all)
            make(nc.gpsimd.memset(ks[:, :, :], 0.0), k_all)
            make(nc.gpsimd.memset(NM[:, :, :], 0.0), k_all)
            for p in range(2):
                make(nc.gpsimd.memset(V[p][:, :, :], 0.0), k_all)
                make(nc.gpsimd.memset(V[p][:, :, D:D + 1], 1.0), k_all)
            make(nc.gpsimd.memset(gT[:, FK, :], 1.0), k_all)
            make(nc.gpsimd.memset(headsel[:, :, :, :], 0.0), k_all)
            for p in range(2):
                rows = headsel[:, p, :, :]
                for n in range(3):
                    make(nc.gpsimd.affine_select(out=rows, in_=rows, compare_op=ALU.not_equal, fill=1.0, base=-64 * p - n,
                                                 pattern=[[-3, 8], [0, 128]], channel_multiplier=1), k_all)
            for p in range(2):
                for n in range(2):
                    make(nc.gpsimd.memset(KT[p][n][:, :, :, :], 0.0), k_all)
            make(nc.gpsimd.memset(sumsel[:, :, :], 1.0), k_all)
            make(nc.gpsimd.memset(sumsel[:, :, 0:4], 0.0), k_all)
            for q in range(4):
                make(nc.gpsimd.memset(sumsel[:, q, q:q + 1], 1.0), k_all)
            rows = sumrow[:, :, :].rearrange("p q (i r) -> p q i r", i=4)
            make(nc.gpsimd.memset(sumrow[:, :, :], 0.0), k_all)
            make(nc.gpsimd.affine_select(out=rows, in_=rows, compare_op=ALU.not_equal, fill=1.0, base=0,
                                         pattern=[[-1, 4], [-32, 4], [0, 32]], channel_multiplier=1), k_all)

            def inverse_roots(seen, n, done):
                wait(pool, seen, n, s_apart[0])
                var = mv[:, :, 1:2].rearrange("p b a -> p (b a)")
                link(nc.gpsimd.tensor_scalar(rstd[:, :], var, EPS, None, ALU.add))
                nc.gpsimd.tensor_tensor(rstd[:, :], rstd[:, :], mhalf[:, :], ALU.pow).then_inc(done, 1)

            inverse_roots(s_var1, 1, s_rstd1)

            def rest(b, which, stack):
                wait(pool, s_hi, 2 * b + 1 + which, s_apart[0])
                wait(pool, s_lo, 2 * b, s_apart[0])
                nc.gpsimd.tensor_tensor(heads_of(res, which), heads_of(qk32, which),
                                        parts_of(stack, PLACES[which][0][0], 1, 1), ALU.subtract).then_inc(s_rest, 1)

            def low(b, which, stack):
                wait(pool, s_mid, 2 * b + 1 + which, s_apart[0])
                nc.gpsimd.tensor_tensor(parts_of(stack, *PLACES[which][2]), heads_of(res, which),
                                        parts_of(stack, PLACES[which][1][0], 1, 1), ALU.subtract).then_inc(s_lo, 1)

            def selector(k, n):
                wait(pool, s_Brow, k - 3, s_apart[0])
                nc.gpsimd.tensor_copy(sel[:, n, :], ident[:, bass.ds(k, 1)].to_broadcast([128, 128])).then_inc(s_sel, 1)

            def square_root(k):
                wait(pool, s_Gstep, k + 1, s_apart[0])
                at = bass.ds(k, 1)
                link(nc.gpsimd.tensor_tensor(root[:, at], rec[:, at], mhalf[:, 0:1], ALU.pow))
                nc.gpsimd.tensor_tensor(root2[:, at], root[:, at], root[:, at], ALU.add).then_inc(s_root, 1)

            def attention(b, parity):
                for q in range(4):
                    if q == 1 and prepares(b):
                        rest(b + 1, 0, qs)
                        rest(b + 1, 1, ks)
                    if q == 2 and prepares(b):
                        low(b + 1, 0, qs)
                        low(b + 1, 1, ks)
                    if scoring(b):
                        square_root(QB * b + q)
                        if not (isinstance(b, int) and b == B - 1 and q > 0):
                            selector(QB * b + q + 3, (q + 3) % 4)

            for k in range(3):
                selector(k, k)
            lk.paired(attention, QB, B - 3)

            pool.wait_ge(s_Bstep, RD)
            nc.gpsimd.tensor_tensor(dG[:, :], Z[:, 0:RD], eye2[:, :], ALU.mult).then_inc(s_diag, 1)
            nc.gpsimd.tensor_tensor(dB[:, :], Z[:, 2 * RD:3 * RD], eye2[:, :], ALU.mult).then_inc(s_diag, 1)
            pool.wait_ge(s_dred, 2)
            link(nc.gpsimd.tensor_tensor(usc[:, 2:3], usc[:, 0:1], mhalf[:, 0:1], ALU.pow))
            link(nc.gpsimd.tensor_scalar(usc[:, 3:4], usc[:, 1:2], 0.0, -2.0, ALU.is_ge, ALU.mult))
            nc.gpsimd.tensor_scalar(usc[:, 0:1], usc[:, 3:4], 1.0, usc[:, 2:3], ALU.add, ALU.mult).then_inc(s_usc, 1)
            inverse_roots(s_var2, 1, s_rstd2)

        @block.scalar
        def _(act):
            lk = Links(act, o_act)
            link = lk.link
            act.dma_start(wada1[:, :], W_ada[0:C1, :]).then_inc(s_lda, 16)
            act.dma_start(wada2[0:C2, :], W_ada[C1:C, :]).then_inc(s_lda, 16)
            act.dma_start(wada2[C2:K2, :], b_ada.rearrange("(a n) -> a n", a=1)).then_inc(s_lda, 16)
            for p in range(2):
                act.dma_start(p1[:, p, :], P[0:C1, :]).then_inc(s_ldP, 16)
                act.dma_start(p2[:, p, :], P[C1:C, :]).then_inc(s_ldP, 16)
            act.dma_start(wqkv1[:, :], W_qkv[0:C1, :]).then_inc(s_ldq, 16)
            act.wait_ge(k_pad, 1)
            act.dma_start(wqkv2[0:C2, :], W_qkv[C1:C, :]).then_inc(s_ldq, 16)
            act.dma_start(wqkv2[C2:K2, :], b_qkv.rearrange("(a n) -> a n", a=1)).then_inc(s_ldq, 16)
            act.wait_ge(s_ldc, 16)
            nc.scalar.activation(sexp[:, :], cond_sb[:, :], ACT.Exp, scale=-1.0).then_inc(s_sil, 1)
            for n in range(4):
                wait(act, s_wTp, n + 1)
                nc.scalar.activation(wskT1[:, 504 * n:504 * n + 504], bank[2 * (n % 2)][:, 0:504], ACT.Copy).then_inc(s_wTd1, 1)
            for n in range(4):
                wait(act, s_vP, n + 1)
                nc.scalar.activation(v[:, 1 + 504 * n:505 + 504 * n], bank[n][0:B, 0:504], ACT.Copy).then_inc(s_v, 1)
            for n in range(SQ):
                wait(act, s_sqp, 2 * n + 2)
                nc.scalar.activation(Ym[:, :, :].rearrange("p c n -> p (c n)"), bank[5][:, :], ACT.Copy).then_inc(s_sqY, 1)

            def modulated(b, tp, done, free, freed, row, src):
                wait(act, tp, b + 1)
                wait(act, free, freed)
                for t, m, n in ((hT1[:, :], mod1, C1), (hT2[0:C2, :], mod2, C2)):
                    nc.scalar.activation(t, src[0:n, (0 if n == C1 else 128):(128 if n == C1 else 256)], ACT.Identity,
                                         bias=m[:, row, bass.ds(b, 1)], scale=m[:, row + 1, bass.ds(b, 1)]).then_inc(done, 1)

            def attention(b, parity):
                if weighing(b):
                    act.wait_ge(s_nmT, b)
                    wait(act, s_ST, 4 * b - 4)
                    nc.scalar.activation(NMT[:, :], bank[0][:, 256:320].bitcast(BF16), ACT.Copy).then_inc(s_NMT, 1)
                if prepares(b):
                    modulated(b + 1, s_xnT, s_hT, s_qkv, b + 1, 0, bank[0])
                if scoring(b):
                    stacks_transposed(b, parity, 1)
                if closing(b):
                    act.wait_ge(s_pv, 4 * b - 4)
                    nc.scalar.activation(Osb[:, :], bank[5][:, :], ACT.Copy).then_inc(s_O, 1)
                if scoring(b):
                    act.wait_ge(s_qkv, b + 1)
                    wait(act, s_pv, 4 * b - 4)
                    nc.scalar.activation(V[parity][:, :, 0:D], bank[1][:, 2 * C:3 * C].rearrange("p (h d) -> p h d", h=H),
                                         ACT.Copy).then_inc(s_V, 1)
                if weighing(b):
                    exponentials(b - 1, 0)
                if prepares(b):
                    wait(act, s_qkv, b + 2)
                    wait(act, s_rest, 2 * b + 2)
                    nc.scalar.activation(qk32[:, 0, :], bank[1][:, 0:C], ACT.Copy, scale=SCALE).then_inc(s_qk32, 1)
                    nc.scalar.activation(qk32[:, 1, :], bank[1][:, C:2 * C], ACT.Copy).then_inc(s_qk32, 1)
                if weighing(b):
                    exponentials(b - 1, 1)
                if prepares(b):
                    wait(act, s_QKp, 2 * b + 2)
                    wait(act, s_qk32, 2 * b + 4)
                    for which, stack in enumerate((qs, ks)):
                        place = PLACES[which][0]
                        nc.scalar.activation(parts_of(stack, *place), heads_of(qk32, which).to_broadcast([128, H, place[1], D]),
                                             ACT.Copy).then_inc(s_hi, 1)
                    for which, stack in enumerate((qs, ks)):
                        place = PLACES[which][1]
                        wait(act, s_rest, 2 * b + 3 + which)
                        nc.scalar.activation(parts_of(stack, *place), heads_of(res, which).to_broadcast([128, H, place[1], D]),
                                             ACT.Copy).then_inc(s_mid, 1)
                if weighing(b):
                    exponentials(b - 1, 2)
                if prepares(b):
                    stacks_transposed(b + 1, 1 - parity, 0)
                if weighing(b):
                    exponentials(b - 1, 3)

            def exponentials(b, q):
                act.wait_ge(s_ST, 4 * b + q + 1)
                wait(act, s_sums, b)
                nc.scalar.activation(E[:, q, :, :].rearrange("p i t -> p (i t)"), bank[4][:, :],
                                     ACT.Exp).then_inc(s_E, 1)

            def stacks_transposed(b, parity, n):
                wait(act, s_QKp, 2 * b + n + 1)
                wait(act, s_ST, 4 * b - 6 + 2 * n)
                nc.scalar.activation(QT[parity][n][:, :, :].rearrange("p g t -> p (g t)"),
                                     bank[2][:, 0:256].bitcast(BF16), ACT.Copy).then_inc(s_QKT, 1)
                for p in range(2):
                    own = slice(64 * p, 64 * p + 64)
                    nc.scalar.activation(KT[parity][n][own, p, :, :].rearrange("p g t -> p (g t)"),
                                         bank[2][own, 256:512].bitcast(BF16), ACT.Copy).then_inc(s_QKT, 1)

            act.wait_ge(s_mod, 4)
            act.wait_ge(k_all, N_ALL)
            lk.paired(attention, 0, B - 3)

            def gelu(b):
                wait(act, m_fc1, b + 1)
                wait(act, m_fc2, b)
                nc.scalar.activation(gT[:, 0:FK, :].rearrange("p k t -> p (k t)"), bank[1][:, :],
                                     ACT.Gelu_apprx_tanh).then_inc(m_gT, 1)
                nc.scalar.activation(gT[0:FR, FK, :], bank[2][0:FR, 0:128], ACT.Gelu_apprx_tanh).then_inc(m_gT, 1)

            def mlp(b):
                more = not (isinstance(b, int) and b == B - 1)
                if more:
                    modulated(b + 1, m_xnT, m_hT, m_fc1, b + 1, 2, bank[0])
                    gelu(b + 1)

            act.wait_ge(k_all, N_ALL)
            modulated(0, m_xnT, m_hT, m_fc1, 0, 2, bank[0])
            gelu(0)
            lk.rolled(mlp, 0, B - 2)

        @block.vector
        def _(dve):
            lk = Links(dve, o_dve)
            link = lk.link
            TT, TS, STT = nc.vector.tensor_tensor, nc.vector.tensor_scalar, nc.vector.scalar_tensor_tensor

            def flat(t):
                return t[:, :, :].rearrange("p c n -> p (c n)")

            dve.wait_ge(k_id, N_ID)
            dve.wait_ge(s_Gp, 1)
            nc.vector.tensor_copy(Z[:, 0:RD], bank[7][:, 0:RD]).then_inc(s_Z, 1)
            nc.vector.tensor_copy(Z[:, 2 * RD:3 * RD], bank[7][:, RD:2 * RD]).then_inc(s_Z, 1)
            nc.vector.tensor_copy(Z[:, RD:2 * RD], eye2[:, :]).then_inc(s_Z, 1)
            nc.vector.tensor_copy(PT[:, :], bank[7][0:RD, 2 * RD:2 * RD + C]).then_inc(s_Z, 1)
            dve.wait_ge(s_sil, 1)
            link(TS(sexp[:, :], sexp[:, :], 1.0, None, ALU.add))
            link(nc.vector.reciprocal(sexp[:, :], sexp[:, :]))
            TT(sil[:, :], cond_sb[:, :], sexp[:, :], ALU.mult).then_inc(s_sil, 1)
            dve.wait_ge(s_sTp, 1)
            dve.wait_ge(k_id, N_ID)
            nc.vector.tensor_copy(sT1[:, :], bank[6][0:C1, 0:B]).then_inc(s_sT, 1)
            nc.vector.tensor_copy(sT2[0:C2, :], bank[6][0:C2, B:2 * B]).then_inc(s_sT, 1)
            for n in range(4):
                wait(dve, s_wTp, n + 1)
                nc.vector.tensor_copy(wskT2[0:C2, 504 * n:504 * n + 504],
                                      bank[1 + 2 * (n % 2)][0:C2, 0:504]).then_inc(s_wTd2, 1)
            dve.wait_ge(s_adaP, 1)
            for m, n, o in ((mod1, C1, 0), (mod2, C2, 64)):
                ps = bank[6][0:n, o:o + 4 * B].rearrange("p (k a b) -> p k a b", k=2, a=2)
                mm = m[:, :, :].rearrange("p (k a) b -> p k a b", k=2)
                nc.vector.tensor_copy(mm[:, :, 0, :], ps[:, :, 0, :]).then_inc(s_mod, 1)
                TS(mm[:, :, 1, :], ps[:, :, 1, :], 1.0, None, ALU.add).then_inc(s_mod, 1)
            nc.vector.tensor_copy(gates_sb[:, :], bank[6][0:B, 128:128 + 2 * C]).then_inc(s_gsb, 1)
            dve.wait_ge(s_ldx, 64)
            for b in range(B):
                ins = nc.vector.bn_stats(stats[:, b, :], x_all[:, b, :])
            link(ins)
            for b in range(B):
                ins = nc.vector.bn_aggr(mv[:, b, :], stats[:, b, :])
            ins.then_inc(s_var1, 1)
            dve.wait_ge(k_id, N_ID)
            dve.wait_ge(s_LP, 1)
            TT(A0[:, :, 0:RD - 1].rearrange("p c i -> p i c"),
               bank[4][:, 0:(RD - 1) * NC].rearrange("p (i c) -> p i c", c=NC),
               lower[:, 0:RD - 1].rearrange("p (i a) -> p i a", a=1).to_broadcast([128, RD - 1, NC]),
               ALU.mult).then_inc(s_L, 1)
            dve.wait_ge(s_LTp, 1)
            dve.wait_ge(s_L, 1)
            link(TT(flat(Bm), flat(A0), bank[0][:, :], ALU.subtract))
            link(TT(flat(A0), flat(Bm), flat(Bm), ALU.mult))
            nc.vector.tensor_reduce(rowsq[:, :], A0[:, :, :], AX.X, ALU.add).then_inc(s_rsq, 1)
            dve.wait_ge(s_frp, 1)
            link(nc.vector.tensor_copy(fro[:, :], bank[1][:, 0:NC]))
            for i in range(XSQ):
                ins = TS(over[:, :, i], fro[:, :], 2 * (THETA * 2 ** (SQ + i)) ** 2, 0.5 ** (i + 1), ALU.is_gt, ALU.mult)
            link(ins)
            link(nc.vector.tensor_reduce(nsc[:, :], over[:, :, :], AX.X, ALU.add))
            link(TS(nsc[:, :], nsc[:, :], -(0.5 ** SQ), 0.5 ** SQ, ALU.mult, ALU.add))
            TT(Bm[:, :, :], Bm[:, :, :], nsc[:, :].rearrange("p (c a) -> p c a", a=1).to_broadcast([128, NC, RD]),
               ALU.mult).then_inc(s_Bs, 1)
            dve.wait_ge(s_Bs, 1)
            eye_c = eye2[:, :].rearrange("p (a n) -> p a n", a=1).to_broadcast([128, NC, RD])

            def ev(i):
                return eo[i][:, :, 0, :]

            def od(i):
                return eo[i][:, :, 1, :]

            dve.wait_ge(s_nCp, 1)
            nc.vector.tensor_copy(flat(Cm), bank[0][:, :]).then_inc(s_C, 1)
            dve.wait_ge(s_C, 1)
            for i in range(3):
                if i < 2:
                    ins = TS(ev(i), eye_c, 1.0 / factorial(4 * i), None, ALU.mult)
                else:
                    ins = TS(ev(i), eye_c, 1.0 / factorial(8), None, ALU.mult)
            link(ins)
            for i in range(3):
                ins = STT(ev(i), Cm[:, :, :], -1.0 / factorial(4 * i + 2), ev(i), ALU.mult, ALU.add)
            link(ins)
            dve.wait_ge(s_DFp, 1)
            link(nc.vector.tensor_copy(flat(Dm), bank[1][:, :]))
            nc.vector.tensor_copy(flat(Fm), bank[2][:, :]).then_inc(s_DF, 1)
            for i in range(3):
                ins = TS(od(i), Bm[:, :, :], 1.0 / factorial(4 * i + 1), None, ALU.mult)
            link(ins)
            for i in range(3):
                ins = STT(od(i), Dm[:, :, :], -1.0 / factorial(4 * i + 3), od(i), ALU.mult, ALU.add)
            dve.wait_ge(s_DF, 1)
            link(ins)
            STT(ev(2), Fm[:, :, :], 1.0 / factorial(12), ev(2), ALU.mult, ALU.add).then_inc(s_DF, 1)

            def halfbank(n):
                return bank[4 + n][:, :].rearrange("p (c e n) -> p c e n", c=NC // 2, e=2)

            for step, (dst, add) in enumerate(((T1, eo[1]), (eo[0], eo[0]))):
                for n in range(2):
                    cs = slice(n * NC // 2, (n + 1) * NC // 2)
                    wait(dve, s_hp, 2 * step + n + 1)
                    TT(dst[:, cs, :, :], halfbank(n), add[:, cs, :, :], ALU.add).then_inc(s_h, 1)
            dve.wait_ge(s_h, 4)
            TT(Xm[:, :, :], ev(0), od(0), ALU.add).then_inc(s_XY, 1)
            TT(Ym[:, :, :], ev(0), od(0), ALU.subtract).then_inc(s_XY, 1)
            for n in range(SQ):
                wait(dve, s_sqp, 2 * n + 2)
                nc.vector.tensor_copy(flat(Xm), bank[4][:, :]).then_inc(s_sqX, 1)
            dve.wait_ge(s_anyp, 1)
            link(nc.vector.tensor_reduce(nsc[0:32, 0:1], bank[1][0:32, NC:2 * NC], AX.X, ALU.add))
            nc.vector.tensor_copy(flag[0:1, 0:1], nsc[0:1, 0:1]).then_inc(s_flag, 1)
            dve.wait_ge(s_flag, 1)
            dve.wait_ge(s_sqY, SQ)
            dve.wait_ge(s_sqX, SQ)
            more_squarings = dve.value_load(flag[0:1, 0:1])
            with dve.If(more_squarings > 0):
                with dve.Fori(0, XSQ) as i:
                    wait(dve, s_xsp, i + 1)
                    take, keep = mstep[:, :], nsc[:, :]
                    o = over[:, :, bass.ds(i, 1)].rearrange("p c a -> p (c a)")
                    TS(take, o, 0.0, None, ALU.is_gt).then_inc(s_xd, 1)
                    TS(keep, o, 0.0, None, ALU.is_equal).then_inc(s_xd, 1)
                    wait(dve, s_xd, 8 * i + 2)
                    tb, kb = (t.rearrange("p (c a) -> p c a", a=1).to_broadcast([128, NC, RD]) for t in (take, keep))
                    for M, bk, T in ((Xm, 4, A0), (Ym, 5, Dm)):
                        TT(T[:, :, :], bank[bk][:, :].rearrange("p (c n) -> p c n", c=NC), tb, ALU.mult).then_inc(s_xd, 1)
                        TT(M[:, :, :], M[:, :, :], kb, ALU.mult).then_inc(s_xd, 1)
                    wait(dve, s_xd, 8 * i + 6)
                    TT(flat(Xm), flat(Xm), flat(A0), ALU.add).then_inc(s_xd, 1)
                    TT(flat(Ym), flat(Ym), flat(Dm), ALU.add).then_inc(s_xd, 1)
                    wait(dve, s_xd, 8 * i + 8)
                    dve.sem_inc(s_xs, 1)
            TT(Xm[:, :, :], Xm[:, :, :], eye_c, ALU.subtract).then_inc(s_R, 1)

            def normalized(b, free, done):
                wait(dve, free, b)
                TS(xn[:, :], x_all[:, bass.ds(b, 1), :].rearrange("p a c -> p (a c)"),
                   mv[:, bass.ds(b, 1), 0:1].rearrange("p a c -> p (a c)"), rstd[:, bass.ds(b, 1)],
                   ALU.subtract, ALU.mult).then_inc(done, 1)

            def eliminations(k, G, B):
                if B:
                    j, jp = bass.ds(k - 1, 1), bass.ds(k - 1 + 2 * RD, 1)
                    bkk = bank[7][:, jp]
                    dve.wait_ge(s_Brow, k)
                if G:
                    kk = bass.ds(k, 1)
                    dve.wait_ge(s_Grow, k + 1)
                    got_rec = lk.mark(nc.vector.reciprocal(rec[:, kk], bank[7][:, kk]))
                if B:
                    got_c = lk.mark(STT(c[:, :], bkk, cG[:, j], Z[:, jp], ALU.mult, ALU.add))
                    wait(dve, s_root, k)
                    got_sign = lk.mark(TS(cB[:, :], bkk, 0.0, root2[:, j], ALU.is_ge, ALU.mult))
                if G:
                    lk.need(got_rec)
                    got_cG = lk.mark(TS(cG[:, kk], Z[:, kk], rec[:, kk], negmask[:, kk], ALU.mult, ALU.mult))
                if B:
                    lk.need(got_sign)
                    got_pivot = lk.mark(STT(w[:, :], cB[:, :], root[:, j], bkk, ALU.subtract, ALU.add))
                if G:
                    lk.need(got_cG)
                    STT(Z[:, 0:2 * RD], bank[7][:, 0:2 * RD], cG[:, kk], Z[:, 0:2 * RD],
                        ALU.mult, ALU.add).then_inc(s_Gstep, 1)
                if B:
                    lk.need(got_pivot)
                    link(nc.vector.reciprocal(w[:, :], w[:, :]))
                    link(STT(cB[:, :], c[:, :], w[:, :], negmask[:, j], ALU.mult, ALU.mult))
                    link(TT(cB[:, :], cB[:, :], cG[:, j], ALU.add))
                    STT(Z[:, 2 * RD:3 * RD], bank[7][:, 2 * RD:3 * RD], cB[:, :], Z[:, 2 * RD:3 * RD],
                        ALU.mult, ALU.add).then_inc(s_Bstep, 1)

            def residual(b):
                dve.wait_ge(s_proj, b + 1)
                TT(tmp[:, :], bank[6][:, 0:C],
                   gates[:, bass.ds(b, 1), 0:C].rearrange("p a c -> p (a c)"), ALU.mult).then_inc(s_pr, 1)
                wait(dve, s_pr, b + 1)
                xb = x_all[:, bass.ds(b, 1), :].rearrange("p a c -> p (a c)")
                TT(xb, xb, tmp[:, :], ALU.add).then_inc(s_x1, 1)
                wait(dve, s_x1, b + 1)
                nc.vector.bn_stats(stats[:, bass.ds(b, 1), :].rearrange("p a c -> p (a c)"), xb).then_inc(s_st1, 1)

            def reciprocal_sums(b):
                dve.wait_ge(s_sums, b + 1)
                nc.vector.reciprocal(rsum[:, :], bank[7][:, 3 * RD:3 * RD + 128]).then_inc(s_rsum, 1)

            def divided(b):
                dve.wait_ge(s_O, b + 1)
                dve.wait_ge(s_div, b + 1)
                TT(ON[:, :, :].rearrange("p q t -> p (q t)"), Osb[:, :], bank[6][:, :], ALU.mult).then_inc(s_on, 1)

            def attention(b, parity):
                for q in range(4):
                    if scoring(b):
                        dve.wait_ge(s_S, 4 * b + q + 1)
                        nc.vector.tensor_reduce(nmax[:, q % 2, 4 * (q // 2):4 * (q // 2) + 4],
                                                bank[3][:, :].rearrange("p (i m) -> p i m", i=4),
                                                AX.X, ALU.max, negate=True).then_inc(s_max, 1)
                    if q == 3 and scoring(b):
                        maxima_parts(b)
                    if scoring(b) or q == 0 and within(b, 0, B):
                        eliminations(QB * b + q, scoring(b), not (isinstance(b, int) and QB * b + q == 0))
                    if q == 0 and closing(b):
                        reciprocal_sums(b - 2)
                    if q == 1 and closing(b):
                        divided(b - 2)
                    if q == 2 and within(b, -1, B - 3):
                        normalized(b + 2, s_xnT, s_xn)
                    if q == 2 and closing(b):
                        residual(b - 2)

            def maxima_parts(b):
                dve.wait_ge(s_max, 4 * b + 4)
                wait(dve, s_nmT, b)
                parts = NM[:, :, 0:24].rearrange("p s (g r) -> p s g r", r=3)
                link(nc.vector.tensor_copy(parts[:, :, :, 0], nmax[:, :, :]))
                link(TT(nmr[:, :, :], nmax[:, :, :], parts[:, :, :, 0], ALU.subtract))
                link(nc.vector.tensor_copy(parts[:, :, :, 1], nmr[:, :, :]))
                TT(parts[:, :, :, 2], nmr[:, :, :], parts[:, :, :, 1], ALU.subtract).then_inc(s_nm, 1)

            dve.wait_ge(s_rstd1, 1)
            dve.wait_ge(k_all, N_ALL)
            normalized(0, s_xnT, s_xn)
            dve.wait_ge(s_gld, 16)
            lk.paired(attention, 3 + 8 * 4, B - 3)

            dve.wait_ge(s_st1, B)
            for b in range(B):
                ins = nc.vector.bn_aggr(mv[:, b, :], stats[:, b, :])
            ins.then_inc(s_var2, 1)
            dve.wait_ge(s_diag, 2)
            nc.vector.tensor_reduce(usc[:, 0:1], dG[:, :], AX.X, ALU.add).then_inc(s_dred, 1)
            nc.vector.tensor_reduce(usc[:, 1:2], dB[:, :], AX.X, ALU.add).then_inc(s_dred, 1)
            dve.wait_ge(s_ETp, 1)
            for p in range(2):
                nc.vector.tensor_copy(ET[:, p, :], bank[0][0:RD, 0:RD]).then_inc(s_ET, 1)
            dve.wait_ge(s_UTp, 1)
            dve.wait_ge(s_usc, 1)
            TS(UT[:, :], bank[1][:, 0:C], usc[:, 0:1], None, ALU.mult).then_inc(s_UT, 1)
            dve.wait_ge(s_rstd2, 1)
            normalized(0, m_xnT, m_xn)
            dve.wait_ge(s_Up, 1)
            nc.vector.tensor_copy(U1[:, :], bank[1][:, 0:RD]).then_inc(s_U, 1)
            nc.vector.tensor_copy(U2[:, :], bank[1][0:C2, RD:2 * RD]).then_inc(s_U, 1)
            for p in range(2):
                dve.wait_ge(s_Mp, p + 1)
                for n in range(3):
                    cnt = 3 if n < 2 else 2
                    dst = M_all[:, :, :].rearrange("d (c b) n -> d c b n", b=2)[:, 3 * n:3 * n + cnt, p, :]
                    nc.vector.tensor_copy(dst, bank[2 + 3 * p + n][0:RD, 0:cnt * C].rearrange(
                        "d (c n) -> d c n", c=cnt)).then_inc(s_M, 1)

            def mlp(b):
                more = not (isinstance(b, int) and b == B - 1)
                if more:
                    normalized(b + 1, m_xnT, m_xn)
                xb = x_all[:, bass.ds(b, 1), :].rearrange("p a c -> p (a c)")
                wait(dve, m_fc2, b + 1)
                link(TT(tmp[:, :], bank[3][:, 0:C],
                        gates[:, bass.ds(b, 1), C:2 * C].rearrange("p a c -> p (a c)"), ALU.mult))
                TT(x2[:, :], tmp[:, :], xb, ALU.add).then_inc(m_x2, 1)
                wait(dve, m_x2T, b + 1)
                nc.vector.tensor_copy(xT1[:, :], bank[4][:, 0:128]).then_inc(m_xT, 1)
                nc.vector.tensor_copy(xT2[:, :], bank[4][0:C2, 128:256]).then_inc(m_xT, 1)
                wait(dve, m_z, b + 1)
                nc.vector.tensor_copy(zT[:, :], bank[5][0:RD, 0:128]).then_inc(m_zT, 1)
                wait(dve, m_rot, b + 1)
                wait(dve, m_x2, b + 1)
                TT(xb, x2[:, :], bank[6][:, 0:C], ALU.add).then_inc(m_out, 1)

            lk.rolled(mlp, 0, B - 2)
            mlp(B - 1)

        @block.tensor
        def _(pe):
            mm = nc.tensor.matmul
            pe.wait_ge(s_ldP, 64)
            pe.wait_ge(k_id, N_ID)

            def twice(t):
                return t.rearrange("p a n -> p (a n)")

            mm(bank[7][:, 0:RD], twice(p1[:, :, :]), p1[:, 0, :], start=True, stop=False)
            mm(bank[7][:, 0:RD], twice(p2[:, :, :]), p2[:, 0, :], start=False, stop=True)
            mm(bank[7][:, RD:2 * RD], twice(p1[0:RD, :, :]), ident[0:RD, 0:RD], start=True, stop=True)
            mm(bank[7][0:RD, 2 * RD:2 * RD + C1], p1[:, 0, :], ident[:, :], start=True, stop=True)
            mm(bank[7][0:RD, 2 * RD + C1:2 * RD + C], p2[:, 0, :], ident[0:C2, 0:C2], start=True, stop=True).then_inc(s_Gp, 1)
            pe.wait_ge(s_sil, 2)
            pe.transpose(bank[6][0:C1, 0:B], sil[:, 0:C1], ident[0:B, 0:B])
            pe.transpose(bank[6][0:C2, B:2 * B], sil[:, C1:C], ident[0:B, 0:B]).then_inc(s_sTp, 1)
            for n in range(4):
                pe.wait_ge(s_ldw, 80)
                wait(pe, s_wTd1, n - 1)
                wait(pe, s_wTd2, n - 1)
                for j in range(4):
                    pe.transpose(bank[2 * (n % 2)][:, WP * j:WP * j + WP], wskew[:, 4 * n + j, 0:C1], ident[0:WP, 0:WP])
                    ins = pe.transpose(bank[1 + 2 * (n % 2)][0:C2, WP * j:WP * j + WP], wskew[:, 4 * n + j, C1:C],
                                       ident[0:WP, 0:WP])
                ins.then_inc(s_wTp, 1)
            pe.wait_ge(s_sT, 2)
            pe.wait_ge(s_lda, 48)
            for kind, col in enumerate((0, 1, 3, 4)):
                for o, c0, n in ((0, 0, C1), (64, C1, C2)):
                    cols = slice(col * C + c0, col * C + c0 + n)
                    dst = bank[6][0:n, o + B * kind:o + B * kind + B]
                    mm(dst, wada1[:, cols], sT1[:, :], start=True, stop=False)
                    mm(dst, wada2[:, cols], sT2[:, :], start=False, stop=True)
            for n, col in enumerate((2, 5)):
                dst = bank[6][0:B, 128 + C * n:128 + C * n + C]
                mm(dst, sT1[:, :], wada1[:, col * C:col * C + C], start=True, stop=False)
                ins = mm(dst, sT2[:, :], wada2[:, col * C:col * C + C], start=False, stop=True)
            ins.then_inc(s_adaP, 1)
            pe.wait_ge(s_wTd1, 4)
            pe.wait_ge(s_wTd2, 4)
            for n in range(4):
                mm(bank[n][0:B, 0:504], sT1[:, :], wskT1[:, 504 * n:504 * n + 504], start=True, stop=False)
                mm(bank[n][0:B, 0:504], sT2[:, :], wskT2[:, 504 * n:504 * n + 504], start=False, stop=True).then_inc(s_vP, 1)
            pe.wait_ge(s_v, 4)
            for i in range(RD - 1):
                at = (RD - 1) * i - i * (i - 1) // 2 - i
                for p in range(2):
                    ins = mm(bank[4][64 * p:64 * p + RD, NC * i:NC * i + NC], v[:, at:at + RD],
                             ident[0:B, p:B:2], start=True, stop=True)
            ins.then_inc(s_LP, 1)

            def both(c):
                for p in range(2):
                    yield slice(64 * p, 64 * p + 64), slice(RD * c, RD * c + RD)

            def product(bk, lhs, rhs, done):
                for c in range(NC):
                    for own, cols in both(c):
                        ins = mm(bank[bk][own, cols], lhs[own, c, :], rhs[own, c, :], start=True, stop=True)
                ins.then_inc(done, 1)

            pe.wait_ge(s_L, 1)
            for c in range(NC):
                for own, cols in both(c):
                    ins = mm(bank[0][own, cols], A0[own, c, :], eye2[own, :], start=True, stop=True)
            ins.then_inc(s_LTp, 1)
            pe.wait_ge(s_rsq, 1)
            mm(bank[1][:, 0:NC], halves[:, :], rowsq[:, :], start=True, stop=True).then_inc(s_frp, 1)
            pe.wait_ge(s_Bs, 1)
            product(0, Bm, Bm, s_nCp)
            pe.wait_ge(s_C, 1)
            product(1, Cm, Bm, s_DFp0)
            product(2, Cm, Cm, s_DFp)
            pe.wait_ge(s_DF, 2)
            for step, src in enumerate((eo[2], T1)):
                for n in range(2):
                    if step:
                        pe.wait_ge(s_h, 2)
                    for c in range(NC // 2):
                        for p in range(2):
                            own = slice(64 * p, 64 * p + 64)
                            cc = n * NC // 2 + c
                            ins = mm(bank[4 + n][own, 128 * c:128 * c + 128], Fm[own, cc, :],
                                     src[own, cc, :, :].rearrange("p e n -> p (e n)"), start=True, stop=True)
                    ins.then_inc(s_hp, 1)
            pe.wait_ge(s_XY, 2)
            for n in range(SQ):
                wait(pe, s_sqX, n)
                wait(pe, s_sqY, n)
                product(4, Ym, Xm, s_sqp)
                product(5, Xm, Ym, s_sqp)
            mm(bank[1][0:32, NC:2 * NC], ones[:, :], over[:, :, 0], start=True, stop=True).then_inc(s_anyp, 1)
            pe.wait_ge(s_flag, 1)
            more_squarings = pe.value_load(flag[0:1, 0:1])
            with pe.If(more_squarings > 0):
                pe.wait_ge(s_sqX, SQ)
                pe.wait_ge(s_sqY, SQ)
                pe.sem_inc(s_xs, 1)
                with pe.Fori(0, XSQ) as i:
                    wait(pe, s_xs, i + 1, s_apart[1])
                    for c in range(NC):
                        for own, cols in both(c):
                            mm(bank[4][own, cols], Ym[own, c, :], Xm[own, c, :], start=True, stop=True)
                            ins = mm(bank[5][own, cols], Xm[own, c, :], Ym[own, c, :], start=True, stop=True)
                    ins.then_inc(s_xsp, 1)

            def transposed(b, src_ready, done, free, freed):
                wait(pe, src_ready, b + 1)
                wait(pe, free, freed)
                pe.transpose(bank[0][:, 0:128], xn[:, 0:C1], ident[:, :])
                pe.transpose(bank[0][0:C2, 128:256], xn[:, C1:C], ident[:, :]).then_inc(done, 1)

            def qkv(b):
                pe.wait_ge(s_hT, 2 * b + 2)
                wait(pe, s_qk32, 2 * b)
                wait(pe, s_V, b)
                mm(bank[1][:, 0:3 * C], hT1[:, :], wqkv1[:, :], start=True, stop=False)
                mm(bank[1][:, 0:3 * C], hT2[:, :], wqkv2[:, :], start=False, stop=True).then_inc(s_qkv, 1)

            def stacks_T(b, n):
                wait(pe, s_lo, 2 * b + 2)
                wait(pe, s_QKT, 6 * b + 3 * n)
                for which, stack in enumerate((qs, ks)):
                    for g in range(4):
                        h = 2 * (4 * n + g)
                        at = 256 * which + 64 * g
                        ins = pe.transpose(bank[2][:, at:at + 64].bitcast(BF16),
                                           stack[:, h:h + 2, :].rearrange("p h s -> p (h s)"), identb[:, :])
                ins.then_inc(s_QKp, 1)

            def scores(q, b, parity):
                wait(pe, s_QKT, 6 * b + 3 + 3 * (q // 2))
                wait(pe, s_max, 4 * b + q)
                for i in range(4):
                    ins = mm(bank[3][:, 128 * i:128 * i + 128], QT[parity][q // 2][:, i, :],
                             KT[parity][q // 2][:, q % 2, i, :], start=True, stop=True)
                ins.then_inc(s_S, 1)

            def scores_T(q, b, parity):
                wait(pe, s_NMT, b + 1)
                wait(pe, s_E, 4 * b + q)
                for i in range(4):
                    dst = bank[4][:, 128 * i:128 * i + 128]
                    mm(dst, KT[parity][q // 2][:, q % 2, i, :], QT[parity][q // 2][:, i, :], start=True, stop=False)
                    ins = mm(dst, headsel[:, q % 2, 4 * (q // 2) + i, :], NMT[:, :], start=False, stop=True)
                ins.then_inc(s_ST, 1)

            def values(q, b, parity):
                wait(pe, s_E, 4 * b + q + 1)
                if q == 0:
                    wait(pe, s_O, b)
                    pe.wait_ge(s_V, b + 1)
                for i in range(4):
                    own, cols = slice(32 * i, 32 * i + 32), slice(128 * q, 128 * q + 128)
                    ins = mm(bank[5][own, cols], V[parity][:, head(q, i), :], E[:, q, i, :], start=True, stop=True)
                ins.then_inc(s_pv, 1)

            def sums(b):
                for q in range(4):
                    for i in range(4):
                        own = slice(32 * i, 32 * i + 32)
                        ins = mm(bank[7][own, 3 * RD:3 * RD + 128], sumsel[:, q, :], E[:, q, i, :],
                                 start=(q == 0), stop=(q == 3))
                ins.then_inc(s_sums, 1)

            def division(b):
                pe.wait_ge(s_rsum, b + 1)
                for q in range(4):
                    ins = mm(bank[6][:, 128 * q:128 * q + 128], sumrow[:, q, :], rsum[:, :], start=True, stop=True)
                ins.then_inc(s_div, 1)

            def G_row(k, n):
                pe.wait_ge(s_sel, k + 1)
                mm(bank[7][:, 0:2 * RD], sel[:, n, :], Z[:, 0:2 * RD], start=True, stop=True).then_inc(s_Grow, 1)

            def B_row(k, n):
                mm(bank[7][:, 2 * RD:3 * RD], sel[:, n, :], Z[:, 2 * RD:3 * RD], start=True, stop=True).then_inc(s_Brow, 1)

            def projection(b):
                pe.wait_ge(s_on, b + 1)
                for q in range(4):
                    ins = mm(bank[6][:, 0:C], ON[:, q, :], wproj[:, q, :], start=(q == 0), stop=(q == 3))
                ins.then_inc(s_proj, 1)

            def attention(b, parity):
                for q in range(4):
                    if scoring(b):
                        scores(q, b, parity)
                    if q == 0:
                        if prepares(b):
                            transposed(b + 1, s_xn, s_xnT, s_hT, 2 * b + 2)
                        if weighing(b):
                            pe.wait_ge(s_nm, b)
                            wait(pe, s_NMT, b - 1)
                            pe.transpose(bank[0][:, 256:320].bitcast(BF16), NM[:, :, :].rearrange("p s n -> p (s n)"),
                                         identb[:, :]).then_inc(s_nmT, 1)
                        if scoring(b):
                            stacks_T(b, 1)
                    if q == 1 and prepares(b):
                        qkv(b + 1)
                    if q == 2 and closing(b):
                        projection(b - 2)
                    if q == 3 and prepares(b):
                        stacks_T(b + 1, 0)
                    if q == 0 and closing(b):
                        values(3, b - 2, parity)
                    if q and weighing(b):
                        values(q - 1, b - 1, 1 - parity)
                    k = QB * b + q
                    if isinstance(b, int):
                        wait(pe, s_Gstep, min(k, RD))
                        wait(pe, s_Bstep, min(k - 1, RD))
                    else:
                        wait(pe, s_Gstep, k)
                        wait(pe, s_Bstep, k - 1)
                    if q == 0 and closing(b):
                        sums(b - 2)
                    if q == 1 and closing(b):
                        pe.wait_ge(s_rsum, b - 1)
                    if scoring(b):
                        G_row(k, q)
                    if (scoring(b) or q == 0 and within(b, 0, B)) and not (isinstance(b, int) and k == 0):
                        B_row(k - 1, (q + 3) % 4)
                    if q == 1 and closing(b):
                        division(b - 2)
                    if weighing(b):
                        scores_T(q, b - 1, 1 - parity)

            pe.wait_ge(s_ldq, 48)
            pe.wait_ge(k_all, N_ALL)
            pe.wait_ge(s_R, 1)
            pe.wait_ge(s_Z, 4)
            pe.wait_ge(s_ldp, 16 * 17)
            paired(pe, attention, B - 3)

            pe.wait_ge(s_Bstep, RD)
            pe.wait_ge(s_NMT, B)
            pe.transpose(bank[0][0:RD, 0:RD], Z[0:RD, RD:2 * RD], ident[0:RD, 0:RD]).then_inc(s_ETp, 1)
            pe.wait_ge(s_ET, 2)
            pe.wait_ge(s_V, B)
            mm(bank[1][:, 0:C], twice(ET[:, :, :]), PT[:, :], start=True, stop=True).then_inc(s_UTp, 1)
            pe.wait_ge(s_UT, 1)
            pe.transpose(bank[1][:, 0:RD], UT[0:RD, 0:C1], ident[0:RD, 0:RD])
            pe.transpose(bank[1][0:C2, RD:2 * RD], UT[0:RD, C1:C], ident[0:RD, 0:RD]).then_inc(s_Up, 1)
            pe.wait_ge(s_E, 4 * B)
            pe.wait_ge(s_O, B)
            pe.wait_ge(s_pr, B)
            for p in range(2):
                own = slice(64 * p, 64 * p + 64)
                for c in range(NC):
                    ins = mm(bank[2 + 3 * p + c // 3][0:RD, C * (c % 3):C * (c % 3) + C], Xm[own, c, :], UT[own, :],
                             start=True, stop=True)
                ins.then_inc(s_Mp, 1)

            def fc1(b):
                wait(pe, m_hT, 2 * b + 2)
                wait(pe, m_gT, 2 * b)
                for k in range(FK + 1):
                    n = 128 if k < FK else FR
                    dst = bank[1][:, 128 * k:128 * k + 128] if k < FK else bank[2][0:FR, 0:128]
                    mm(dst, wfc1a[:, 128 * k:128 * k + n], hT1[:, :], start=True, stop=False)
                    ins = mm(dst, wfc1b[:, 128 * k:128 * k + n], hT2[:, :], start=False, stop=True)
                ins.then_inc(m_fc1, 1)

            def fc2(b):
                wait(pe, m_gT, 2 * b + 2)
                wait(pe, m_x2, b)
                for k in range(FK):
                    mm(bank[3][:, 0:C], gT[:, k, :], wfc2a[:, k, :], start=(k == 0), stop=False)
                mm(bank[3][:, 0:C], gT[0:FR + 1, FK, :], wfc2b[:, :], start=False, stop=True).then_inc(m_fc2, 1)

            def rotation(b):
                wait(pe, m_x2, b + 1)
                wait(pe, m_xT, 2 * b)
                pe.transpose(bank[4][:, 0:128], x2[:, 0:C1], ident[:, :])
                pe.transpose(bank[4][0:C2, 128:256], x2[:, C1:C], ident[:, :]).then_inc(m_x2T, 1)
                wait(pe, m_xT, 2 * b + 2)
                wait(pe, m_zT, b)
                mm(bank[5][0:RD, 0:128], U1[:, :], xT1[:, :], start=True, stop=False)
                mm(bank[5][0:RD, 0:128], U2[:, :], xT2[:, :], start=False, stop=True).then_inc(m_z, 1)
                wait(pe, m_zT, b + 1)
                wait(pe, m_out, b)
                mm(bank[6][:, 0:C], zT[:, :], M_all[:, bass.ds(b, 1), :].rearrange("p a c -> p (a c)"),
                   start=True, stop=True).then_inc(m_rot, 1)

            def mlp(b):
                more = not (isinstance(b, int) and b == B - 1)
                if more:
                    transposed(b + 1, m_xn, m_xnT, m_hT, 2 * b + 2)
                fc2(b)
                if more:
                    fc1(b + 1)
                rotation(b)

            pe.wait_ge(s_ldm, 96)
            transposed(0, m_xn, m_xnT, s_ET, 2)
            pe.wait_ge(s_U, 2)
            pe.wait_ge(s_M, 6)
            fc1(0)
            rolled(pe, mlp, 0, B - 2)
            mlp(B - 1)


def paired(eng, body, last):
    Links(eng, None).paired(body, 0, last)


def rolled(eng, body, first, last):
    body(first)
    with eng.Fori(first + 1, last + 1) as i:
        body(i)


_INS = ["x", "cond_1152", "L0_cond_W_qkv", "L0_cond_b_qkv", "L0_cond_W_proj", "L0_cond_b_proj", "L0_cond_W_fc1",
        "L0_cond_b_fc1", "L0_cond_W_fc2", "L0_cond_b_fc2", "L0_cond_W_ada", "L0_cond_b_ada", "L1_cond_P", "L1_cond_W",
        "L1_cond_b"]


def kernel(**inputs):
    import numpy as _np
    import concourse.bacc as _bacc
    from concourse import mybir as _mybir
    from concourse.bass_utils import run_bass_kernel_spmd as _run

    nc = _bacc.Bacc("TRN2", target_bir_lowering=False, num_devices=1)
    arrays, args = {}, []
    for name in _INS:
        a = _np.ascontiguousarray(inputs[name])
        arrays[f"in_{name}_dram"] = a
        args.append(nc.dram_tensor(f"in_{name}_dram", a.shape, _mybir.dt.from_np(a.dtype), kind="ExternalInput").ap())
    B, L, C = inputs["x"].shape
    args.append(nc.dram_tensor("gates_dram", (B, 2 * C), _mybir.dt.float32, kind="Internal").ap())
    args.append(nc.dram_tensor("out_dram", (B, L, C), _mybir.dt.float32, kind="ExternalOutput").ap())
    adaln_block_then_rotation(nc, *args)
    r = _run(nc, [arrays], core_ids=[0])
    return r.results[0]["out_dram"]
```

```python
from contextlib import ExitStack
from math import factorial

import concourse.bass as bass
from concourse import mybir

ALU = mybir.AluOpType
ACT = mybir.ActivationFunctionType
AX = mybir.AxisListType
F32 = mybir.dt.float32
BF16 = mybir.dt.bfloat16
I32 = mybir.dt.int32


class Links:

    def __init__(self, eng, sem, apart=None):
        self.eng, self.sem, self.base, self.n, self.apart = eng, sem, 0, 0, apart

    def link(self, ins):
        self.n += 1
        ins.then_inc(self.sem, 1)
        wait(self.eng, self.sem, self.base + self.n, self.apart)

    def mark(self, ins):
        self.n += 1
        ins.then_inc(self.sem, 1)
        return self.n

    def need(self, mark):
        wait(self.eng, self.sem, self.base + mark, self.apart)

    def paired(self, body, per, first, loop_first, loop_last, last):
        for b in range(first, loop_first):
            body(b, b % 2)
        with self.eng.Fori(loop_first // 2, (loop_last + 1) // 2) as i:
            outer_n, outer_base = self.n, self.base
            self.base, self.n = (i - loop_first // 2) * (2 * per) + (outer_base + outer_n), 0
            for parity in range(2):
                body(2 * i + parity, parity)
            assert self.n == 2 * per, self.n
            self.base, self.n = outer_base, outer_n
        self.n += per * (loop_last - loop_first + 1)
        for b in range(loop_last + 1, last + 1):
            body(b, b % 2)


def wait(eng, sem, value, apart=None):
    if isinstance(value, int) and value <= 0:
        return
    eng.wait_ge(sem, value)
    if apart is not None and not isinstance(value, int):
        eng.sem_inc(apart, 1)


def adaln_block_then_rotation(nc, x, cond, W_qkv, b_qkv, W_proj, b_proj, W_fc1, b_fc1, W_fc2, b_fc2,
                              W_ada, b_ada, P, W, bvec, gates_dram, out):
    B, L, C = x.shape
    H = 16
    D = C // H
    FF = W_fc1.shape[1]
    RD = P.shape[1]
    NSK = W.shape[0]
    EPS = 1e-6
    SCALE = float(D) ** -0.5
    C1, C2 = 128, C - 128
    K2 = C2 + 1
    SL = 64
    NP6 = 6 * D
    NC = B // 2
    FK = FF // 128
    FR = FF - 128 * FK
    WP = 126
    WK = NSK // WP
    QB = RD // B
    N_ID, N_ALL, N_FILL = 8, 11, 21
    SQ = 4
    DEG = 12
    THETA = 1.58
    XSQ = 12
    assert B >= DEG + SQ and L == 128 and NSK == RD * (RD - 1) // 2 and WP * WK == NSK and B % 2 == 0

    with ExitStack() as ctx:
        def sb(name, shape, dt=F32):
            return ctx.enter_context(nc.sbuf_tensor(name, shape, dt))

        def sem(name):
            return ctx.enter_context(nc.semaphore(name))

        bank = [ctx.enter_context(nc.psum_tensor(f"bank{i}", [128, 512], F32)) for i in range(8)]

        x_all = sb("x_all", [128, B, C])
        cond_sb = sb("cond_sb", [B, C])
        wada1, wada2 = sb("wada1", [C1, 6 * C]), sb("wada2", [K2, 6 * C])
        wqkv1, wqkv2 = sb("wqkv1", [C1, 3 * C]), sb("wqkv2", [128, 3 * C])
        wfc1a, wfc1b = sb("wfc1a", [C1, FF]), sb("wfc1b", [128, FF])
        wfc2a, wfc2b = sb("wfc2a", [128, FK, C]), sb("wfc2b", [FR + 1, C])
        wproj = sb("wproj", [128, 4, C])
        wskew = sb("wskew", [WP, WK, C])
        wskT1, wskT2 = sb("wskT1", [C1, NSK]), sb("wskT2", [128, NSK])
        p1, p2 = sb("p1", [C1, 2, RD]), sb("p2", [C2, 2, RD])
        ident = sb("ident", [128, 128])
        identb = sb("identb", [128, 128], BF16)
        eye2 = sb("eye2", [128, RD])
        ones = sb("ones", [128, 32])
        halves = sb("halves", [128, 128])
        lower = sb("lower", [128, RD])
        negmask = sb("negmask", [128, RD])
        headsel = sb("headsel", [128, 2, 8, 128], BF16)
        zeros = sb("zeros", [128, 128])
        hs = sb("hs", [128, 2, 8])
        eye8 = sb("eye8", [128, 8, RD])
        coef = sb("coef", [128, DEG - 1])
        ckI = sb("ckI", [128, 128])
        mhalf = sb("mhalf", [128, B])
        mtwo = sb("mtwo", [128, 1])
        sumsel = sb("sumsel", [128, 4, 32])
        sumrow = sb("sumrow", [128, 4, 128])
        sil = sb("sil", [B, C])
        sexp = sb("sexp", [B, C])
        sT1, sT2 = sb("sT1", [C1, B]), sb("sT2", [128, B])
        mod1, mod2 = sb("mod1", [C1, 4, B]), sb("mod2", [C2, 4, B])
        gates_sb = sb("gates_sb", [B, 2 * C])
        gates = sb("gates", [128, B, 2 * C])
        stats = sb("stats", [128, B, 6])
        mv = sb("mv", [128, B, 2])
        rstd = sb("rstd", [128, B])
        xn = sb("xn", [128, C])
        hT1, hT2 = sb("hT1", [C1, 128]), sb("hT2", [128, 128])
        qk32 = sb("qk32", [128, 2, C])
        res = sb("res", [128, 2, C])
        qs = sb("qs", [128, H, SL], BF16)
        ks = sb("ks", [128, H, SL], BF16)
        QT = [[sb(f"QT{p}{n}", [128, H // 4, 128], BF16) for n in range(2)] for p in range(2)]
        KT = [[sb(f"KT{p}{n}", [128, 2, H // 4, 128], BF16) for n in range(2)] for p in range(2)]
        v144 = sb("v144", [128, C])
        V = [sb(f"V{p}", [128, H, 32]) for p in range(2)]
        nmax = sb("nmax", [128, 2, 8])
        nmr = sb("nmr", [128, 2, 8])
        NM = sb("NM", [128, 2, SL], BF16)
        NMT = sb("NMT", [128, 128], BF16)
        E = sb("E", [128, 4, 4, 128])
        Osb = sb("Osb", [128, 512])
        rsum = sb("rsum", [128, 128])
        ON = sb("ON", [128, 4, 128])
        tmp = sb("tmp", [128, C])
        gT = [sb(f"gT{p}", [128, FK + 1, 128]) for p in range(2)]
        x2 = [sb(f"x2{p}", [128, C]) for p in range(2)]
        xT1, xT2 = sb("xT1", [C1, 128]), sb("xT2", [C2, 128])
        zT = sb("zT", [RD, 128])
        M_all = sb("M_all", [RD, B, C])
        UT = sb("UT", [128, C])
        U1, U2 = sb("U1", [C1, RD]), sb("U2", [C2, RD])
        ET = sb("ET", [RD, 2, RD])
        PT = sb("PT", [RD, C])
        Z = sb("Z", [128, 3 * RD])
        sel = sb("sel", [128, QB, 128])
        rec = sb("rec", [128, RD])
        root, nroot2 = sb("root", [128, RD]), sb("nroot2", [128, RD])
        zm = sb("zm", [128, 1])
        cG = sb("cG", [128, RD])
        cB, c, w = sb("cB", [128, 1]), sb("c", [128, 1]), sb("w", [128, 1])
        dG, dB, usc = sb("dG", [128, RD]), sb("dB", [128, RD]), sb("usc", [128, 4])
        v = sb("v", [B, NSK + 1])
        A0, Bm = sb("A0", [128, NC, RD]), sb("Bm", [128, NC, RD])
        Dm = sb("Dm", [128, NC, RD])
        Xm = sb("Xm", [128, NC, RD])
        Ym = sb("Ym", [128, NC, RD])
        rowsq = sb("rowsq", [128, NC])
        fro = sb("fro", [128, NC])
        over = sb("over", [128, NC, XSQ])
        limit, halving = sb("limit", [128, XSQ]), sb("halving", [128, XSQ])
        nsc = sb("nsc", [128, NC])
        mstep = sb("mstep", [128, NC])
        flag = sb("flag", [1, 2], I32)

        s_ldc, s_lda, s_ldw, s_ldb, s_ldq, s_ldp, s_ldm, s_ldP = (
            sem(n) for n in ("s_ldc", "s_lda", "s_ldw", "s_ldb", "s_ldq", "s_ldp", "s_ldm", "s_ldP"))
        s_ldx = [sem(f"s_ldx{n}") for n in range(4)]
        s_gst, s_gld, s_out = sem("s_gst"), sem("s_gld"), sem("s_out")
        o_dve, o_act, o_pool = sem("o_dve"), sem("o_act"), sem("o_pool")
        s_apart = [sem(f"s_apart{i}") for i in range(2)]
        k_id, k_zero, k_all, k_pad, k_fill, k_more, k_head = (
            sem(n) for n in ("k_id", "k_zero", "k_all", "k_pad", "k_fill", "k_more", "k_head"))
        s_sil, s_sTp, s_sT, s_adaP, s_mod, s_gsb, s_wTp, s_wTd1, s_wTd2, s_vP, s_v = (
            sem(n) for n in ("s_sil", "s_sTp", "s_sT", "s_adaP", "s_mod", "s_gsb", "s_wTp", "s_wTd1", "s_wTd2", "s_vP", "s_v"))
        s_LP, s_L, s_LTp, s_rsq, s_frp, s_anyp, s_flag = (
            sem(n) for n in ("s_LP", "s_L", "s_LTp", "s_rsq", "s_frp", "s_anyp", "s_flag"))
        s_Bs, s_ck, s_typ, s_Y, s_X, s_Xp, s_xsp, s_xs, s_xd, s_R = (
            sem(n) for n in ("s_Bs", "s_ck", "s_typ", "s_Y", "s_X", "s_Xp", "s_xsp", "s_xs", "s_xd", "s_R"))
        s_Gp, s_Z, s_var1, s_rstd1, s_var2, s_rstd2 = (
            sem(n) for n in ("s_Gp", "s_Z", "s_var1", "s_rstd1", "s_var2", "s_rstd2"))
        (s_xn, s_xnT, s_hT, s_qkv, s_qk32, s_v144, s_V, s_hi, s_rest, s_mid, s_lo, s_QKp, s_QKT, s_S, s_max, s_nm,
         s_nmT, s_NMT, s_ST, s_E, s_pv, s_on, s_proj, s_x1, s_st1) = (
            sem(n) for n in ("s_xn", "s_xnT", "s_hT", "s_qkv", "s_qk32", "s_v144", "s_V", "s_hi", "s_rest", "s_mid", "s_lo",
                             "s_QKp", "s_QKT", "s_S", "s_max", "s_nm", "s_nmT", "s_NMT", "s_ST", "s_E", "s_pv",
                             "s_on", "s_proj", "s_x1", "s_st1"))
        s_zm, s_sel, s_Grow, s_Gstep, s_root, s_Brow, s_Bstep, s_O, s_sums, s_rsum, s_div, s_pr = (
            sem(n) for n in ("s_zm", "s_sel", "s_Grow", "s_Gstep", "s_root", "s_Brow", "s_Bstep", "s_O", "s_sums", "s_rsum", "s_div", "s_pr"))
        s_diag, s_dred, s_usc, s_ETp, s_ET, s_UTp, s_UT, s_Up, s_U, s_Mp, s_M = (
            sem(n) for n in ("s_diag", "s_dred", "s_usc", "s_ETp", "s_ET", "s_UTp", "s_UT", "s_Up", "s_U", "s_Mp", "s_M"))
        (m_xn, m_xnT, m_hT, m_fc1, m_gT, m_fc2, m_x2, m_x2T, m_xT, m_z, m_zT, m_rot, m_out) = (
            sem(n) for n in ("m_xn", "m_xnT", "m_hT", "m_fc1", "m_gT", "m_fc2", "m_x2", "m_x2T", "m_xT", "m_z",
                             "m_zT", "m_rot", "m_out"))

        def slot(h):
            g, p = h // 2, h % 2
            return g, p, 2 * (g // 4) + p, g % 4

        def head(q, i):
            return 2 * (4 * (q // 2) + i) + q % 2

        def within(b, first, last):
            return not isinstance(b, int) or first <= b <= last

        def normalizing(b):
            return within(b, -2, B - 3)

        def prepares(b):
            return within(b, -1, B - 2)

        def scoring(b):
            return within(b, 0, B - 1)

        def weighing(b):
            return within(b, 1, B)

        def closing(b):
            return within(b, 2, B + 1)

        ATTENTION = (-2, 2, DEG - 1, B + 1)

        MLP = (-1, 4, B - 3, B + 2)

        def only(b, step):
            return isinstance(b, int) and b == step

        def term(b):
            return within(b, 2, DEG)

        def squaring(b):
            return isinstance(b, int) and DEG + 2 <= b < DEG + 2 + SQ

        def parts_of(stack, first, n, step):
            slots = stack[:, :, 0:NP6].rearrange("p h (s d) -> p h s d", d=D)
            return slots[:, :, first:first + (n - 1) * step + 1:step, :]

        PLACES = (((0, 3, 1), (3, 2, 2), (4, 1, 1)), ((2, 3, 1), (0, 2, 5), (1, 1, 1)))

        def heads_of(t, which):
            return t[:, which, :].rearrange("p (h a d) -> p h a d", h=H, a=1)

        block = ctx.enter_context(nc.Block())

        @block.sync
        def _(sp):
            sp.dma_start(cond_sb[:, :], cond).then_inc(s_ldc, 16)
            wv = W.rearrange("(k p) c -> p k c", p=WP)
            for n in range(4):
                sp.dma_start(wskew[:, 4 * n:4 * n + 4, :], wv[:, 4 * n:4 * n + 4, :]).then_inc(s_ldw, 16)
            xv = x.rearrange("b t c -> t b c")
            for n in range(4):
                sp.dma_start(x_all[:, 4 * n:4 * n + 4, :], xv[:, 4 * n:4 * n + 4, :]).then_inc(s_ldx[n], 16)
            sp.wait_ge(k_fill, 1)
            sp.dma_start(wskT2[C2:K2, :], bvec.rearrange("(a n) -> a n", a=1)).then_inc(s_ldb, 16)
            sp.dma_start(wfc1a[:, :], W_fc1[0:C1, :]).then_inc(s_ldm, 16)
            sp.wait_ge(k_pad, 2)
            sp.dma_start(wfc1b[0:C2, :], W_fc1[C1:C, :]).then_inc(s_ldm, 16)
            sp.dma_start(wfc1b[C2:K2, :], b_fc1.rearrange("(a n) -> a n", a=1)).then_inc(s_ldm, 16)
            sp.dma_start(wfc2a[:, :, :], W_fc2[0:128 * FK, :].rearrange("(k p) n -> p k n", p=128)).then_inc(s_ldm, 16)
            sp.dma_start(wfc2b[0:FR, :], W_fc2[128 * FK:FF, :]).then_inc(s_ldm, 16)
            sp.dma_start(wfc2b[FR:FR + 1, :], b_fc2.rearrange("(a n) -> a n", a=1)).then_inc(s_ldm, 16)
            sp.wait_ge(k_fill, 2)
            wp = W_proj.rearrange("(a i b d) n -> i a b d n", a=2, i=4, b=2)
            for i in range(4):
                for q in range(4):
                    sp.dma_start(wproj[32 * i:32 * i + D, q, :], wp[i, q // 2, q % 2, :, :]).then_inc(s_ldp, 16)
            sp.dma_start(wproj[D:D + 1, 0, :], b_proj.rearrange("(a n) -> a n", a=1)).then_inc(s_ldp, 16)
            sp.wait_ge(s_gsb, 1)
            sp.dma_start(gates_dram, gates_sb[:, :]).then_inc(s_gst, 16)
            sp.wait_ge(s_gst, 16)
            gd = gates_dram.rearrange("(a b) n -> a (b n)", a=1)
            sp.dma_start(gates[:, :, :].rearrange("p b n -> p (b n)"),
                         gd.to_broadcast([128, B * 2 * C])).then_inc(s_gld, 16)

            def store(b):
                wait(sp, m_out, b + 1)
                sp.dma_start(out[bass.ds(b, 1), :, :].rearrange("a t c -> t (a c)"),
                             x_all[:, bass.ds(b, 1), :].rearrange("p a c -> p (a c)")).then_inc(s_out, 16)

            store(0)
            with sp.Fori(1, B) as b:
                store(b)
            sp.wait_ge(s_out, 16 * B)

        @block.gpsimd
        def _(pool):
            lk = Links(pool, o_pool, s_apart[0])
            link = lk.link
            made = {}

            def make(ins, done):
                made[done] = made.get(done, 0) + 1
                ins.then_inc(done, 1)
                pool.wait_ge(done, made[done])

            def diagonal(t, own=slice(0, 128)):
                size = t.shape[1]
                make(nc.gpsimd.affine_select(out=t, in_=zeros[own, 0:size], compare_op=ALU.not_equal, fill=1.0,
                                             base=0, pattern=[[-1, size]], channel_multiplier=1), k_id)

            def below_diagonal(t, own, fill):
                make(nc.gpsimd.affine_select(out=t, in_=zeros[own, 0:RD], compare_op=ALU.is_ge, fill=fill,
                                             base=0, pattern=[[1, RD]], channel_multiplier=-1), k_id)

            lo, hi = slice(0, 64), slice(64, 128)
            make(nc.gpsimd.memset(zeros[:, :], 0.0), k_zero)
            make(nc.gpsimd.memset(wqkv2[:, :], 0.0), k_pad)
            make(nc.gpsimd.memset(wfc1b[:, :], 0.0), k_pad)
            diagonal(ident[:, :])
            for own in (lo, hi):
                diagonal(eye2[own, :], own)
            for own in (lo, hi):
                below_diagonal(negmask[own, :], own, -1.0)
            for own in (lo, hi):
                below_diagonal(lower[own, :], own, 1.0)
            make(nc.gpsimd.tensor_copy(identb[:, :], ident[:, :]), k_id)
            assert made[k_id] == N_ID
            pool.wait_ge(k_fill, N_FILL)
            for p in range(2):
                for n in range(3):
                    make(nc.gpsimd.affine_select(out=hs[:, p, :], in_=hs[:, p, :], compare_op=ALU.not_equal, fill=1.0,
                                                 base=-64 * p - n, pattern=[[-3, 8]], channel_multiplier=1), k_all)
            rows = sumrow[:, :, :].rearrange("p q (i r) -> p q i r", i=4)
            make(nc.gpsimd.affine_select(out=rows, in_=rows, compare_op=ALU.not_equal, fill=1.0, base=0,
                                         pattern=[[-1, 4], [-32, 4], [0, 32]], channel_multiplier=1), k_all)
            for p in range(2):
                for n in range(2):
                    make(nc.gpsimd.memset(KT[p][n][:, :, :, :], 0.0), k_all)
            assert made[k_all] == N_ALL

            def inverse_roots(first, last, seen, n, done):
                wait(pool, seen, n, s_apart[0])
                var = mv[:, first:last, 1:2].rearrange("p b a -> p (b a)")
                link(nc.gpsimd.tensor_scalar(rstd[:, first:last], var, EPS, None, ALU.add))
                nc.gpsimd.tensor_tensor(rstd[:, first:last], rstd[:, first:last], mhalf[:, first:last],
                                        ALU.pow).then_inc(done, 1)

            inverse_roots(0, B, s_var1, 1, s_rstd1)

            def rest(b, which, stack):
                wait(pool, s_hi, 2 * b + 1 + which, s_apart[0])
                wait(pool, s_lo, 2 * b, s_apart[0])
                nc.gpsimd.tensor_tensor(heads_of(res, which), heads_of(qk32, which),
                                        parts_of(stack, PLACES[which][0][0], 1, 1), ALU.subtract).then_inc(s_rest, 1)

            def low(b, which, stack):
                wait(pool, s_mid, 2 * b + 1 + which, s_apart[0])
                nc.gpsimd.tensor_tensor(parts_of(stack, *PLACES[which][2]), heads_of(res, which),
                                        parts_of(stack, PLACES[which][1][0], 1, 1), ALU.subtract).then_inc(s_lo, 1)

            def selector(k, n):
                wait(pool, s_Brow, k - 3, s_apart[0])
                nc.gpsimd.tensor_copy(sel[:, n, :], ident[:, bass.ds(k, 1)].to_broadcast([128, 128])).then_inc(s_sel, 1)

            def square_root(k):
                wait(pool, s_Gstep, k + 1, s_apart[0])
                at = bass.ds(k, 1)
                link(nc.gpsimd.tensor_tensor(root[:, at], rec[:, at], mhalf[:, 0:1], ALU.pow))
                nc.gpsimd.tensor_tensor(nroot2[:, at], root[:, at], mtwo[:, :], ALU.mult).then_inc(s_root, 1)

            def masked_column(k):
                wait(pool, s_Bstep, k, s_apart[0])
                nc.gpsimd.tensor_tensor(zm[:, :], Z[:, bass.ds(k + 2 * RD, 1)], negmask[:, bass.ds(k, 1)],
                                        ALU.mult).then_inc(s_zm, 1)

            def coefficient(b):
                nc.gpsimd.tensor_tensor(ckI[:, :], ident[:, :], coef[:, bass.ds(b - 2, 1)].to_broadcast([128, 128]),
                                        ALU.mult).then_inc(s_ck, 1)

            def spread_values(b, parity):
                wait(pool, s_v144, b + 1, s_apart[0])
                wait(pool, s_pv, 4 * b - 4, s_apart[0])
                nc.gpsimd.tensor_copy(V[parity][:, :, 0:D], v144[:, :].rearrange("p (h d) -> p h d", h=H)).then_inc(s_V, 1)

            def added(b):
                wait(pool, s_pr, b + 2, s_apart[0])
                xb = x_all[:, bass.ds(b, 1), :].rearrange("p a c -> p (a c)")
                nc.gpsimd.tensor_tensor(xb, xb, tmp[:, :], ALU.add).then_inc(s_x1, 1)

            def scales_of_U():
                pool.wait_ge(s_Bstep, RD)
                nc.gpsimd.tensor_tensor(dG[:, :], Z[:, 0:RD], eye2[:, :], ALU.mult).then_inc(s_diag, 1)
                nc.gpsimd.tensor_tensor(dB[:, :], Z[:, 2 * RD:3 * RD], eye2[:, :], ALU.mult).then_inc(s_diag, 1)
                pool.wait_ge(s_dred, 2)
                link(nc.gpsimd.tensor_tensor(usc[:, 2:3], usc[:, 0:1], mhalf[:, 0:1], ALU.pow))
                link(nc.gpsimd.tensor_scalar(usc[:, 3:4], usc[:, 1:2], 0.0, -2.0, ALU.is_ge, ALU.mult))
                nc.gpsimd.tensor_scalar(usc[:, 0:1], usc[:, 3:4], 1.0, usc[:, 2:3], ALU.add, ALU.mult).then_inc(s_usc, 1)

            def attention(b, parity):
                for q in range(4):
                    if q == 1 and only(b, B):
                        scales_of_U()
                        inverse_roots(0, B - 2, s_var2, 1, s_rstd2)
                    if q == 3 and closing(b):
                        added(b - 2)
                    if scoring(b):
                        square_root(QB * b + q)
                        masked_column(QB * b + q)
                    if q == 0 and term(b):
                        coefficient(b)
                    if q == 0 and prepares(b):
                        rest(b + 1, 0, qs)
                        rest(b + 1, 1, ks)
                    if q == 1 and prepares(b):
                        low(b + 1, 0, qs)
                        low(b + 1, 1, ks)
                    if scoring(b) and not (isinstance(b, int) and b == B - 1 and q > 0):
                        selector(QB * b + q + 3, (q + 3) % 4)
                    if q == 0 and scoring(b):
                        spread_values(b, parity)

            for k in range(3):
                selector(k, k)
            lk.paired(attention, QB, *ATTENTION)

            inverse_roots(B - 2, B, s_var2, 2, s_rstd2)

        @block.scalar
        def _(act):
            lk = Links(act, o_act)
            link = lk.link
            act.dma_start(wada1[:, :], W_ada[0:C1, :]).then_inc(s_lda, 16)
            act.dma_start(wada2[0:C2, :], W_ada[C1:C, :]).then_inc(s_lda, 16)
            act.dma_start(wada2[C2:K2, :], b_ada.rearrange("(a n) -> a n", a=1)).then_inc(s_lda, 16)
            for p in range(2):
                act.dma_start(p1[:, p, :], P[0:C1, :]).then_inc(s_ldP, 16)
                act.dma_start(p2[:, p, :], P[C1:C, :]).then_inc(s_ldP, 16)
            act.dma_start(wqkv1[:, :], W_qkv[0:C1, :]).then_inc(s_ldq, 16)
            act.wait_ge(k_pad, 1)
            act.dma_start(wqkv2[0:C2, :], W_qkv[C1:C, :]).then_inc(s_ldq, 16)
            act.dma_start(wqkv2[C2:K2, :], b_qkv.rearrange("(a n) -> a n", a=1)).then_inc(s_ldq, 16)
            act.wait_ge(s_ldc, 16)
            nc.scalar.activation(sexp[:, :], cond_sb[:, :], ACT.Exp, scale=-1.0).then_inc(s_sil, 1)
            act.wait_ge(k_all, 6)
            nc.scalar.activation(headsel[:, :, :, :].rearrange("p a g t -> p (a g) t"),
                                 hs[:, :, :].rearrange("p a (g t) -> p (a g) t", t=1).to_broadcast([128, 16, 128]),
                                 ACT.Copy).then_inc(k_head, 1)
            for n in range(4):
                wait(act, s_wTp, n + 1)
                nc.scalar.activation(wskT1[:, 504 * n:504 * n + 504], bank[2 * (n % 2)][:, 0:504], ACT.Copy).then_inc(s_wTd1, 1)
            def evacuated(M, bk, seen, n, done):
                act.wait_ge(seen, n)
                nc.scalar.activation(M[:, :, :].rearrange("p c n -> p (c n)"), bank[bk][:, :], ACT.Copy).then_inc(done, 1)

            def generator_entries(first, last):
                for n in range(first, last):
                    wait(act, s_vP, n + 1)
                    nc.scalar.activation(v[:, 1 + 504 * n:505 + 504 * n], bank[5 - 2 * (n % 2)][0:B, 0:504],
                                         ACT.Copy).then_inc(s_v, 1)

            def modulated(b, tp, done, free, freed, row, src):
                wait(act, tp, b + 1)
                wait(act, free, freed)
                for t, m, n in ((hT1[:, :], mod1, C1), (hT2[0:C2, :], mod2, C2)):
                    nc.scalar.activation(t, src[0:n, (0 if n == C1 else 128):(128 if n == C1 else 256)], ACT.Identity,
                                         bias=m[:, row, bass.ds(b, 1)], scale=m[:, row + 1, bass.ds(b, 1)]).then_inc(done, 1)

            def attention(b, parity):
                if weighing(b):
                    act.wait_ge(s_nmT, b)
                    wait(act, s_ST, 4 * b - 4)
                    nc.scalar.activation(NMT[:, :], bank[0][:, 256:320].bitcast(BF16), ACT.Copy).then_inc(s_NMT, 1)
                if prepares(b):
                    wait(act, s_qkv, b + 2)
                    wait(act, s_rest, 2 * b + 2)
                    nc.scalar.activation(qk32[:, 0, :], bank[1][:, 0:C], ACT.Copy, scale=SCALE).then_inc(s_qk32, 1)
                    nc.scalar.activation(qk32[:, 1, :], bank[1][:, C:2 * C], ACT.Copy).then_inc(s_qk32, 1)
                if prepares(b):
                    wait(act, s_QKp, 2 * b + 2)
                    wait(act, s_qk32, 2 * b + 4)
                    for which, stack in enumerate((qs, ks)):
                        place = PLACES[which][0]
                        nc.scalar.activation(parts_of(stack, *place), heads_of(qk32, which).to_broadcast([128, H, place[1], D]),
                                             ACT.Copy).then_inc(s_hi, 1)
                if only(b, -1):
                    generator_entries(3, 4)
                if closing(b):
                    act.wait_ge(s_pv, 4 * b - 4)
                    nc.scalar.activation(Osb[:, :], bank[5][:, :], ACT.Copy).then_inc(s_O, 1)
                if weighing(b):
                    exponentials(b - 1, 0)
                if prepares(b):
                    for which, stack in enumerate((qs, ks)):
                        place = PLACES[which][1]
                        wait(act, s_rest, 2 * b + 3 + which)
                        nc.scalar.activation(parts_of(stack, *place), heads_of(res, which).to_broadcast([128, H, place[1], D]),
                                             ACT.Copy).then_inc(s_mid, 1)
                if weighing(b):
                    exponentials(b - 1, 1)
                if squaring(b):
                    evacuated(Xm, 0, s_Xp, b - DEG - 1, s_X)
                    evacuated(Ym, 2, s_Xp, b - DEG - 1, s_Y)
                if only(b, B + 1):
                    modulated(0, m_xnT, m_hT, m_fc1, 0, 2, bank[0])
                if prepares(b):
                    wait(act, s_V, b + 1)
                    nc.scalar.activation(v144[:, :], bank[1][:, 2 * C:3 * C], ACT.Copy).then_inc(s_v144, 1)
                    stacks_transposed(b + 1, 1 - parity, 0)
                if term(b):
                    evacuated(Ym, 0, s_typ, b - 1, s_Y)
                if only(b, DEG + 1):
                    evacuated(Xm, 0, s_typ, DEG, s_X)
                if weighing(b):
                    exponentials(b - 1, 2)
                if normalizing(b):
                    modulated(b + 2, s_xnT, s_hT, s_qkv, b + 2, 0, bank[0])
                if weighing(b):
                    exponentials(b - 1, 3)
                if prepares(b):
                    stacks_transposed(b + 1, 1 - parity, 1)

            def exponentials(b, q):
                act.wait_ge(s_ST, 4 * b + q + 1)
                wait(act, s_sums, b)
                nc.scalar.activation(E[:, q, :, :].rearrange("p i t -> p (i t)"), bank[4][:, :],
                                     ACT.Exp).then_inc(s_E, 1)

            def stacks_transposed(b, parity, n):
                wait(act, s_QKp, 2 * b + n + 1)
                wait(act, s_ST, 4 * b - 6 + 2 * n)
                nc.scalar.activation(QT[parity][n][:, :, :].rearrange("p g t -> p (g t)"),
                                     bank[2][:, 0:256].bitcast(BF16), ACT.Copy).then_inc(s_QKT, 1)
                for p in range(2):
                    own = slice(64 * p, 64 * p + 64)
                    nc.scalar.activation(KT[parity][n][own, p, :, :].rearrange("p g t -> p (g t)"),
                                         bank[2][own, 256:512].bitcast(BF16), ACT.Copy).then_inc(s_QKT, 1)

            act.wait_ge(s_mod, 4)
            act.wait_ge(k_all, N_ALL)
            act.wait_ge(k_fill, N_FILL)
            generator_entries(0, 3)
            lk.paired(attention, 0, *ATTENTION)

            def gelu(b, parity):
                wait(act, m_fc1, b + 1)
                wait(act, m_fc2, b - 1)
                nc.scalar.activation(gT[parity][:, 0:FK, :].rearrange("p k t -> p (k t)"), bank[1][:, :],
                                     ACT.Gelu_apprx_tanh).then_inc(m_gT, 1)
                nc.scalar.activation(gT[parity][0:FR, FK, :], bank[2][0:FR, 0:128], ACT.Gelu_apprx_tanh).then_inc(m_gT, 1)

            def mlp(b, parity):
                if within(b, 0, B - 1):
                    gelu(b, parity)
                if within(b, 0, B - 2):
                    modulated(b + 1, m_xnT, m_hT, m_fc1, b + 1, 2, bank[0])

            lk.paired(mlp, 0, *MLP)

        @block.vector
        def _(dve):
            lk = Links(dve, o_dve)
            link = lk.link
            TT, TS, STT = nc.vector.tensor_tensor, nc.vector.tensor_scalar, nc.vector.scalar_tensor_tensor

            def flat(t):
                return t[:, :, :].rearrange("p c n -> p (c n)")

            def fill(t, value):
                nc.vector.memset(t, value).then_inc(k_fill, 1)

            fill(wskT2[:, :], 0.0)
            fill(wproj[:, :, :], 0.0)
            fill(sT2[:, :], 1.0)
            fill(mhalf[:, :], -0.5)
            fill(mtwo[:, :], -2.0)
            fill(v[:, 0:1], 0.0)
            fill(ones[:, :], 1.0)
            fill(A0[:, :, :], 0.0)
            for p in range(2):
                fill(halves[64 * p:64 * p + 64, 0:128], 0.0)
            fill(hs[:, :, :], 0.0)
            fill(hT2[:, :], 1.0)
            fill(qs[:, :, :], 0.0)
            fill(ks[:, :, :], 0.0)
            fill(NM[:, :, :], 0.0)
            for p in range(2):
                fill(V[p][:, :, :], 0.0)
                fill(gT[p][:, FK, :], 1.0)
            fill(sumsel[:, :, :], 1.0)
            fill(sumrow[:, :, :], 0.0)
            for k in range(DEG - 1):
                lk.mark(nc.vector.memset(coef[:, k:k + 1], 1.0 / factorial(DEG - 2 - k)))
            for i in range(XSQ):
                lk.mark(nc.vector.memset(limit[:, i:i + 1], 2 * (THETA * 2 ** (SQ + i)) ** 2))
                lk.mark(nc.vector.memset(halving[:, i:i + 1], 0.5 ** (i + 1)))
            dve.wait_ge(k_fill, N_FILL)
            for p in range(2):
                lk.mark(nc.vector.memset(V[p][:, :, D:D + 1], 1.0))
                lk.mark(nc.vector.memset(halves[64 * p:64 * p + 64, 64 * p:64 * p + 64], 1.0))
            link(nc.vector.memset(sumsel[:, :, 0:4], 0.0))
            for q in range(4):
                ins = nc.vector.memset(sumsel[:, q, q:q + 1], 1.0)
            link(ins)
            dve.wait_ge(k_id, N_ID)
            dve.wait_ge(s_Gp, 1)
            nc.vector.tensor_copy(Z[:, 0:RD], bank[7][:, 0:RD]).then_inc(s_Z, 1)
            nc.vector.tensor_copy(Z[:, 2 * RD:3 * RD], bank[7][:, RD:2 * RD]).then_inc(s_Z, 1)
            nc.vector.tensor_copy(Z[:, RD:2 * RD], eye2[:, :]).then_inc(s_Z, 1)
            nc.vector.tensor_copy(PT[:, :], bank[7][0:RD, 2 * RD:2 * RD + C]).then_inc(s_Z, 1)
            dve.wait_ge(s_sil, 1)
            link(TS(sexp[:, :], sexp[:, :], 1.0, None, ALU.add))
            link(nc.vector.reciprocal(sexp[:, :], sexp[:, :]))
            TT(sil[:, :], cond_sb[:, :], sexp[:, :], ALU.mult).then_inc(s_sil, 1)
            dve.wait_ge(s_sTp, 1)
            dve.wait_ge(k_id, N_ID)
            nc.vector.tensor_copy(sT1[:, :], bank[6][0:C1, 0:B]).then_inc(s_sT, 1)
            nc.vector.tensor_copy(sT2[0:C2, :], bank[6][0:C2, B:2 * B]).then_inc(s_sT, 1)
            for n in range(4):
                wait(dve, s_wTp, n + 1)
                nc.vector.tensor_copy(wskT2[0:C2, 504 * n:504 * n + 504],
                                      bank[1 + 2 * (n % 2)][0:C2, 0:504]).then_inc(s_wTd2, 1)
                dve.wait_ge(s_ldx[n], 16)
                for b in range(4 * n, 4 * n + 4):
                    ins = nc.vector.bn_stats(stats[:, b, :], x_all[:, b, :])
            link(ins)
            for b in range(B):
                ins = nc.vector.bn_aggr(mv[:, b, :], stats[:, b, :])
            ins.then_inc(s_var1, 1)
            dve.wait_ge(s_adaP, 1)
            for m, n, o in ((mod1, C1, 0), (mod2, C2, 64)):
                ps = bank[6][0:n, o:o + 4 * B].rearrange("p (k a b) -> p k a b", k=2, a=2)
                mm = m[:, :, :].rearrange("p (k a) b -> p k a b", k=2)
                nc.vector.tensor_copy(mm[:, :, 0, :], ps[:, :, 0, :]).then_inc(s_mod, 1)
                TS(mm[:, :, 1, :], ps[:, :, 1, :], 1.0, None, ALU.add).then_inc(s_mod, 1)
            nc.vector.tensor_copy(gates_sb[:, :], bank[6][0:B, 128:128 + 2 * C]).then_inc(s_gsb, 1)
            link(nc.vector.tensor_copy(eye8[:, :, :], eye2[:, :].rearrange("p (a n) -> p a n", a=1).to_broadcast([128, 8, RD])))
            dve.sem_inc(k_more, 1)

            def triangles():
                dve.wait_ge(s_LP, 1)
                TT(A0[:, :, 0:RD - 1].rearrange("p c i -> p i c"),
                   bank[4][:, 0:(RD - 1) * NC].rearrange("p (i c) -> p i c", c=NC),
                   lower[:, 0:RD - 1].rearrange("p (i a) -> p i a", a=1).to_broadcast([128, RD - 1, NC]),
                   ALU.mult).then_inc(s_L, 1)

            def generator():
                dve.wait_ge(s_LTp, 1)
                link(TT(flat(Bm), flat(A0), bank[6][:, :], ALU.subtract))
                link(TT(flat(A0), flat(Bm), flat(Bm), ALU.mult))
                nc.vector.tensor_reduce(rowsq[:, :], A0[:, :, :], AX.X, ALU.add).then_inc(s_rsq, 1)

            eye_c = eye2[:, :].rearrange("p (a n) -> p a n", a=1).to_broadcast([128, NC, RD])

            def scaled():
                dve.wait_ge(s_frp, 1)
                link(nc.vector.tensor_copy(fro[:, :], bank[6][:, 0:NC]))
                def each(t):
                    return t[:, :].rearrange("p (a i) -> p a i", a=1).to_broadcast([128, NC, XSQ])

                link(TT(over[:, :, :], fro[:, :].rearrange("p (c a) -> p c a", a=1).to_broadcast([128, NC, XSQ]),
                        each(limit), ALU.is_gt))
                link(TT(over[:, :, :], over[:, :, :], each(halving), ALU.mult))
                link(nc.vector.tensor_reduce(nsc[:, :], over[:, :, :], AX.X, ALU.add))
                link(TS(nsc[:, :], nsc[:, :], -(0.5 ** SQ), 0.5 ** SQ, ALU.mult, ALU.add))
                TT(Bm[:, :, :], Bm[:, :, :], nsc[:, :].rearrange("p (c a) -> p c a", a=1).to_broadcast([128, NC, RD]),
                   ALU.mult).then_inc(s_Bs, 1)
                dve.wait_ge(s_Bs, 1)
                link(TS(flat(Ym), flat(Bm), -1.0 / factorial(DEG), None, ALU.mult))
                STT(Ym[:, :, :], eye_c, 1.0 / factorial(DEG - 1), Ym[:, :, :], ALU.mult, ALU.add).then_inc(s_Y, 1)

            def any_over():
                dve.wait_ge(s_anyp, 1)
                link(nc.vector.tensor_reduce(nsc[0:32, 0:1], bank[6][0:32, NC:2 * NC], AX.X, ALU.add))
                nc.vector.tensor_copy(flag[0:1, 0:1], nsc[0:1, 0:1]).then_inc(s_flag, 1)
                dve.wait_ge(s_flag, 1)
                dve.sem_inc(s_pr, 1)

            def more_squarings_then_R():
                dve.wait_ge(s_flag, 1)
                dve.wait_ge(s_Y, DEG + SQ)
                dve.wait_ge(s_X, 1 + SQ)
                more_squarings = dve.value_load(flag[0:1, 0:1])
                with dve.If(more_squarings > 0):
                    with dve.Fori(0, XSQ) as i:
                        wait(dve, s_xsp, i + 1)
                        take, keep = mstep[:, :], nsc[:, :]
                        o = over[:, :, bass.ds(i, 1)].rearrange("p c a -> p (c a)")
                        TS(take, o, 0.0, None, ALU.is_gt).then_inc(s_xd, 1)
                        TS(keep, o, 0.0, None, ALU.is_equal).then_inc(s_xd, 1)
                        wait(dve, s_xd, 8 * i + 2)
                        tb, kb = (t.rearrange("p (c a) -> p c a", a=1).to_broadcast([128, NC, RD]) for t in (take, keep))
                        for M, bk, T in ((Xm, 4, A0), (Ym, 5, Dm)):
                            TT(T[:, :, :], bank[bk][:, :].rearrange("p (c n) -> p c n", c=NC), tb, ALU.mult).then_inc(s_xd, 1)
                            TT(M[:, :, :], M[:, :, :], kb, ALU.mult).then_inc(s_xd, 1)
                        wait(dve, s_xd, 8 * i + 6)
                        TT(flat(Xm), flat(Xm), flat(A0), ALU.add).then_inc(s_xd, 1)
                        TT(flat(Ym), flat(Ym), flat(Dm), ALU.add).then_inc(s_xd, 1)
                        wait(dve, s_xd, 8 * i + 8)
                        dve.sem_inc(s_xs, 1)
                TT(Xm[:, :, :], Xm[:, :, :], eye_c, ALU.subtract).then_inc(s_R, 1)

            def normalized(b, free, done):
                wait(dve, free, b)
                TS(xn[:, :], x_all[:, bass.ds(b, 1), :].rearrange("p a c -> p (a c)"),
                   mv[:, bass.ds(b, 1), 0:1].rearrange("p a c -> p (a c)"), rstd[:, bass.ds(b, 1)],
                   ALU.subtract, ALU.mult).then_inc(done, 1)

            def eliminations(k, G, B):
                if B:
                    j, jp = bass.ds(k - 1, 1), bass.ds(k - 1 + 2 * RD, 1)
                    bkk = bank[7][:, jp]
                    dve.wait_ge(s_Brow, k)
                if G:
                    kk = bass.ds(k, 1)
                    dve.wait_ge(s_Grow, k + 1)
                    got_rec = lk.mark(nc.vector.reciprocal(rec[:, kk], bank[7][:, kk]))
                if B:
                    wait(dve, s_zm, k)
                    got_c = lk.mark(STT(c[:, :], bkk, cG[:, j], zm[:, :], ALU.mult, ALU.subtract))
                    wait(dve, s_root, k)
                    got_sign = lk.mark(TS(cB[:, :], bkk, 0.0, nroot2[:, j], ALU.is_ge, ALU.mult))
                if G:
                    lk.need(got_rec)
                    got_cG = lk.mark(TS(cG[:, kk], Z[:, kk], rec[:, kk], negmask[:, kk], ALU.mult, ALU.mult))
                if B:
                    lk.need(got_sign)
                    got_pivot = lk.mark(STT(w[:, :], cB[:, :], root[:, j], bkk, ALU.add, ALU.subtract))
                if G:
                    lk.need(got_cG)
                    STT(Z[:, 0:2 * RD], bank[7][:, 0:2 * RD], cG[:, kk], Z[:, 0:2 * RD],
                        ALU.mult, ALU.add).then_inc(s_Gstep, 1)
                if B:
                    lk.need(got_pivot)
                    link(nc.vector.reciprocal(w[:, :], w[:, :]))
                    link(STT(cB[:, :], c[:, :], w[:, :], cG[:, j], ALU.mult, ALU.add))
                    STT(Z[:, 2 * RD:3 * RD], bank[7][:, 2 * RD:3 * RD], cB[:, :], Z[:, 2 * RD:3 * RD],
                        ALU.mult, ALU.add).then_inc(s_Bstep, 1)

            def gated(b):
                dve.wait_ge(s_proj, b + 1)
                TT(tmp[:, :], bank[6][:, 0:C],
                   gates[:, bass.ds(b, 1), 0:C].rearrange("p a c -> p (a c)"), ALU.mult).then_inc(s_pr, 1)

            def statistics(b):
                dve.wait_ge(s_x1, b + 1)
                nc.vector.bn_stats(stats[:, bass.ds(b, 1), :].rearrange("p a c -> p (a c)"),
                                   x_all[:, bass.ds(b, 1), :].rearrange("p a c -> p (a c)")).then_inc(s_st1, 1)

            def reciprocal_sums(b):
                dve.wait_ge(s_sums, b + 1)
                nc.vector.reciprocal(rsum[:, :], bank[6][:, 0:128]).then_inc(s_rsum, 1)

            def divided(b):
                dve.wait_ge(s_O, b + 1)
                dve.wait_ge(s_div, b + 1)
                TT(ON[:, :, :].rearrange("p q t -> p (q t)"), Osb[:, :], bank[6][:, :], ALU.mult).then_inc(s_on, 1)

            def variances(first, last):
                dve.wait_ge(s_st1, last)
                for b in range(first, last):
                    ins = nc.vector.bn_aggr(mv[:, b, :], stats[:, b, :])
                ins.then_inc(s_var2, 1)

            def transposed_E():
                dve.wait_ge(s_ETp, 1)
                for p in range(2):
                    nc.vector.tensor_copy(ET[:, p, :], bank[1][0:RD, 512 - RD:512]).then_inc(s_ET, 1)
                dve.wait_ge(s_diag, 2)
                nc.vector.tensor_reduce(usc[:, 0:1], dG[:, :], AX.X, ALU.add).then_inc(s_dred, 1)
                nc.vector.tensor_reduce(usc[:, 1:2], dB[:, :], AX.X, ALU.add).then_inc(s_dred, 1)

            def scaled_UT():
                dve.wait_ge(s_UTp, 1)
                dve.wait_ge(s_usc, 1)
                TS(UT[:, :], bank[1][:, 0:C], usc[:, 0:1], None, ALU.mult).then_inc(s_UT, 1)

            def U_copied():
                dve.wait_ge(s_Up, 1)
                nc.vector.tensor_copy(U1[:, :], bank[1][:, 0:RD]).then_inc(s_U, 1)
                nc.vector.tensor_copy(U2[:, :], bank[1][0:C2, RD:2 * RD]).then_inc(s_U, 1)

            def attention(b, parity):
                for q in range(4):
                    if scoring(b):
                        dve.wait_ge(s_S, 4 * b + q + 1)
                        nc.vector.tensor_reduce(nmax[:, q % 2, 4 * (q // 2):4 * (q // 2) + 4],
                                                bank[3][:, :].rearrange("p (i m) -> p i m", i=4),
                                                AX.X, ALU.max, negate=True).then_inc(s_max, 1)
                    if q == 3 and closing(b):
                        gated(b - 2)
                    if q == 3 and scoring(b):
                        maxima_parts(b)
                    if scoring(b) or q == 0 and within(b, 0, B):
                        eliminations(QB * b + q, scoring(b), not (isinstance(b, int) and QB * b + q == 0))
                    if q == 0 and closing(b):
                        reciprocal_sums(b - 2)
                    if q == 1 and closing(b):
                        divided(b - 2)
                    if q == 2 and normalizing(b):
                        normalized(b + 2, s_xnT, s_xn)
                    if q == 3 and closing(b):
                        statistics(b - 2)
                    if q == 0 and only(b, B):
                        variances(0, B - 2)
                        transposed_E()
                    if q == 1 and only(b, B):
                        scaled_UT()
                    if q == 3 and only(b, B):
                        U_copied()
                        dve.wait_ge(s_rstd2, 1)
                        normalized(0, m_xnT, m_xn)
                    if q == 2 and only(b, B + 1):
                        more_squarings_then_R()
                    if q == 3 and only(b, B + 1):
                        variances(B - 2, B)
                    if q == 3 and only(b, 0):
                        triangles()
                    if q == 0 and only(b, 1):
                        generator()
                    if q == 2 and only(b, 1):
                        scaled()
                    if q == 3 and only(b, 1):
                        any_over()
                        dve.wait_ge(s_gld, 16)

            def maxima_parts(b):
                dve.wait_ge(s_max, 4 * b + 4)
                wait(dve, s_nmT, b)
                parts = NM[:, :, 0:24].rearrange("p s (g r) -> p s g r", r=3)
                link(nc.vector.tensor_copy(parts[:, :, :, 0], nmax[:, :, :]))
                link(TT(nmr[:, :, :], nmax[:, :, :], parts[:, :, :, 0], ALU.subtract))
                link(nc.vector.tensor_copy(parts[:, :, :, 1], nmr[:, :, :]))
                TT(parts[:, :, :, 2], nmr[:, :, :], parts[:, :, :, 1], ALU.subtract).then_inc(s_nm, 1)

            dve.wait_ge(s_rstd1, 1)
            dve.wait_ge(k_all, N_ALL)
            lk.paired(attention, 3 + 7 * 4, *ATTENTION)

            def products_evacuated(p):
                dve.wait_ge(s_Mp, p + 1)
                for n in range(3):
                    cnt = 3 if n < 2 else 2
                    dst = M_all[:, :, :].rearrange("d (c b) n -> d c b n", b=2)[:, 3 * n:3 * n + cnt, p, :]
                    nc.vector.tensor_copy(dst, bank[5 + n][0:RD, 0:cnt * C].rearrange(
                        "d (c n) -> d c n", c=cnt)).then_inc(s_M, 1)

            def mlp(b, parity):
                if only(b, 1) or only(b, 2):
                    products_evacuated(b - 1)
                if only(b, 1):
                    dve.wait_ge(s_rstd2, 2)
                if within(b, 3, B + 2):
                    wait(dve, m_rot, b - 2)
                    TT(x_all[:, bass.ds(b - 3, 1), :].rearrange("p a c -> p (a c)"), x2[1 - parity][:, :],
                       bank[6][:, 0:C], ALU.add).then_inc(m_out, 1)
                if within(b, 2, B + 1):
                    wait(dve, m_x2T, b - 1)
                    wait(dve, m_z, b - 2)
                    nc.vector.tensor_copy(xT1[:, :], bank[4][:, 0:128]).then_inc(m_xT, 1)
                    nc.vector.tensor_copy(xT2[:, :], bank[4][0:C2, 128:256]).then_inc(m_xT, 1)
                if within(b, 1, B):
                    wait(dve, m_fc2, b)
                    wait(dve, m_x2T, b - 2)
                    link(TT(tmp[:, :], bank[3][:, 0:C],
                            gates[:, bass.ds(b - 1, 1), C:2 * C].rearrange("p a c -> p (a c)"), ALU.mult))
                    TT(x2[1 - parity][:, :], tmp[:, :], x_all[:, bass.ds(b - 1, 1), :].rearrange("p a c -> p (a c)"),
                       ALU.add).then_inc(m_x2, 1)
                if within(b, 2, B + 1):
                    wait(dve, m_z, b - 1)
                    wait(dve, m_rot, b - 2)
                    nc.vector.tensor_copy(zT[:, :], bank[5][0:RD, 0:128]).then_inc(m_zT, 1)
                if within(b, -1, B - 3):
                    normalized(b + 2, m_xnT, m_xn)

            lk.paired(mlp, 1, *MLP)

        @block.tensor
        def _(pe):
            mm = nc.tensor.matmul
            pe.wait_ge(s_ldP, 64)
            pe.wait_ge(k_id, N_ID)
            pe.wait_ge(k_fill, N_FILL)

            def twice(t):
                return t.rearrange("p a n -> p (a n)")

            mm(bank[7][:, 0:RD], twice(p1[:, :, :]), p1[:, 0, :], start=True, stop=False)
            mm(bank[7][:, 0:RD], twice(p2[:, :, :]), p2[:, 0, :], start=False, stop=True)
            mm(bank[7][:, RD:2 * RD], twice(p1[0:RD, :, :]), ident[0:RD, 0:RD], start=True, stop=True)
            mm(bank[7][0:RD, 2 * RD:2 * RD + C1], p1[:, 0, :], ident[:, :], start=True, stop=True)
            mm(bank[7][0:RD, 2 * RD + C1:2 * RD + C], p2[:, 0, :], ident[0:C2, 0:C2], start=True, stop=True).then_inc(s_Gp, 1)
            pe.wait_ge(s_sil, 2)
            pe.transpose(bank[6][0:C1, 0:B], sil[:, 0:C1], ident[0:B, 0:B])
            pe.transpose(bank[6][0:C2, B:2 * B], sil[:, C1:C], ident[0:B, 0:B]).then_inc(s_sTp, 1)
            for n in range(4):
                pe.wait_ge(s_ldw, 64)
                wait(pe, s_wTd1, n - 1)
                wait(pe, s_wTd2, n - 1)
                for j in range(4):
                    pe.transpose(bank[2 * (n % 2)][:, WP * j:WP * j + WP], wskew[:, 4 * n + j, 0:C1], ident[0:WP, 0:WP])
                    ins = pe.transpose(bank[1 + 2 * (n % 2)][0:C2, WP * j:WP * j + WP], wskew[:, 4 * n + j, C1:C],
                                       ident[0:WP, 0:WP])
                ins.then_inc(s_wTp, 1)
            pe.wait_ge(s_sT, 2)
            pe.wait_ge(s_lda, 48)
            for kind, col in enumerate((0, 1, 3, 4)):
                for o, c0, n in ((0, 0, C1), (64, C1, C2)):
                    cols = slice(col * C + c0, col * C + c0 + n)
                    dst = bank[6][0:n, o + B * kind:o + B * kind + B]
                    mm(dst, wada1[:, cols], sT1[:, :], start=True, stop=False)
                    mm(dst, wada2[:, cols], sT2[0:K2, :], start=False, stop=True)
            for n, col in enumerate((2, 5)):
                dst = bank[6][0:B, 128 + C * n:128 + C * n + C]
                mm(dst, sT1[:, :], wada1[:, col * C:col * C + C], start=True, stop=False)
                ins = mm(dst, sT2[0:K2, :], wada2[:, col * C:col * C + C], start=False, stop=True)
            ins.then_inc(s_adaP, 1)
            def generator_entries(first, last):
                for n in range(first, last):
                    wait(pe, s_v, n - 1)
                    dst = bank[5 - 2 * (n % 2)][0:B, 0:504]
                    mm(dst, sT1[:, :], wskT1[:, 504 * n:504 * n + 504], start=True, stop=False)
                    mm(dst, sT2[:, :], wskT2[:, 504 * n:504 * n + 504], start=False, stop=True).then_inc(s_vP, 1)

            def both(c):
                for p in range(2):
                    yield slice(64 * p, 64 * p + 64), slice(RD * c, RD * c + RD)

            def product(bk, lhs, rhs):
                for c in range(NC):
                    for own, cols in both(c):
                        ins = mm(bank[bk][own, cols], lhs[own, c, :], rhs[own, c, :], start=True, stop=True)
                return ins

            def windows(first, last):
                for i in range(first, last):
                    at = (RD - 1) * i - i * (i - 1) // 2 - i
                    for p in range(2):
                        ins = mm(bank[4][64 * p:64 * p + RD, NC * i:NC * i + NC], v[:, at:at + RD],
                                 ident[0:B, p:B:2], start=True, stop=True)
                if last == RD - 1:
                    ins.then_inc(s_LP, 1)

            def matrices_T(M, bk, done):
                for c in range(NC):
                    for own, cols in both(c):
                        ins = mm(bank[bk][own, cols], M[own, c, :], eye2[own, :], start=True, stop=True)
                ins.then_inc(done, 1)

            def horner(b):
                pe.wait_ge(s_ck, b - 1)
                pe.wait_ge(s_Y, b - 1)
                wait(pe, s_NMT, b)
                mm(bank[0][:, :], ckI[:, :], eye8[:, :, :].rearrange("p c n -> p (c n)"), start=True, stop=False)
                for c in range(NC):
                    for own, cols in both(c):
                        ins = mm(bank[0][own, cols], Bm[own, c, :], Ym[own, c, :], start=False, stop=(c == NC - 1))
                ins.then_inc(s_typ, 1)

            def squared(b):
                pe.wait_ge(s_X, b - DEG - 1)
                pe.wait_ge(s_Y, b - 2)
                wait(pe, s_NMT, min(b, B))
                wait(pe, s_QKT, min(6 * b + 6, 6 * B))
                product(0, Ym, Xm)
                product(2, Xm, Ym).then_inc(s_Xp, 1)

            def transposed(b, src_ready, done, free, freed):
                wait(pe, src_ready, b + 1)
                wait(pe, free, freed)
                pe.transpose(bank[0][:, 0:128], xn[:, 0:C1], ident[:, :])
                pe.transpose(bank[0][0:C2, 128:256], xn[:, C1:C], ident[:, :]).then_inc(done, 1)

            def qkv(b):
                pe.wait_ge(s_hT, 2 * b + 2)
                wait(pe, s_qk32, 2 * b)
                wait(pe, s_v144, b)
                mm(bank[1][:, 0:3 * C], hT1[:, :], wqkv1[:, :], start=True, stop=False)
                mm(bank[1][:, 0:3 * C], hT2[:, :], wqkv2[:, :], start=False, stop=True).then_inc(s_qkv, 1)

            def stacks_T(b, n):
                wait(pe, s_lo, 2 * b + 2)
                wait(pe, s_QKT, 6 * b + 3 * n)
                for which, stack in enumerate((qs, ks)):
                    for g in range(4):
                        h = 2 * (4 * n + g)
                        at = 256 * which + 64 * g
                        ins = pe.transpose(bank[2][:, at:at + 64].bitcast(BF16),
                                           stack[:, h:h + 2, :].rearrange("p h s -> p (h s)"), identb[:, :])
                ins.then_inc(s_QKp, 1)

            def scores(q, b, parity):
                wait(pe, s_QKT, 6 * b + (2, 3, 5, 6)[q])
                wait(pe, s_max, 4 * b + q)
                for i in range(4):
                    ins = mm(bank[3][:, 128 * i:128 * i + 128], QT[parity][q // 2][:, i, :],
                             KT[parity][q // 2][:, q % 2, i, :], start=True, stop=True)
                ins.then_inc(s_S, 1)

            def scores_T(q, b, parity):
                wait(pe, s_NMT, b + 1)
                wait(pe, s_E, 4 * b + q)
                for i in range(4):
                    dst = bank[4][:, 128 * i:128 * i + 128]
                    mm(dst, KT[parity][q // 2][:, q % 2, i, :], QT[parity][q // 2][:, i, :], start=True, stop=False)
                    ins = mm(dst, headsel[:, q % 2, 4 * (q // 2) + i, :], NMT[:, :], start=False, stop=True)
                ins.then_inc(s_ST, 1)

            def values(q, b, parity):
                wait(pe, s_E, 4 * b + q + 1)
                if q == 0:
                    wait(pe, s_O, b)
                    pe.wait_ge(s_V, b + 1)
                for i in range(4):
                    own, cols = slice(32 * i, 32 * i + 32), slice(128 * q, 128 * q + 128)
                    ins = mm(bank[5][own, cols], V[parity][:, head(q, i), :], E[:, q, i, :], start=True, stop=True)
                ins.then_inc(s_pv, 1)

            def sums(b):
                wait(pe, s_pr, b + 1)
                for q in range(4):
                    for i in range(4):
                        own = slice(32 * i, 32 * i + 32)
                        ins = mm(bank[6][own, 0:128], sumsel[:, q, :], E[:, q, i, :],
                                 start=(q == 0), stop=(q == 3))
                ins.then_inc(s_sums, 1)

            def division(b):
                pe.wait_ge(s_rsum, b + 1)
                for q in range(4):
                    ins = mm(bank[6][:, 128 * q:128 * q + 128], sumrow[:, q, :], rsum[:, :], start=True, stop=True)
                ins.then_inc(s_div, 1)

            def G_row(k, n):
                pe.wait_ge(s_sel, k + 1)
                wait(pe, s_Gstep, k)
                wait(pe, s_Bstep, k - 1)
                mm(bank[7][:, 0:2 * RD], sel[:, n, :], Z[:, 0:2 * RD], start=True, stop=True).then_inc(s_Grow, 1)

            def B_row(k, n):
                wait(pe, s_Bstep, k)
                mm(bank[7][:, 2 * RD:3 * RD], sel[:, n, :], Z[:, 2 * RD:3 * RD], start=True, stop=True).then_inc(s_Brow, 1)

            def projection(b):
                pe.wait_ge(s_on, b + 1)
                for q in range(4):
                    ins = mm(bank[6][:, 0:C], ON[:, q, :], wproj[:, q, :], start=(q == 0), stop=(q == 3))
                ins.then_inc(s_proj, 1)

            def more_squarings():
                pe.wait_ge(s_flag, 1)
                pe.wait_ge(s_X, 1 + SQ)
                pe.wait_ge(s_Y, DEG + SQ)
                pe.wait_ge(s_E, 4 * B)
                pe.wait_ge(s_O, B)
                asked = pe.value_load(flag[0:1, 0:1])
                with pe.If(asked > 0):
                    pe.sem_inc(s_xs, 1)
                    with pe.Fori(0, XSQ) as i:
                        wait(pe, s_xs, i + 1, s_apart[1])
                        for c in range(NC):
                            for own, cols in both(c):
                                mm(bank[4][own, cols], Ym[own, c, :], Xm[own, c, :], start=True, stop=True)
                                ins = mm(bank[5][own, cols], Xm[own, c, :], Ym[own, c, :], start=True, stop=True)
                        ins.then_inc(s_xsp, 1)

            def attention(b, parity):
                for q in range(4):
                    if scoring(b):
                        scores(q, b, parity)
                    k = QB * b + q
                    if q == 0:
                        if weighing(b):
                            pe.wait_ge(s_nm, b)
                            wait(pe, s_NMT, b - 1)
                            wait(pe, s_hT, min(2 * b + 4, 2 * B) if isinstance(b, int) else 2 * b + 4)
                            pe.transpose(bank[0][:, 256:320].bitcast(BF16), NM[:, :, :].rearrange("p s n -> p (s n)"),
                                         identb[:, :]).then_inc(s_nmT, 1)
                        if prepares(b):
                            qkv(b + 1)
                        if only(b, 1):
                            pe.wait_ge(s_L, 1)
                            pe.wait_ge(s_gsb, 1)
                            matrices_T(A0, 6, s_LTp)
                    if scoring(b):
                        G_row(k, q)
                    if (scoring(b) or q == 0 and within(b, 0, B)) and not (isinstance(b, int) and k == 0):
                        B_row(k - 1, (q + 3) % 4)
                    if q == 0 and closing(b):
                        values(3, b - 2, parity)
                        sums(b - 2)
                    if q == 2 and prepares(b):
                        if squaring(b):
                            pe.wait_ge(s_Y, b - 1)
                        stacks_T(b + 1, 0)
                    if q == 3 and normalizing(b):
                        wait(pe, s_NMT, b)
                        if term(b):
                            pe.wait_ge(s_Y, b)
                        if only(b, DEG + 1):
                            pe.wait_ge(s_X, 1)
                        transposed(b + 2, s_xn, s_xnT, s_hT, 2 * b + 4)
                    if q == 3 and prepares(b):
                        stacks_T(b + 1, 1)
                    if q and weighing(b):
                        values(q - 1, b - 1, 1 - parity)
                    if q == 1 and only(b, B + 1):
                        squared(b)
                    if q == 1 and closing(b):
                        division(b - 2)
                    if weighing(b):
                        scores_T(q, b - 1, 1 - parity)
                    if q == 0 and only(b, B):
                        pe.wait_ge(s_Bstep, RD)
                        pe.wait_ge(s_v144, B)
                        pe.transpose(bank[1][0:RD, 512 - RD:512], Z[0:RD, RD:2 * RD], ident[0:RD, 0:RD]).then_inc(s_ETp, 1)
                    if q == 1 and only(b, B):
                        pe.wait_ge(s_ET, 2)
                        mm(bank[1][:, 0:C], twice(ET[:, :, :]), PT[:, :], start=True, stop=True).then_inc(s_UTp, 1)
                    if q == 2 and only(b, B + 1):
                        pe.wait_ge(s_X, 1 + SQ)
                        transposed(0, m_xn, m_xnT, m_hT, 0)
                    if q == 2 and closing(b):
                        projection(b - 2)
                    if q == 2 and only(b, B + 1):
                        more_squarings()
                    if q == 2 and only(b, B):
                        pe.wait_ge(s_UT, 1)
                        pe.transpose(bank[1][:, 0:RD], UT[0:RD, 0:C1], ident[0:RD, 0:RD])
                        pe.transpose(bank[1][0:C2, RD:2 * RD], UT[0:RD, C1:C], ident[0:RD, 0:RD]).then_inc(s_Up, 1)
                    if only(b, -1) and q == 0:
                        generator_entries(3, 4)
                    if only(b, -1) and q < 2:
                        pe.wait_ge(s_v, 3 + q)
                        windows(16 * q, 16 * q + 16)
                    if only(b, 0):
                        windows(32 + 8 * q, min(40 + 8 * q, RD - 1))
                    if q == 1 and term(b):
                        horner(b)
                    if q == 1 and only(b, DEG + 1):
                        pe.wait_ge(s_Y, DEG)
                        pe.wait_ge(s_NMT, b)
                        matrices_T(Ym, 0, s_typ)
                    if q == 1 and squaring(b) and b < B + 1:
                        squared(b)
                    if q == 1 and only(b, 1):
                        pe.wait_ge(s_rsq, 1)
                        mm(bank[6][:, 0:NC], halves[:, :], rowsq[:, :], start=True, stop=True).then_inc(s_frp, 1)
                    if q == 3 and only(b, 1):
                        pe.wait_ge(s_Bs, 1)
                        mm(bank[6][0:32, NC:2 * NC], ones[:, :], over[:, :, 0], start=True, stop=True).then_inc(s_anyp, 1)
                        pe.wait_ge(s_ldp, 16 * 17)
            pe.wait_ge(s_wTd1, 4)
            pe.wait_ge(s_wTd2, 4)
            pe.wait_ge(s_ldb, 16)
            generator_entries(0, 3)
            pe.wait_ge(s_ldq, 48)
            pe.wait_ge(k_all, N_ALL)
            pe.wait_ge(k_more, 1)
            pe.wait_ge(k_head, 1)
            pe.wait_ge(s_Z, 4)
            paired(pe, attention, *ATTENTION)

            def products(p):
                if p == 0:
                    pe.wait_ge(s_R, 1)
                    pe.wait_ge(s_pr, B + 1)
                else:
                    pe.wait_ge(s_M, 3)
                own = slice(64 * p, 64 * p + 64)
                for c in range(NC):
                    ins = mm(bank[5 + c // 3][0:RD, C * (c % 3):C * (c % 3) + C], Xm[own, c, :], UT[own, :],
                             start=True, stop=True)
                ins.then_inc(s_Mp, 1)

            def fc1(b):
                wait(pe, m_hT, 2 * b + 2)
                wait(pe, m_gT, 2 * b)
                for k in range(FK + 1):
                    n = 128 if k < FK else FR
                    dst = bank[1][:, 128 * k:128 * k + 128] if k < FK else bank[2][0:FR, 0:128]
                    mm(dst, wfc1a[:, 128 * k:128 * k + n], hT1[:, :], start=True, stop=False)
                    ins = mm(dst, wfc1b[:, 128 * k:128 * k + n], hT2[:, :], start=False, stop=True)
                ins.then_inc(m_fc1, 1)

            def fc2(b, parity):
                wait(pe, m_gT, 2 * b + 2)
                wait(pe, m_x2, b)
                for k in range(FK):
                    mm(bank[3][:, 0:C], gT[parity][:, k, :], wfc2a[:, k, :], start=(k == 0), stop=False)
                mm(bank[3][:, 0:C], gT[parity][0:FR + 1, FK, :], wfc2b[:, :], start=False, stop=True).then_inc(m_fc2, 1)

            def x2_T(b, parity):
                wait(pe, m_x2, b + 1)
                wait(pe, m_xT, 2 * b)
                pe.transpose(bank[4][:, 0:128], x2[parity][:, 0:C1], ident[:, :])
                pe.transpose(bank[4][0:C2, 128:256], x2[parity][:, C1:C], ident[:, :]).then_inc(m_x2T, 1)

            def projected(b):
                wait(pe, m_xT, 2 * b + 2)
                wait(pe, m_zT, b)
                mm(bank[5][0:RD, 0:128], U1[:, :], xT1[:, :], start=True, stop=False)
                mm(bank[5][0:RD, 0:128], U2[:, :], xT2[:, :], start=False, stop=True).then_inc(m_z, 1)

            def rotated(b):
                wait(pe, m_zT, b + 1)
                wait(pe, m_out, b)
                mm(bank[6][:, 0:C], zT[:, :], M_all[:, bass.ds(b, 1), :].rearrange("p a c -> p (a c)"),
                   start=True, stop=True).then_inc(m_rot, 1)

            def mlp(b, parity):
                if within(b, 0, B - 1):
                    fc1(b)
                if within(b, 0, B - 2):
                    transposed(b + 1, m_xn, m_xnT, m_hT, 2 * b + 2)
                if within(b, 3, B + 2):
                    rotated(b - 3)
                if within(b, 2, B + 1):
                    x2_T(b - 2, parity)
                if within(b, 1, B):
                    fc2(b - 1, 1 - parity)
                if only(b, 2):
                    pe.wait_ge(s_M, 6)
                if within(b, 2, B + 1):
                    projected(b - 2)
                if only(b, 0) or only(b, 1):
                    products(b)

            pe.wait_ge(s_ldm, 96)
            pe.wait_ge(s_U, 2)
            paired(pe, mlp, *MLP)


def paired(eng, body, *steps):
    Links(eng, None).paired(body, 0, *steps)


_INS = ["x", "cond_1152", "L0_cond_W_qkv", "L0_cond_b_qkv", "L0_cond_W_proj", "L0_cond_b_proj", "L0_cond_W_fc1",
        "L0_cond_b_fc1", "L0_cond_W_fc2", "L0_cond_b_fc2", "L0_cond_W_ada", "L0_cond_b_ada", "L1_cond_P", "L1_cond_W",
        "L1_cond_b"]


def kernel(**inputs):
    import numpy as _np
    import concourse.bacc as _bacc
    from concourse import mybir as _mybir
    from concourse.bass_utils import run_bass_kernel_spmd as _run

    nc = _bacc.Bacc("TRN2", target_bir_lowering=False, num_devices=1)
    arrays, args = {}, []
    for name in _INS:
        a = _np.ascontiguousarray(inputs[name])
        arrays[f"in_{name}_dram"] = a
        args.append(nc.dram_tensor(f"in_{name}_dram", a.shape, _mybir.dt.from_np(a.dtype), kind="ExternalInput").ap())
    B, L, C = inputs["x"].shape
    args.append(nc.dram_tensor("gates_dram", (B, 2 * C), _mybir.dt.float32, kind="Internal").ap())
    args.append(nc.dram_tensor("out_dram", (B, L, C), _mybir.dt.float32, kind="ExternalOutput").ap())
    adaln_block_then_rotation(nc, *args)
    r = _run(nc, [arrays], core_ids=[0])
    return r.results[0]["out_dram"]
```
